# Optimizing a Trainium2 kernel written in Bass

```python
import numpy as np
import jax
import jax.numpy as jnp

def _softmax(x, axis=-1):
    return jax.nn.softmax(x, axis=axis)

def _gelu(x):
    return jax.nn.gelu(x, approximate=True)

def _silu(x):
    return jax.nn.silu(x)

def _sigmoid(x):
    return jax.nn.sigmoid(x)

def _layernorm(x, axis=-1, eps=1e-05):
    m = jnp.mean(x, axis=axis, keepdims=True)
    v = jnp.var(x, axis=axis, keepdims=True)
    return (x - m) / jnp.sqrt(v + eps)

def _scatter_add(tgt, idx, src, axis=0):
    return tgt.at[idx].add(src)

def _segment_sum(src, seg, n):
    return jax.ops.segment_sum(src, seg, n)
kernel_name = 'mk_adj_resnorm_d4_adj_r2_5aa681'

def setup_inputs(seed: int=0):
    np.random.seed(seed)
    _w = jnp.asarray

    def _rec_inputs():
        import jax
        import jax.numpy as jnp
        _gk = jax.random.key(seed)
        x = -0.0002928 + 1 * jax.random.normal(jax.random.fold_in(_gk, 1), (16, 512, 128), jnp.float32)
        _a = jax.random.bernoulli(jax.random.fold_in(_gk, 2), 0.00390625, (16, 512, 512))
        _a = jnp.logical_or(_a, jnp.swapaxes(_a, -1, -2))
        _a = jnp.logical_or(_a, jnp.eye(512, dtype=bool))
        _af = _a.astype(jnp.float32)
        _af = _af * jax.random.uniform(jax.random.fold_in(_gk, 3), (16, 512, 512), jnp.float32, 0.05, 1)
        adj = _af
        return (x, adj)
    x, adj = _rec_inputs()

    def _L0_gnn_setup():
        import jax, jax.numpy as jnp
        import numpy as np
        key = jax.random.key(seed)
        k1, k2, k3, k4 = jax.random.split(key, 4)
        B, N, F_in, F_out = (8, 1024, 128, 128)
        x = jax.random.normal(k1, (B, N, F_in), dtype=jnp.float32)
        adj = jax.random.uniform(k2, (B, N, N), dtype=jnp.float32)
        stdv = 1.0 / np.sqrt(F_out)
        weight = jax.random.uniform(k3, (F_in, F_out), dtype=jnp.float32, minval=-stdv, maxval=stdv)
        bias = jax.random.uniform(k4, (F_out,), dtype=jnp.float32, minval=-stdv, maxval=stdv)
        return {'x': x, 'adj': adj, 'weight': weight, 'bias': bias}
    _L0_gnn_all = _L0_gnn_setup()
    _L0_gnn_in = {k: v for k, v in _L0_gnn_all.items() if k in ('weight', 'bias')}
    del _L0_gnn_all

    def _L1_gnn_setup():
        import jax, jax.numpy as jnp
        import numpy as np
        GROUPS = [list(range(25)), [0, 1, 2, 3, 4, 5, 6, 7, 8], [0, 9, 10, 11, 12, 13, 14], [6, 7, 8, 12, 13, 14], [3, 4, 5, 9, 10, 11]]
        B, N, D_IN, D_HID = (4096, 25, 128, 256)

        def _graph_conv(x, adj, W, b):
            n = adj.shape[-1]
            A = adj + jnp.eye(n, dtype=adj.dtype)
            deg = jnp.sum(A, axis=-1)
            deg_safe = jnp.where(deg == 0, 1.0, deg)
            dinv = jnp.where(deg == 0, 0.0, deg_safe ** (-0.5))
            norm_adj = dinv[:, :, None] * A * dinv[:, None, :]
            support = jnp.einsum('bnd,de->bne', x, W)
            out = jnp.einsum('bnm,bme->bne', norm_adj, support) + b
            return jax.nn.relu(out)
        key = jax.random.key(seed)
        ks = jax.random.split(key, 7)
        s1 = float(np.sqrt(6.0 / (D_IN + D_HID)))
        s2 = float(np.sqrt(6.0 / (D_HID + D_IN)))
        return {'x': jax.random.normal(ks[0], (B, N, D_IN), dtype=jnp.float32), 'adj': jax.random.uniform(ks[1], (B, N, N), dtype=jnp.float32), 'W1': jax.random.uniform(ks[2], (5, D_IN, D_HID), jnp.float32, -s1, s1), 'b1': jnp.zeros((5, D_HID), dtype=jnp.float32), 'W2': jax.random.uniform(ks[3], (5, D_HID, D_IN), jnp.float32, -s2, s2), 'b2': jnp.zeros((5, D_IN), dtype=jnp.float32), 'fusion_w': jnp.ones((5,), dtype=jnp.float32)}
    _L1_gnn_all = _L1_gnn_setup()
    _L1_gnn_in = {k: v for k, v in _L1_gnn_all.items() if k in ('W1', 'b1', 'W2', 'b2', 'fusion_w')}
    del _L1_gnn_all

    def _L2_gnn_setup():
        import jax, jax.numpy as jnp
        import numpy as np
        B, N, D = (2, 2048, 128)
        key = jax.random.key(seed)
        ks = jax.random.split(key, 6)
        return {'hidden': jax.random.normal(ks[0], (B, N, D), dtype=jnp.float32), 'mask': jax.random.uniform(ks[1], (B, N, N), dtype=jnp.float32), 'W_w': jax.random.normal(ks[2], (D, D), dtype=jnp.float32) * 0.05, 'W_b': jax.random.normal(ks[3], (D,), dtype=jnp.float32) * 0.05, 'a_w': jax.random.normal(ks[4], (2 * D,), dtype=jnp.float32) * 0.05, 'a_b': jax.random.normal(ks[5], (1,), dtype=jnp.float32) * 0.05}
    _L2_gnn_all = _L2_gnn_setup()
    _L2_gnn_in = {k: v for k, v in _L2_gnn_all.items() if k in ('W_w', 'W_b', 'a_w', 'a_b')}
    del _L2_gnn_all

    def _L3_gnn_setup():
        import jax, jax.numpy as jnp
        import numpy as np
        from jax import lax
        DIM = 128
        EPS = 1e-05

        def _bn(h, g, b, m, v):
            scale = g / jnp.sqrt(v + EPS)
            return h * scale[None, :, None] + (b - m * scale)[None, :, None]

        def _conv1d(h, w, pad):
            return lax.conv_general_dilated(h, w, window_strides=(1,), padding=[(pad, pad)], dimension_numbers=('NCH', 'OIH', 'NCH'))
        key = jax.random.key(seed)
        ks = jax.random.split(key, 16)
        bs, n, d = (16, 1024, DIM)
        s = 0.05
        return {'x': jax.random.normal(ks[0], (bs, n, d), jnp.float32), 'mask': jnp.ones((bs, n, n), jnp.float32), 'w_se': jax.random.normal(ks[1], (3, d), jnp.float32) * s, 'b_se': jnp.zeros((3,), jnp.float32), 'conv1_w': jax.random.normal(ks[2], (d, d, 1), jnp.float32) * s, 'bn1_g': jnp.ones((d,), jnp.float32), 'bn1_b': jnp.zeros((d,), jnp.float32), 'bn1_m': jnp.zeros((d,), jnp.float32), 'bn1_v': jnp.ones((d,), jnp.float32), 'conv2_w': jax.random.normal(ks[3], (d, d, 17), jnp.float32) * s, 'bn2_g': jnp.ones((d,), jnp.float32), 'bn2_b': jnp.zeros((d,), jnp.float32), 'bn2_m': jnp.zeros((d,), jnp.float32), 'bn2_v': jnp.ones((d,), jnp.float32), 'w_msg': jax.random.normal(ks[4], (d, d), jnp.float32) * s, 'b_msg': jnp.zeros((d,), jnp.float32), 'w_ih': jax.random.normal(ks[5], (3 * d, 2 * d), jnp.float32) * s, 'b_ih': jnp.zeros((3 * d,), jnp.float32), 'w_hh': jax.random.normal(ks[6], (3 * d, d), jnp.float32) * s, 'b_hh': jnp.zeros((3 * d,), jnp.float32)}
    _L3_gnn_all = _L3_gnn_setup()
    _L3_gnn_in = {k: v for k, v in _L3_gnn_all.items() if k in ('w_se', 'b_se', 'conv1_w', 'bn1_g', 'bn1_b', 'bn1_m', 'bn1_v', 'conv2_w', 'bn2_g', 'bn2_b', 'bn2_m', 'bn2_v', 'w_msg', 'b_msg', 'w_ih', 'b_ih', 'w_hh', 'b_hh')}
    del _L3_gnn_all
    return {'x': x, 'adj': adj, 'L0_gnn_weight': _L0_gnn_in['weight'], 'L0_gnn_bias': _L0_gnn_in['bias'], 'L1_gnn_W1': _L1_gnn_in['W1'], 'L1_gnn_b1': _L1_gnn_in['b1'], 'L1_gnn_W2': _L1_gnn_in['W2'], 'L1_gnn_b2': _L1_gnn_in['b2'], 'L1_gnn_fusion_w': _L1_gnn_in['fusion_w'], 'L2_gnn_W_w': _L2_gnn_in['W_w'], 'L2_gnn_W_b': _L2_gnn_in['W_b'], 'L2_gnn_a_w': _L2_gnn_in['a_w'], 'L2_gnn_a_b': _L2_gnn_in['a_b'], 'L3_gnn_w_se': _L3_gnn_in['w_se'], 'L3_gnn_b_se': _L3_gnn_in['b_se'], 'L3_gnn_conv1_w': _L3_gnn_in['conv1_w'], 'L3_gnn_bn1_g': _L3_gnn_in['bn1_g'], 'L3_gnn_bn1_b': _L3_gnn_in['bn1_b'], 'L3_gnn_bn1_m': _L3_gnn_in['bn1_m'], 'L3_gnn_bn1_v': _L3_gnn_in['bn1_v'], 'L3_gnn_conv2_w': _L3_gnn_in['conv2_w'], 'L3_gnn_bn2_g': _L3_gnn_in['bn2_g'], 'L3_gnn_bn2_b': _L3_gnn_in['bn2_b'], 'L3_gnn_bn2_m': _L3_gnn_in['bn2_m'], 'L3_gnn_bn2_v': _L3_gnn_in['bn2_v'], 'L3_gnn_w_msg': _L3_gnn_in['w_msg'], 'L3_gnn_b_msg': _L3_gnn_in['b_msg'], 'L3_gnn_w_ih': _L3_gnn_in['w_ih'], 'L3_gnn_b_ih': _L3_gnn_in['b_ih'], 'L3_gnn_w_hh': _L3_gnn_in['w_hh'], 'L3_gnn_b_hh': _L3_gnn_in['b_hh']}

def reference(x, adj, L0_gnn_weight, L0_gnn_bias, L1_gnn_W1, L1_gnn_b1, L1_gnn_W2, L1_gnn_b2, L1_gnn_fusion_w, L2_gnn_W_w, L2_gnn_W_b, L2_gnn_a_w, L2_gnn_a_b, L3_gnn_w_se, L3_gnn_b_se, L3_gnn_conv1_w, L3_gnn_bn1_g, L3_gnn_bn1_b, L3_gnn_bn1_m, L3_gnn_bn1_v, L3_gnn_conv2_w, L3_gnn_bn2_g, L3_gnn_bn2_b, L3_gnn_bn2_m, L3_gnn_bn2_v, L3_gnn_w_msg, L3_gnn_b_msg, L3_gnn_w_ih, L3_gnn_b_ih, L3_gnn_w_hh, L3_gnn_b_hh):
    import jax
    import jax.numpy as jnp

    def _L0_gnn_ref(x, adj, weight, bias):
        import jax, jax.numpy as jnp
        import numpy as np
        support = jnp.einsum('bni,io->bno', x, weight)
        out = jnp.einsum('bnm,bmo->bno', adj, support)
        return out + bias

    def _L1_gnn_ref(x, adj, W1, b1, W2, b2, fusion_w):
        import jax, jax.numpy as jnp
        import numpy as np
        GROUPS = [list(range(25)), [0, 1, 2, 3, 4, 5, 6, 7, 8], [0, 9, 10, 11, 12, 13, 14], [6, 7, 8, 12, 13, 14], [3, 4, 5, 9, 10, 11]]
        B, N, D_IN, D_HID = (4096, 25, 128, 256)

        def _graph_conv(x, adj, W, b):
            n = adj.shape[-1]
            A = adj + jnp.eye(n, dtype=adj.dtype)
            deg = jnp.sum(A, axis=-1)
            deg_safe = jnp.where(deg == 0, 1.0, deg)
            dinv = jnp.where(deg == 0, 0.0, deg_safe ** (-0.5))
            norm_adj = dinv[:, :, None] * A * dinv[:, None, :]
            support = jnp.einsum('bnd,de->bne', x, W)
            out = jnp.einsum('bnm,bme->bne', norm_adj, support) + b
            return jax.nn.relu(out)
        norm_w = jax.nn.softmax(fusion_w)
        fused = jnp.zeros_like(x)
        for g, idx_list in enumerate(GROUPS):
            idx = jnp.asarray(idx_list)
            x_g = x[:, idx, :]
            adj_g = adj[:, idx][:, :, idx]
            h = _graph_conv(x_g, adj_g, W1[g], b1[g])
            out_g = _graph_conv(h, adj_g, W2[g], b2[g])
            fused = fused.at[:, idx, :].add(norm_w[g] * out_g)
        return fused

    def _L2_gnn_ref(hidden, mask, W_w, W_b, a_w, a_b):
        import jax, jax.numpy as jnp
        import numpy as np
        B, N, D = (2, 2048, 128)
        h = jnp.einsum('bnd,ed->bne', hidden, W_w) + W_b
        Dh = h.shape[-1]
        a1, a2 = (a_w[:Dh], a_w[Dh:])
        e = h @ a1
        f = h @ a2
        logits = e[:, :, None] + f[:, None, :] + a_b[0]
        u = mask * jnp.exp(logits)
        a = u / jnp.sum(u, axis=2, keepdims=True)
        h_prime = jnp.einsum('bnm,bmd->bnd', a, h)
        return h_prime

    def _L3_gnn_ref(x, mask, w_se, b_se, conv1_w, bn1_g, bn1_b, bn1_m, bn1_v, conv2_w, bn2_g, bn2_b, bn2_m, bn2_v, w_msg, b_msg, w_ih, b_ih, w_hh, b_hh):
        import jax, jax.numpy as jnp
        import numpy as np
        from jax import lax
        DIM = 128
        EPS = 1e-05

        def _bn(h, g, b, m, v):
            scale = g / jnp.sqrt(v + EPS)
            return h * scale[None, :, None] + (b - m * scale)[None, :, None]

        def _conv1d(h, w, pad):
            return lax.conv_general_dilated(h, w, window_strides=(1,), padding=[(pad, pad)], dimension_numbers=('NCH', 'OIH', 'NCH'))
        d = x.shape[-1]
        xc = jnp.transpose(x, (0, 2, 1))
        h = _bn(_conv1d(xc, conv1_w, 0), bn1_g, bn1_b, bn1_m, bn1_v)
        h = jax.nn.relu(h)
        h = _bn(_conv1d(h, conv2_w, 8), bn2_g, bn2_b, bn2_m, bn2_v)
        x_conv = jnp.transpose(jax.nn.relu(h + xc), (0, 2, 1))
        s = x @ w_se.T + b_se
        sq = jnp.sum(s * s, axis=-1)
        dist = sq[:, :, None] + sq[:, None, :] - 2.0 * jnp.einsum('bnd,bmd->bnm', s, s)
        A = jnp.exp(-dist) * mask
        msg = jax.nn.relu(x @ w_msg.T + b_msg)
        x_nmp = jnp.einsum('bnm,bmd->bnd', A, msg)
        x_in = jnp.concatenate([x_conv, x_nmp], axis=-1)
        gi = x_in @ w_ih.T + b_ih
        gh = x @ w_hh.T + b_hh
        gi_r, gi_z, gi_n = (gi[..., :d], gi[..., d:2 * d], gi[..., 2 * d:])
        gh_r, gh_z, gh_n = (gh[..., :d], gh[..., d:2 * d], gh[..., 2 * d:])
        r = jax.nn.sigmoid(gi_r + gh_r)
        z = jax.nn.sigmoid(gi_z + gh_z)
        nn_ = jnp.tanh(gi_n + r * gh_n)
        return (1.0 - z) * nn_ + z * x
    x = _layernorm(x + _L0_gnn_ref(x, adj, L0_gnn_weight, L0_gnn_bias), axis=-1)
    x = _layernorm(x + _L1_gnn_ref(x, adj, L1_gnn_W1, L1_gnn_b1, L1_gnn_W2, L1_gnn_b2, L1_gnn_fusion_w), axis=-1)
    x = _layernorm(x + _L2_gnn_ref(x, adj, L2_gnn_W_w, L2_gnn_W_b, L2_gnn_a_w, L2_gnn_a_b), axis=-1)
    x = _layernorm(x + _L3_gnn_ref(x, adj, L3_gnn_w_se, L3_gnn_b_se, L3_gnn_conv1_w, L3_gnn_bn1_g, L3_gnn_bn1_b, L3_gnn_bn1_m, L3_gnn_bn1_v, L3_gnn_conv2_w, L3_gnn_bn2_g, L3_gnn_bn2_b, L3_gnn_bn2_m, L3_gnn_bn2_v, L3_gnn_w_msg, L3_gnn_b_msg, L3_gnn_w_ih, L3_gnn_b_ih, L3_gnn_w_hh, L3_gnn_b_hh), axis=-1)
    return x

_drawn_inputs = setup_inputs


def setup_inputs(seed=0):
    import zlib

    import numpy as np

    out = dict(_drawn_inputs(seed))
    spreads = {'L1_gnn_b1': (0.0, 2.0),
     'L1_gnn_b2': (0.0, 0.8),
     'L1_gnn_fusion_w': (1.0, 0.6),
     'L3_gnn_b_se': (0.0, 2.0),
     'L3_gnn_bn1_g': (1.0, 0.57),
     'L3_gnn_bn1_b': (0.0, 0.444),
     'L3_gnn_bn1_m': (0.0, 0.35),
     'L3_gnn_bn1_v': (1.0, 0.6),
     'L3_gnn_bn2_g': (1.0, 0.2),
     'L3_gnn_bn2_b': (0.0, 0.742),
     'L3_gnn_bn2_m': (0.0, 0.693),
     'L3_gnn_bn2_v': (1.0, 0.6),
     'L3_gnn_b_msg': (0.0, 0.625),
     'L3_gnn_b_ih': (0.0, 0.308),
     'L3_gnn_b_hh': (0.0, 0.393)}
    factors = {'L1_gnn_W1': 3.037}
    for name, (base, spread) in spreads.items():
        noise = np.random.default_rng([zlib.crc32(name.encode()), seed]).standard_normal(out[name].shape)
        drawn = base * np.exp(spread * noise) if base else spread * noise
        out[name] = jnp.asarray(drawn.astype(out[name].dtype))
    for name, factor in factors.items():
        out[name] = (out[name] * factor).astype(out[name].dtype)
    return out
```

```python
import concourse.bass as bass
from concourse import mybir
from contextlib import ExitStack

B, N, D = 16, 512, 128
NC = N // 128
HID = 256
GROUPS = [[(0, 25)], [(0, 9)], [(0, 1), (9, 15)], [(6, 9), (12, 15)], [(3, 6), (9, 12)]]
NG = len(GROUPS)
NODES = 25
SLOT = 32
GT = B // 4
TAPS = 17
PAD = TAPS // 2
EVEN, ODD = TAPS // 2 + 1, TAPS // 2
HALF = N // 2
HP = PAD // 2
PH = HALF + 2 * HP + 2
P1W = HALF + 2
EPS = 1e-5
SE, CONV1, IH, HH, TAP, SUMTAP = 0, 1, 2, 8, 11, 28
NW = SUMTAP + EVEN - 1
A1, A2, WB, G1, BB1, M1, V1, G2, BB2, M2, V2, BIH, BHH, HB = 0, 1, 2, 3, 4, 5, 6, 7, 8, 9, 10, 11, 14, 17
NROWS = HB + NG * HID // 128
NCST = 6 + 2 * NC + 4


def network_kernel(nc, a, out):
    f32 = mybir.dt.float32
    f32r = mybir.dt.float32r
    ALU = mybir.AluOpType
    ACT = mybir.ActivationFunctionType
    X = mybir.AxisListType.X

    ctx = ExitStack()
    with ctx:
        def sb(name, shape, dt=f32):
            return ctx.enter_context(nc.sbuf_tensor(name, shape, dt))

        def sem(name):
            return ctx.enter_context(nc.semaphore(name))

        def sems(name, n):
            return [sem(f"{name}{i}") for i in range(n)]

        def f(ap):
            return ap.bitcast(f32)

        fused_dram = nc.dram_tensor("fused_dram", (B, SLOT, D), f32, kind="Internal").ap()

        bank = [ctx.enter_context(nc.psum_tensor(f"bank{i}", [128, 512], f32)) for i in range(8)]
        AT_BANK = [bank[0], bank[1]]
        X_BANK = bank[2]
        CV_BANK = bank[3]
        MS_BANK = bank[4]
        AG_BANK = bank[5]
        SQ_BANK = bank[6]
        HN_BANK = bank[7]

        ident = sb("ident", [128, 128])
        ones = sb("ones", [128, 128])
        neg_half = sb("neg_half", [128, NG])
        bias0 = sb("bias0", [128, D])
        w0 = sb("w0", [128, D])
        wb_bc = sb("wb_bc", [128, D])
        v12 = sb("v12", [128, 2, D])
        c12 = sb("c12", [128, 2])
        ab_col = sb("ab_col", [128, 1])
        plainT = sb("plainT", [128, 2, 128])
        wwT, wmsgT = plainT[:, 0, :], plainT[:, 1, :]
        w_hi = sb("w_hi", [128, NW, 128], f32r)
        w_lo = sb("w_lo", [128, NW, 128], f32r)
        msg_bias_f = sb("msg_bias_f", [64, NC, D])
        msg_bias = sb("msg_bias", [64, NC, D], f32r)
        ones_r = sb("ones_r", [64, 128], f32r)
        cols = sb("cols", [128, NROWS])
        bn_scale = sb("bn_scale", [128, 2])
        bn_bias = sb("bn_bias", [128, 2])
        gate_bias = sb("gate_bias", [128, 3])
        se_bias = sb("se_bias", [128, 1])
        part_mask = sb("part_mask", [128, 2])
        sq_pick = sb("sq_pick", [128, 128])

        adj_nat = [sb(f"adj_nat{i}", [128, NC, N]) for i in range(2)]
        x_nat = [sb(f"x_nat{i}", [128, NC, D]) for i in range(2)]
        fused_in = [sb(f"fused_in{i}", [NODES, D]) for i in range(2)]
        aT_hi = sb("aT_hi", [128, NC, N], f32r)
        aT_lo = sb("aT_lo", [128, NC, N], f32r)
        x_hi = sb("x_hi", [128, NC, D], f32r)
        x_lo = sb("x_lo", [128, NC, D], f32r)
        x1 = sb("x1", [128, NC, D])
        x2 = sb("x2", [128, NC, D])
        y3 = sb("y3", [128, NC, D])
        agg_sb = sb("agg_sb", [128, N])
        ef = sb("ef", [128, 2, NC])
        pef = sb("pef", [128, 2, NC])
        pf2 = sb("pf2", [128, NC, 2], f32r)
        den_sb = sb("den_sb", [2, N])
        dq = sb("dq", [128, 3, NC])
        x3 = sb("x3", [128, NC, D])
        st = [sb(f"st{i}", [128, NC, 6]) for i in range(4)]
        mv = [sb(f"mv{i}", [128, NC, 2]) for i in range(4)]
        ve = [sb(f"ve{i}", [128, NC]) for i in range(4)]
        rs = [sb(f"rs{i}", [128, NC]) for i in range(4)]
        nmr = sb("nmr", [128, NC])
        nms = sb("nms", [128, NC])
        x3T = sb("x3T", [128, N])
        x3T_hi = sb("x3T_hi", [128, N], f32r)
        x3T_lo = sb("x3T_lo", [128, N], f32r)
        c1 = sb("c1", [128, 2, PH])
        c1_hi = sb("c1_hi", [128, 2, PH], f32r)
        c1_lo = sb("c1_lo", [128, 2, PH], f32r)
        cs = sb("cs", [128, PH])
        cs_hi = sb("cs_hi", [128, PH], f32r)
        cs_lo = sb("cs_lo", [128, PH], f32r)
        msg_hi = sb("msg_hi", [128, N], f32r)
        msg_lo = sb("msg_lo", [128, N], f32r)
        sC = sb("sC", [128, N])
        sH = sb("sH", [96, N], f32r)
        Lf = sb("Lf", [96, N], f32r)
        Rf = sb("Rf", [96, N], f32r)
        xc_hi = sb("xc_hi", [128, N], f32r)
        xc_lo = sb("xc_lo", [128, N], f32r)
        nmp_hi = sb("nmp_hi", [128, N], f32r)
        nmp_lo = sb("nmp_lo", [128, N], f32r)
        P_hi = sb("P_hi", [128, NC, N], f32r)
        P_lo = sb("P_lo", [128, NC, N], f32r)
        y_out = sb("y_out", [128, NC, D])
        tv = sb("tv", [128, 2, NC, D])
        x1P = sb("x1P", [128, GT, D])

        ARENA = 10240
        arena = sb("arena", [128, ARENA])

        def carver(flat):
            used = [0]

            def carve(*shape):
                size = 1
                for s in shape:
                    size *= s
                ap = flat[:, used[0]:used[0] + size]
                used[0] += size
                if len(shape) == 2:
                    return ap.rearrange("p (a b) -> p a b", a=shape[0])
                if len(shape) == 3:
                    return ap.rearrange("p (a b c) -> p a b c", a=shape[0], b=shape[1])
                return ap
            return carve

        carve = carver(arena)
        aT = [carve(NC, N) for _ in range(2)]
        E = carve(2, N)
        P = carve(2, N)
        P0s = carve(HALF)
        conv = carve(N)
        gh, th_r, th_z, nn, gd, ga = [carve(N) for _ in range(6)]
        carve = carver(arena)
        adjP = carve(GT, N)
        nadjT = carve(GT, NG, 128)
        U = carve(NG, GT, 128)
        hw1 = carve(NG, HID)
        hw2 = carve(NG, 2, D)
        carve = carver(arena[:, GT * N:])
        nat_ww = carve(2, 128)
        nat_se = carve(128)
        nat_c1 = carve(128)
        nat_ih = carve(3, 2, 128)
        nat_hh = carve(3, 128)
        nat_c2 = carve(D, TAPS)
        nat_sum = carve(D, ODD)
        abc = carve(2, 128)
        carve = carver(adj_nat[0][:, :, :].rearrange("p c n -> p (c n)"))
        CM = carve(NG, 128)
        GM = carve(NG, 128)
        A5 = carve(NG, 128)
        A0 = carve(128)
        carve = carver(adj_nat[1][:, :, :].rearrange("p c n -> p (c n)"))
        hT = carve(2, N)
        S2 = carve(N)
        R2 = carve(N)
        xr = [x1, x2, y3, x3]
        xP = y_out
        aPT = [agg_sb[:, :], x3T[:, :]]
        TTs = sC
        fusedP = x3
        mb_rest = tv[0:64, 0]
        vrows = sb("vrows", [32, 128])
        fw = sb("fw", [128, 4, NG])
        fmx = sb("fmx", [128, 3])
        rm = sb("rm", [128, NG])
        wm = sb("wm", [128, NG])
        mk = sb("mk", [128, 2, 128])
        deg = sb("deg", [128, 4, NG])
        hb2 = sb("hb2", [1, NG, D])
        b2row = sb("b2row", [1, N])
        stP = sb("stP", [128, 6])
        mvP = sb("mvP", [128, 2])
        veP = sb("veP", [128, 1])
        rsP = sb("rsP", [128, 1])

        def wait(eng, s, count):
            if not (isinstance(count, int) and count <= 0):
                eng.wait_ge(s, count)

        def hold(eng, s, count):
            if not (isinstance(count, int) and count <= 0):
                eng.wait_ge(s, count)
                eng.nop(nofuse=True)

        def over_graphs(eng, step, end=B - 1):
            def fixed(b):
                step(lambda k: b + k, lambda k: 16 * ((b + k) // 2 + 1), b % 2, lambda k: b + k,
                     lambda k: 0 <= b + k < B, 16 * b)
            fixed(-1)
            fixed(0)
            with eng.Fori(1, end, 2) as b:
                v = [eng.snap(b + k) for k in range(0, 4)]
                d = [eng.snap(b * 8 + k) for k in (8, 24, 40)]
                o = [eng.snap(b * 16 + k) for k in (0, 16)]
                for h in range(2):
                    step(lambda k, h=h: v[h + k], lambda k, h=h: d[(h + k + 1) // 2], (1 + h) % 2,
                         lambda k, h=h: b + (h + k), lambda k: True, o[h])
            for b in range(end, B + 1):
                fixed(b)

        def three(pe, o, lh, ll, rh, rl, start, stop):
            nc.tensor.matmul(o, lh, rh, start=start, stop=False)
            nc.tensor.matmul(o, lh, rl, start=False, stop=False)
            return nc.tensor.matmul(o, ll, rh, start=False, stop=stop)

        def ch(c):
            return slice(c * 128, (c + 1) * 128)

        def bc(ap, n):
            return ap.unsqueeze(1).to_broadcast([128, n, ap.shape[-1]])

        def spread(ap, n):
            return ap.unsqueeze(2).to_broadcast([128, ap.shape[-1], n])

        x_v = a["x"].rearrange("b (c p) d -> b p c d", p=128)
        adj_v = a["adj"].rearrange("b (c p) m -> b p c m", p=128)
        out_v = out.rearrange("b (c p) d -> b p c d", p=128)
        four = "(t j) n d -> j n t d"

        x_in, adj_in, f_in = sems("x_in", 2), sems("adj_in", 2), sems("f_in", 2)

        before = [nc.alloc_semaphore(name=f"before{i}") for i in range(71)]
        (q_zero, q_ident, q_mask, q_row, q_cols, q_colsb, q_wt, q_cst, q_adjP, q_xP, q_h, q_bnv, q_bnr, q_bns,
         q_sc, q_sum, q_abc, q_mt, q_gm, q_v, q_vsb, q_c12, q_wps, q_whi, q_wlo, q_fm, q_fs, q_fe, q_fd, q_fr,
         q_wm, q_aP, q_aPT, q_TT, q_TTs, q_o, q_xPb, q_yP, q_stP, q_mvP, q_veP, q_rsP, q_x1P, q_A0, q_A1, q_A5,
         q_dg, q_dg1, q_dg2, q_dgp, q_dgz, q_dgi, q_B, q_BT, q_nT, q_U, q_Us, q_h2, q_hT, q_S2, q_S2s, q_o2, q_R2,
         q_fu, q_fout, q_mb, q_gb) = before[:67]
        q_xr = before[67:]

        blocks = ([nat_ww[:, 0, :], nat_ww[:, 1, :]], [nat_se, nat_c1[:, :]]
                  + [nat_ih[:, g, h, :] for g in range(3) for h in range(2)] + [nat_hh[:, g, :] for g in range(3)]
                  + [nat_c2[:, :, k] for k in range(TAPS)] + [nat_sum[:, :, k] for k in range(ODD)])
        WG = NW // 4

        def tapblk(i):
            if i < EVEN:
                return TAP + 2 * i
            if i < TAPS:
                return TAP + 2 * (i - EVEN) + 1
            return TAP if i == TAPS else SUMTAP + i - TAPS - 1

        with nc.Block() as block:
            @block.sync
            def _(sp):
                sp.dma_start(nat_ww[:, 0, :], a["L2_gnn_W_w"]).then_inc(q_wt, 16)
                sp.dma_start(nat_ww[:, 1, :], a["L3_gnn_w_msg"]).then_inc(q_wt, 16)
                sp.dma_start(nat_c1, a["L3_gnn_conv1_w"].rearrange("o i k -> o (i k)")).then_inc(q_wt, 16)
                sp.dma_start(nat_ih, a["L3_gnn_w_ih"].rearrange("(g o) (h k) -> o g h k", g=3, h=2)).then_inc(q_wt, 16)
                sp.dma_start(nat_hh, a["L3_gnn_w_hh"].rearrange("(g o) k -> o g k", g=3)).then_inc(q_wt, 16)
                sp.dma_start(nat_c2, a["L3_gnn_conv2_w"]).then_inc(q_wt, 16)
                for j in range(4):
                    if j == 0:
                        sp.wait_ge(q_zero, 1)
                    sp.dma_start(nat_se[3 * j:3 * j + 3, :], a["L3_gnn_w_se"]).then_inc(q_wt, 16)
                for j in range(4):
                    sp.dma_start(adjP[SLOT * j:SLOT * (j + 1), :, :],
                                 a["adj"].rearrange("(t j) n m -> j n t m", j=4)[j, 0:SLOT]).then_inc(q_adjP, 16)
                    sp.dma_start(xP[SLOT * j:SLOT * (j + 1), :, :],
                                 a["x"].rearrange(four, j=4)[j, 0:SLOT]).then_inc(q_xP, 16)
                for t in range(GT):
                    for j in range(4):
                        if t > 0:
                            sp.wait_ge(q_TT, t)
                        sp.dma_start(xr[j][:, :, :], x_v[4 * t + j]).then_inc(q_xr[j], 16)
                    if t == 0:
                        sp.dma_start(hw1, a["L1_gnn_W1"].rearrange("g i h -> i g h")).then_inc(q_h, 16)
                        sp.dma_start(hw2, a["L1_gnn_W2"].rearrange("g (h p) o -> p g h o", h=2)).then_inc(q_h, 16)
                sp.dma_start(x_nat[0][:, :, :], x_v[0]).then_inc(x_in[0], 16)
                sp.wait_ge(q_nT, GT)
                sp.dma_start(adj_nat[0][:, :, :], adj_v[0]).then_inc(adj_in[0], 16)
                sp.wait_ge(q_fu, NG)
                for j in range(4):
                    sp.dma_start(fused_dram.rearrange(four, j=4)[j],
                                 fusedP[SLOT * j:SLOT * (j + 1), :, :]).then_inc(q_fout, 16)
                sp.wait_ge(q_fout, 16 * 4)
                sp.dma_start(fused_in[0][:, :], fused_dram[0, 0:NODES]).then_inc(f_in[0], 16)

            @block.gpsimd
            def _(pool):
                g = nc.gpsimd
                g.memset(ident[:, :], 0.0)
                g.memset(nat_se, 0.0)
                g.memset(se_bias[:, :], 0.0)
                g.memset(msg_bias_f[:, :, :], 0.0).then_inc(q_zero, 1)
                for tile_, value in ((ones[:, :], 1.0), (neg_half[:, :], -0.5), (f(ones_r[:, :]), 1.0), (c1[:, :, :], 0.0),
                                     (sq_pick[:, :], 0.0),
                                     (mk[:, :, :], 0.0), (CM, 0.0)):
                    g.memset(tile_, value)
                g.memset(A0, 0.0).then_inc(q_zero, 1)
                pool.wait_ge(q_zero, 2)
                g.affine_select(out=ident[:, :], in_=ident[:, :], compare_op=ALU.not_equal, fill=1.0, base=0,
                                pattern=[[-1, 128]], channel_multiplier=1).then_inc(q_ident, 1)
                pool.wait_ge(q_colsb, 1)
                pool.nop(nofuse=True)
                g.tensor_scalar(bn_bias[:, :], cols[:, V1:V2 + 1:V2 - V1], EPS, None, ALU.add).then_inc(q_bnv, 1)
                pool.wait_ge(q_bnv, 1)
                g.tensor_tensor(bn_scale[:, :], bn_bias[:, :], neg_half[:, 0:2], ALU.pow).then_inc(q_bnr, 1)
                pool.wait_ge(q_xP, 16 * 4)
                pool.wait_ge(q_cst, 16 * NCST)
                g.tensor_tensor(xP[:, :, :], xP[:, :, :], bc(bias0[:, :], GT), ALU.add).then_inc(q_xPb, 1)
                for t in range(GT):
                    pool.wait_ge(q_dg2, t + 1)
                    g.tensor_tensor(deg[:, 2, :], deg[:, 0, :], neg_half[:, :], ALU.pow).then_inc(q_dgp, 1)
                    pool.wait_ge(q_mvP, t + 1)
                    g.tensor_scalar(veP[:, :], mvP[:, 1:2], EPS, None, ALU.add).then_inc(q_veP, 1)
                    pool.wait_ge(q_veP, t + 1)
                    g.tensor_tensor(rsP[:, :], veP[:, :], neg_half[:, 0:1], ALU.pow).then_inc(q_rsP, 1)

            @block.scalar
            def _(act):
                s = nc.scalar

                def copy_U(t):
                    act.wait_ge(q_U, t + 1)
                    s.activation(U[:, 0:4, t, :], bank[2 + t % 2][:, :].rearrange("p (a b) -> p a b", a=4), ACT.Identity)
                    s.activation(U[:, 4, t, :], bank[4 + t % 2][:, 128:256], ACT.Identity).then_inc(q_Us, 1)

                for row, name, n in ((A1, "L2_gnn_a_w", 2), (WB, "L2_gnn_W_b", 1), (G1, "L3_gnn_bn1_g", 1),
                                     (BB1, "L3_gnn_bn1_b", 1), (M1, "L3_gnn_bn1_m", 1), (V1, "L3_gnn_bn1_v", 1),
                                     (G2, "L3_gnn_bn2_g", 1), (BB2, "L3_gnn_bn2_b", 1), (M2, "L3_gnn_bn2_m", 1),
                                     (V2, "L3_gnn_bn2_v", 1), (BIH, "L3_gnn_b_ih", 3), (BHH, "L3_gnn_b_hh", 3)):
                    act.dma_start(vrows[row:row + n, :], a[name].rearrange("(n d) -> n d", n=n)).then_inc(q_row, 16)
                act.dma_start(vrows[HB:NROWS, :], a["L1_gnn_b1"].rearrange("g (h d) -> (g h) d", h=2)).then_inc(q_row, 16)
                for dst, src in ((w0[:, :], a["L0_gnn_weight"]),
                                 (bias0[:, :], a["L0_gnn_bias"].partition_broadcast(128)),
                                 (wb_bc[:, :], a["L2_gnn_W_b"].partition_broadcast(128)),
                                 (ab_col[:, :], a["L2_gnn_a_b"].partition_broadcast(128)),
                                 (fw[:, 0, :], a["L1_gnn_fusion_w"].partition_broadcast(128)),
                                 (hb2[:, :, :], a["L1_gnn_b2"].rearrange("g o -> (g o)").unsqueeze(0))):
                    act.dma_start(dst, src).then_inc(q_cst, 16)
                act.wait_ge(q_zero, 1)
                for row in (0, 32):
                    for c in range(NC):
                        act.dma_start(msg_bias_f[row:row + 1, c, :], a["L3_gnn_b_msg"].unsqueeze(0)).then_inc(q_cst, 16)
                for j in range(4):
                    act.dma_start(se_bias[3 * j:3 * j + 3, :], a["L3_gnn_b_se"].unsqueeze(1)).then_inc(q_cst, 16)

                act.wait_ge(q_cols, 1)
                s.activation(cols[:, :], bank[7][:, 0:NROWS], ACT.Identity).then_inc(q_colsb, 1)
                act.wait_ge(q_wps, 1)
                s.activation(plainT[:, :, :], bank[0][:, 0:256].rearrange("p (a b) -> p a b", a=2),
                             ACT.Identity).then_inc(q_whi, 1)
                act.wait_ge(q_v, 1)
                s.activation(v12[:, :, :], bank[7][:, 128:384].rearrange("p (a b) -> p a b", a=2),
                             ACT.Identity).then_inc(q_vsb, 1)
                act.wait_ge(q_cst, 16 * NCST)
                s.activation(msg_bias[:, :, :], msg_bias_f[:, :, :], ACT.Identity).then_inc(q_mb, 1)
                for k in range(WG):
                    act.wait_ge(q_wps, k + 2)
                    s.activation(w_hi[:, 4 * k:4 * k + 4, :], bank[(k + 1) % 5][:, :].rearrange("p (a b) -> p a b", a=4),
                                 ACT.Identity).then_inc(q_whi, 1)
                act.wait_ge(q_fs, 1)
                s.activation(fw[:, 2, :], fw[:, 1, :], ACT.Exp).then_inc(q_fe, 1)
                for t in range(GT):
                    act.wait_ge(q_aP, t + 1)
                    if t > 1:
                        act.wait_ge(q_TT, t - 1)
                    s.activation(aPT[t % 2], bank[t % 2][:, :], ACT.Identity).then_inc(q_aPT, 1)
                    act.wait_ge(q_TT, t + 1)
                    s.activation(TTs[:, ch(t)], bank[2 + t % 2][:, 0:128], ACT.Identity).then_inc(q_TTs, 1)
                    if t > 0:
                        copy_U(t - 1)
                copy_U(GT - 1)
                for gi in range(NG):
                    for h in range(2):
                        act.wait_ge(q_h2, 2 * gi + h + 1)
                        if gi > 0:
                            act.wait_ge(q_S2, gi)
                        s.activation(hT[:, h, :], bank[h][:, :], ACT.Relu,
                                     bias=cols[:, HB + 2 * gi + h:HB + 2 * gi + h + 1]).then_inc(q_hT, 1)
                    act.wait_ge(q_S2, gi + 1)
                    if gi > 0:
                        act.wait_ge(q_o2, gi)
                    s.activation(S2, bank[2][:, :], ACT.Identity).then_inc(q_S2s, 1)
                    act.wait_ge(q_o2, gi + 1)
                    act.wait_ge(q_wm, 1)
                    if gi > 0:
                        act.wait_ge(q_fu, gi)
                    s.activation(R2, bank[3][:, :], ACT.Relu, scale=wm[:, gi:gi + 1]).then_inc(q_R2, 1)

            @block.vector
            def _(dve):
                v = nc.vector
                v.memset(f(Lf[64:96, :]), 1.0)
                v.memset(f(Rf[32:64, :]), 1.0)
                dve.wait_ge(q_zero, 2)
                for lo, hi in ((6, 12), (33, 34)):
                    v.memset(mk[:, 0, lo:hi], -1.0)
                for lo, hi in ((3, 6), (9, 12), (65, 66)):
                    v.memset(mk[:, 1, lo:hi], -1.0)
                for lo in (32, 64):
                    v.memset(sq_pick[0:3, lo:lo + 2], -0.5)
                for gi, spans in enumerate(GROUPS):
                    for j in range(4):
                        for lo, hi in spans:
                            last = v.memset(CM[SLOT * j:SLOT * (j + 1), gi, SLOT * j + lo:SLOT * j + hi], 1.0)
                last.then_inc(q_mask, 1)
                dve.wait_ge(q_cst, 16 * NCST)
                v.reduce_max(fmx[:, 0:1], fw[:, 0, :], X).then_inc(q_fm, 1)
                dve.wait_ge(q_fm, 1)
                v.tensor_scalar(fw[:, 1, :], fw[:, 0, :], fmx[:, 0:1], None, ALU.subtract).then_inc(q_fs, 1)
                dve.wait_ge(q_bnr, 1)
                v.tensor_tensor(bn_scale[:, :], bn_scale[:, :], cols[:, G1:G2 + 1:G2 - G1], ALU.mult).then_inc(q_bns, 1)
                dve.wait_ge(q_bns, 1)
                v.tensor_tensor(bn_bias[:, :], cols[:, M1:M2 + 1:M2 - M1], bn_scale[:, :], ALU.mult).then_inc(q_bns, 1)
                dve.wait_ge(q_bns, 2)
                v.tensor_tensor(bn_bias[:, :], cols[:, BB1:BB2 + 1:BB2 - BB1], bn_bias[:, :], ALU.subtract)
                dve.wait_ge(q_wt, 16 * 10)
                v.tensor_scalar(nat_c1, nat_c1, bn_scale[:, 0:1], None, ALU.mult)
                v.tensor_scalar(nat_c2, nat_c2, bn_scale[:, 1:2], None, ALU.mult).then_inc(q_sc, 1)
                dve.wait_ge(q_sc, 1)
                v.tensor_tensor(nat_sum, nat_c2[:, :, 2:TAPS:2], nat_c2[:, :, 1:TAPS:2], ALU.add).then_inc(q_sum, 1)
                for j in range(2):
                    last = v.tensor_scalar(abc[:, j, :], ones[:, :], cols[:, A1 + j:A1 + j + 1], None, ALU.mult)
                last.then_inc(q_abc, 1)
                v.tensor_tensor(gate_bias[:, 0:2], cols[:, BIH:BIH + 2], cols[:, BHH:BHH + 2], ALU.add).then_inc(q_gb, 1)
                dve.wait_ge(q_gb, 1)
                v.tensor_scalar(gate_bias[:, 0:2], gate_bias[:, 0:2], 0.5, None, ALU.mult)
                v.tensor_scalar(gate_bias[:, 2:3], cols[:, BHH + 2:BHH + 3], 0.5, None, ALU.mult)
                dve.wait_ge(q_mt, 1)
                v.tensor_tensor(GM[:, 0:4, :], bank[5][:, :].rearrange("p (a b) -> p a b", a=4), CM[:, 0:4, :], ALU.mult)
                v.tensor_tensor(GM[:, 4, :], bank[6][:, 0:128], CM[:, 4, :], ALU.mult)
                v.reduce_max(rm[:, 0:4], bank[5][:, :].rearrange("p (a b) -> p a b", a=4), X)
                v.reduce_max(rm[:, 4:5], bank[6][:, 0:128], X)
                v.tensor_copy(part_mask[:, :], bank[6][:, 128:384:128]).then_inc(q_gm, 1)
                dve.wait_ge(q_vsb, 1)
                v.tensor_copy(c12[:, :], bank[7][:, 384:386]).then_inc(q_c12, 1)
                dve.wait_ge(q_c12, 1)
                v.tensor_tensor(c12[:, 0:1], c12[:, 0:1], ab_col[:, :], ALU.add)
                dve.wait_ge(q_mb, 1)
                v.tensor_tensor(mb_rest[:, :, :], msg_bias_f[:, :, :], f(msg_bias[:, :, :]), ALU.subtract).then_inc(q_mb, 1)
                dve.wait_ge(q_mb, 2)
                v.tensor_copy(msg_bias[32:64, :, :], mb_rest[32:64, :, :]).then_inc(q_mb, 1)
                for k in range(WG):
                    dve.wait_ge(q_whi, k + 2)
                    v.tensor_tensor(w_lo[:, 4 * k:4 * k + 4, :], bank[(k + 1) % 5][:, :].rearrange("p (a b) -> p a b", a=4),
                                    f(w_hi[:, 4 * k:4 * k + 4, :]), ALU.subtract).then_inc(q_wlo, 1)
                dve.wait_ge(q_fe, 1)
                v.reduce_sum(fmx[:, 1:2], fw[:, 2, :], X).then_inc(q_fd, 1)
                dve.wait_ge(q_fd, 1)
                v.reciprocal(fmx[:, 2:3], fmx[:, 1:2]).then_inc(q_fr, 1)
                dve.wait_ge(q_fr, 1)
                dve.wait_ge(q_gm, 1)
                v.scalar_tensor_tensor(wm[:, :], fw[:, 2, :], fmx[:, 2:3], rm[:, :], ALU.mult, ALU.mult).then_inc(q_wm, 1)
                dve.wait_ge(q_adjP, 16 * 4)
                dve.wait_ge(q_zero, 2)
                dve.wait_ge(q_ident, 1)
                for t in range(GT):
                    if t > 0:
                        dve.wait_ge(q_A5, t)
                    for j in range(4):
                        last = v.tensor_copy(A0[SLOT * j:SLOT * (j + 1), SLOT * j:SLOT * (j + 1)],
                                             adjP[SLOT * j:SLOT * (j + 1), t, 0:SLOT])
                    last.then_inc(q_A0, 1)
                    dve.wait_ge(q_A0, t + 1)
                    v.tensor_tensor(A0, A0, ident[:, :], ALU.add).then_inc(q_A1, 1)
                    dve.wait_ge(q_A1, t + 1)
                    if t > 0:
                        dve.wait_ge(q_BT, t)
                    v.tensor_tensor(A5, bc(A0, NG), GM, ALU.mult).then_inc(q_A5, 1)
                    dve.wait_ge(q_A5, t + 1)
                    v.reduce_sum(deg[:, 3, :], A5, X).then_inc(q_dg, 1)
                    dve.wait_ge(q_dg, t + 1)
                    v.tensor_scalar(deg[:, 1, :], deg[:, 3, :], 0.0, None, ALU.is_equal).then_inc(q_dg1, 1)
                    dve.wait_ge(q_dg1, t + 1)
                    v.tensor_tensor(deg[:, 0, :], deg[:, 3, :], deg[:, 1, :], ALU.add).then_inc(q_dg2, 1)
                    v.tensor_scalar(deg[:, 1, :], deg[:, 1, :], -1.0, 1.0, ALU.mult, ALU.add).then_inc(q_dgz, 1)
                    dve.wait_ge(q_dgz, t + 1)
                    dve.wait_ge(q_dgp, t + 1)
                    v.tensor_tensor(deg[:, 3, :], deg[:, 2, :], deg[:, 1, :], ALU.mult).then_inc(q_dgi, 1)
                    dve.wait_ge(q_dgi, t + 1)
                    v.tensor_tensor(A5, A5, spread(deg[:, 3, :], 128), ALU.mult).then_inc(q_B, 1)
                    dve.wait_ge(q_o, t + 1)
                    dve.wait_ge(q_xPb, 1)
                    v.tensor_tensor(x1P[:, t, :], bank[4 + t % 2][:, 0:128], xP[:, t, :], ALU.add).then_inc(q_yP, 1)
                    dve.wait_ge(q_yP, t + 1)
                    v.bn_stats(stP[:, :], x1P[:, t, :]).then_inc(q_stP, 1)
                    dve.wait_ge(q_stP, t + 1)
                    v.bn_aggr(mvP[:, :], stP[:, :]).then_inc(q_mvP, 1)
                    dve.wait_ge(q_BT, t + 1)
                    v.tensor_tensor(nadjT[:, t, 0:4, :], bank[6][:, :].rearrange("p (a b) -> p a b", a=4),
                                    spread(deg[:, 3, 0:4], 128), ALU.mult)
                    v.tensor_scalar(nadjT[:, t, 4, :], bank[7][:, 0:128], deg[:, 3, 4:5], None, ALU.mult).then_inc(q_nT, 1)
                    dve.wait_ge(q_rsP, t + 1)
                    v.tensor_scalar(x1P[:, t, :], x1P[:, t, :], mvP[:, 0:1], rsP[:, :], ALU.subtract,
                                    ALU.mult).then_inc(q_x1P, 1)
                fusedF = fusedP[:, :, :].rearrange("p t d -> p (t d)")
                for gi in range(NG):
                    dve.wait_ge(q_R2, gi + 1)
                    if gi == 0:
                        v.tensor_copy(fusedF, R2).then_inc(q_fu, 1)
                    else:
                        dve.wait_ge(q_fu, gi)
                        v.tensor_tensor(fusedF, fusedF, R2, ALU.add).then_inc(q_fu, 1)

            @block.tensor
            def _(pe):
                t_ = nc.tensor
                pe.wait_ge(q_ident, 1)
                pe.wait_ge(q_row, 16 * 13)
                t_.transpose(bank[7][:, 0:NROWS], vrows[0:NROWS, :], ident[0:NROWS, 0:NROWS]).then_inc(q_cols, 1)
                pe.wait_ge(q_mask, 1)
                for gi in range(NG):
                    t_.transpose(bank[5 + gi // 4][:, ch(gi % 4)], CM[:, gi, :], ident[:, :])
                t_.transpose(bank[6][:, ch(1)], mk[:, 0, :], ident[:, :])
                t_.transpose(bank[6][:, ch(2)], mk[:, 1, :], ident[:, :]).then_inc(q_mt, 1)
                pe.wait_ge(q_wt, 16 * 10)
                for i, w in enumerate(blocks[0]):
                    last = t_.transpose(bank[0][:, ch(i)], w, ident[:, :])
                last.then_inc(q_wps, 1)
                pe.wait_ge(q_abc, 1)
                pe.wait_ge(q_colsb, 1)
                for j in range(2):
                    t_.matmul(bank[7][:, ch(1 + j)], abc[:, j, :], nat_ww[:, 0, :], start=True, stop=True)
                    last = t_.matmul(bank[7][:, 384 + j:385 + j], abc[:, j, :], cols[:, WB:WB + 1], start=True, stop=True)
                last.then_inc(q_v, 1)
                pe.wait_ge(q_sum, 1)
                for k in range(WG):
                    if k >= 4:
                        pe.wait_ge(q_whi, k - 3)
                        if k >= 5:
                            pe.wait_ge(q_wlo, k - 4)
                    for i in range(4):
                        last = t_.transpose(bank[(k + 1) % 5][:, ch(i)], blocks[1][4 * k + i], ident[:, :])
                    last.then_inc(q_wps, 1)
                pe.wait_ge(q_adjP, 16 * 4)
                pe.wait_ge(q_whi, WG + 1)
                pe.wait_ge(q_wlo, WG)
                pe.wait_ge(q_gm, 1)
                pe.wait_ge(q_c12, 1)
                pe.wait_ge(q_vsb, 1)
                pe.wait_ge(q_cst, 16 * NCST)

                def transpose_rows(t):
                    for mc in range(NC):
                        last = t_.transpose(bank[t % 2][:, ch(mc)], adjP[:, t, ch(mc)], ident[:, :])
                    last.then_inc(q_aP, 1)
                transpose_rows(0)
                for t in range(GT):
                    pe.wait_ge(q_aPT, t + 1)
                    if t > 1:
                        pe.wait_ge(q_Us, t - 1)
                    for j in range(4):
                        pe.wait_ge(q_xr[j], 16 * (t + 1))
                        for mc in range(NC):
                            last = t_.matmul(bank[2 + t % 2][:, SLOT * j:SLOT * (j + 1)], xr[j][:, mc, :],
                                             aPT[t % 2][:, 128 * mc + SLOT * j:128 * mc + SLOT * (j + 1)],
                                             start=(mc == 0), stop=(mc == NC - 1))
                    last.then_inc(q_TT, 1)
                    if t + 1 < GT:
                        transpose_rows(t + 1)
                    pe.wait_ge(q_B, t + 1)
                    if t > 0:
                        pe.wait_ge(q_nT, t)
                    for gi in range(NG):
                        last = t_.transpose(bank[6 + gi // 4][:, ch(gi % 4)], A5[:, gi, :], ident[:, :])
                    last.then_inc(q_BT, 1)
                    pe.wait_ge(q_TTs, t + 1)
                    t_.matmul(bank[4 + t % 2][:, 0:128], TTs[:, ch(t)], w0[:, :], start=True, stop=True).then_inc(q_o, 1)
                    pe.wait_ge(q_x1P, t + 1)
                    pe.wait_ge(q_nT, t + 1)
                    for gi in range(NG):
                        o = bank[2 + t % 2][:, ch(gi)] if gi < 4 else bank[4 + t % 2][:, 128:256]
                        last = t_.matmul(o, x1P[:, t, :], nadjT[:, t, gi, :], start=True, stop=True)
                    last.then_inc(q_U, 1)
                pe.wait_ge(q_h, 16 * 2)
                pe.wait_ge(q_Us, GT)

                def hidden(gi):
                    for h in range(2):
                        if gi > 0:
                            pe.wait_ge(q_hT, 2 * gi - 1 + h)
                        t_.matmul(bank[h][:, :], hw1[:, gi, ch(h)], U[:, gi, :, :].rearrange("p t n -> p (t n)"),
                                  start=True, stop=True).then_inc(q_h2, 1)
                hidden(0)
                for gi in range(NG):
                    pe.wait_ge(q_hT, 2 * gi + 2)
                    if gi > 0:
                        pe.wait_ge(q_S2s, gi)
                    for t in range(GT):
                        for h in range(2):
                            last = t_.matmul(bank[2][:, ch(t)], hT[:, h, ch(t)], hw2[:, gi, h, :],
                                             start=(h == 0), stop=(h == 1))
                    last.then_inc(q_S2, 1)
                    if gi + 1 < NG:
                        hidden(gi + 1)
                    pe.wait_ge(q_S2s, gi + 1)
                    if gi > 0:
                        pe.wait_ge(q_R2, gi)
                    for t in range(GT):
                        t_.matmul(bank[3][:, ch(t)], ones[0:1, :], hb2[0:1, gi, :], start=True, stop=False)
                        last = t_.matmul(bank[3][:, ch(t)], nadjT[:, t, gi, :], S2[:, ch(t)], start=False, stop=True)
                    last.then_inc(q_o2, 1)
                pe.wait_ge(q_mb, 3)
                pe.wait_ge(q_R2, NG)

        nc.clear_and_free_semaphores(before)
        nc.all_engine_barrier()

        pe_aT, ac_aThi, ac_aT, dv_aTlo = sems("pe_aT", NC), sems("ac_aThi", NC), sems("ac_aT", NC), sems("dv_aTlo", NC)
        ac_xhi, dv_xlo, po_xb = sem("ac_xhi"), sem("dv_xlo"), sem("po_xb")
        pe_agg1, ac_agg1, pe_out0, dv_y1 = sem("pe_agg1"), sem("ac_agg1"), sem("pe_out0"), sem("dv_y1")
        dv_st, dv_mv, po_ve, po_rs = sems("dv_st", 4), sems("dv_mv", 4), sems("po_ve", 4), sems("po_rs", 4)
        dv_x1, dv_fused, dv_x2, po_x2b, po_v = sem("dv_x1"), sem("dv_fused"), sem("dv_x2"), sem("po_x2b"), sem("po_v")
        dv_ef, ac_pef, dv_xshi, dv_xslo, dv_pf = sem("dv_ef"), sem("ac_pef"), sem("dv_xshi"), sem("dv_xslo"), sem("dv_pf")
        pe_agg2, pe_den, ac_agg2, ac_den = sem("pe_agg2"), sem("pe_den"), sem("ac_agg2"), sem("ac_den")
        pe_dcol, pe_out2, dv_dq, dv_y3, dv_x3 = sem("pe_dcol"), sem("pe_out2"), sem("dv_dq"), sem("dv_y3"), sem("dv_x3")
        pe_x3T, ac_x3Thi, ac_x3T, dv_x3Tlo = sem("pe_x3T"), sem("ac_x3Thi"), sem("ac_x3T"), sem("dv_x3Tlo")
        pe_s, pe_c1, pe_hn, pe_msg, pe_sq = sem("pe_s"), sem("pe_c1"), sem("pe_hn"), sem("pe_msg"), sem("pe_sq")
        ac_s2, ac_c1, ac_gh, ac_msghi, ac_C, ac_H = [sem(n) for n in ("ac_s2", "ac_c1", "ac_gh", "ac_msghi", "ac_C", "ac_H")]
        dv_c1, dv_cs, dv_csp, dv_msglo, dv_L, dv_R = [sem(n) for n in ("dv_c1", "dv_cs", "dv_csp", "dv_msglo", "dv_L", "dv_R")]
        pe_D, ac_E, dv_P, ac_Phi, po_Plo = sems("pe_D", NC), sems("ac_E", NC), sems("dv_P", NC), sems("ac_Phi", NC), sems("po_Plo", NC)
        pe_P1, pe_P0, pe_Q, ac_P0s, dv_ab, dv_conv = [sem(n) for n in ("pe_P1", "pe_P0", "pe_Q", "ac_P0s", "dv_ab", "dv_conv")]
        ac_xchi, dv_xclo, pe_N, ac_nmphi, dv_nmplo = [sem(n) for n in ("ac_xchi", "dv_xclo", "pe_N", "ac_nmphi", "dv_nmplo")]
        pe_z, pe_r, pe_gn, ac_thz, ac_thr, ac_nn = [sem(n) for n in ("pe_z", "pe_r", "pe_gn", "ac_thz", "ac_thr", "ac_nn")]
        dv_t, po_g, dv_y4, pe_yT = [sem(n) for n in ("dv_t", "po_g", "dv_y4", "pe_yT")]
        po_nms, dv_c1h, dv_csh, dv_q0, dv_q1, dv_q, dv_pfh, dv_t0, dv_m = [sem(n) for n in (
            "po_nms", "dv_c1h", "dv_csh", "dv_q0", "dv_q1", "dv_q", "dv_pfh", "dv_t0", "dv_m")]
        po_nm, ac_out, o_out = sem("po_nm"), sem("ac_out"), sem("o_out")

        block = ctx.enter_context(nc.Block())

        @block.sync
        def _(sp):
            sp.sem_inc(o_out, 16)
            def turn(V, dma, par, graph, has, outs):
                if has(2):
                    wait(sp, ac_xhi, V(1))
                    wait(sp, dv_xlo, V(1))
                    wait(sp, po_xb, V(1))
                    sp.dma_start(x_nat[par][:, :, :], x_v[bass.ds(graph(2), 1)].rearrange("a p c d -> p (a c) d")
                                 ).then_inc(x_in[par], 16)
                    wait(sp, pe_aT[NC - 1], V(1))
                    sp.dma_start(adj_nat[par][:, :, :], adj_v[bass.ds(graph(2), 1)].rearrange("a p c m -> p (a c) m")
                                 ).then_inc(adj_in[par], 16)
                    wait(sp, dv_fused, V(1))
                    sp.dma_start(fused_in[par][:, :],
                                 fused_dram[bass.ds(graph(2), 1), 0:NODES].rearrange("a p d -> p (a d)")
                                 ).then_inc(f_in[par], 16)
                if has(-1):
                    sp.wait_ge(ac_out, V(0))
                    sp.dma_start(out_v[bass.ds(graph(-1), 1)].rearrange("a p c d -> p (a c) d"),
                                 y_out[:, :, :]).then_inc(o_out, 16)

            over_graphs(sp, turn, B - 3)
            sp.wait_ge(o_out, 16 * (B + 1))

        @block.gpsimd
        def _(pool):
            g = nc.gpsimd
            def inverse_root(V, k, i, chunks=NC):
                hold(pool, dv_mv[i], V(k))
                g.tensor_scalar(ve[i][:, :], mv[i][:, :, 1], EPS, None, ALU.add).then_inc(po_ve[i], 1)
                wait(pool, po_ve[i], V(k))
                g.tensor_tensor(rs[i][:, :], ve[i][:, :], neg_half[:, 0:NC], ALU.pow).then_inc(po_rs[i], 1)

            def turn(V, dma, par, graph, has, outs):
                cur, nxt, prev = has(0), has(1), has(-1)
                if nxt:
                    wait(pool, x_in[1 - par], dma(1))
                    wait(pool, dv_x2, V(1))
                    g.tensor_tensor(x1[:, :, :], x_nat[1 - par][:, :, :], bc(bias0[:, :], NC),
                                    ALU.add).then_inc(po_xb, 1)
                if prev:
                    inverse_root(V, 0, 3)
                    wait(pool, po_rs[3], V(0))
                    g.tensor_tensor(nms[:, :], mv[3][:, :, 0], rs[3][:, :], ALU.mult).then_inc(po_nms, 1)
                    hold(pool, po_nms, V(0))
                    g.tensor_scalar(nmr[:, :], nms[:, :], -1.0, None, ALU.mult).then_inc(po_nm, 1)
                if nxt:
                    inverse_root(V, 2, 0)

                def rest(mc):
                    wait(pool, ac_Phi[mc], V(1))
                    wait(pool, pe_N, V(0))
                    g.tensor_tensor(P_lo[:, mc, :], P[:, mc % 2, :], f(P_hi[:, mc, :]),
                                    ALU.subtract).then_inc(po_Plo[mc], 1)
                if cur:
                    rest(0)
                    rest(1)
                if nxt:
                    inverse_root(V, 2, 1)
                    wait(pool, dv_x2, V(2))
                    wait(pool, dv_ef, V(1))
                    g.tensor_tensor(tv[:, 0], x2[:, :, :], bc(v12[:, 0, :], NC), ALU.mult)
                    g.tensor_tensor(tv[:, 1], x2[:, :, :], bc(v12[:, 1, :], NC), ALU.mult).then_inc(po_v, 1)
                if cur:
                    rest(2)
                    rest(3)
                if nxt:
                    wait(pool, dv_x3, V(1))
                    g.tensor_tensor(y3[:, :, :], x2[:, :, :], bc(wb_bc[:, :], NC), ALU.add).then_inc(po_x2b, 1)
                    inverse_root(V, 2, 2)
                if cur:
                    wait(pool, ac_nn, V(1))
                    wait(pool, dv_y4, V(0))
                    wait(pool, pe_yT, V(0))
                    g.tensor_tensor(gd, x3T[:, :], nn, ALU.subtract)
                    g.tensor_tensor(ga, x3T[:, :], nn, ALU.add).then_inc(po_g, 1)

            over_graphs(pool, turn)

        @block.scalar
        def _(act):
            s = nc.scalar
            def turn(V, dma, par, graph, has, outs):
                cur, nxt, prev = has(0), has(1), has(-1)

                def split_adjacency(mc):
                    wait(act, pe_aT[mc], V(2))
                    wait(act, pe_den, V(1))
                    s.activation(aT_hi[:, mc, :], AT_BANK[mc % 2][:, :], ACT.Identity).then_inc(ac_aThi[mc], 1)
                    wait(act, dv_P[NC - 1], V(0))
                    s.activation(aT[1 - par][:, mc, :], AT_BANK[mc % 2][:, :], ACT.Identity).then_inc(ac_aT[mc], 1)

                if cur:
                    wait(act, pe_x3T, V(1))
                    wait(act, pe_gn, V(0))
                    s.activation(x3T_hi[:, :], X_BANK[:, :], ACT.Identity).then_inc(ac_x3Thi, 1)
                    wait(act, dv_y4, V(0))
                    wait(act, po_g, V(0))
                    s.activation(x3T[:, :], X_BANK[:, :], ACT.Identity).then_inc(ac_x3T, 1)
                if nxt:
                    split_adjacency(0)
                    split_adjacency(1)
                if cur:
                    wait(act, pe_s, V(1))
                    wait(act, dv_R, V(0))
                    s.activation(sC[0:32, :], SQ_BANK[0:32, :], ACT.Square, bias=se_bias[0:32, :]).then_inc(ac_s2, 1)
                    wait(act, pe_c1, V(1))
                    wait(act, dv_cs, V(0))
                    s.activation(c1[:, :, HP:HP + HALF], CV_BANK[:, :].rearrange("p (i r) -> p r i", r=2), ACT.Relu,
                                 bias=bn_bias[:, 0:1]).then_inc(ac_c1, 1)
                    wait(act, pe_msg, V(1))
                    wait(act, pe_N, V(0))
                    s.activation(msg_hi[:, :], MS_BANK[:, :], ACT.Relu).then_inc(ac_msghi, 1)
                    wait(act, pe_hn, V(1))
                    wait(act, ac_nn, V(0))
                    s.activation(gh, HN_BANK[:, :], ACT.Identity, bias=gate_bias[:, 2:3], scale=0.5).then_inc(ac_gh, 1)
                if nxt:
                    wait(act, x_in[1 - par], dma(1))
                    wait(act, pe_agg2, V(1))
                    s.activation(x_hi[:, :, :], x_nat[1 - par][:, :, :], ACT.Identity).then_inc(ac_xhi, 1)
                    split_adjacency(2)
                    split_adjacency(3)
                if cur:
                    wait(act, pe_sq, V(1))
                    s.activation(sC[0:96, :], SQ_BANK[0:96, :], ACT.Identity, bias=se_bias[0:96, :]).then_inc(ac_C, 1)
                    wait(act, ac_C, V(1))
                    s.activation(sH[:, :], sC[0:96, :], ACT.Identity).then_inc(ac_H, 1)
                if nxt:
                    wait(act, pe_agg1, V(2))
                    wait(act, pe_out2, V(1))
                    s.activation(agg_sb[:, :], AG_BANK[:, :], ACT.Identity).then_inc(ac_agg1, 1)
                if prev:
                    hold(act, po_nm, V(0))
                    hold(act, o_out, outs)
                    for c in range(NC):
                        last = s.activation(y_out[:, c, :], X_BANK[:, ch(c)], ACT.Identity, bias=nmr[:, c:c + 1],
                                            scale=rs[3][:, c:c + 1])
                    last.then_inc(ac_out, 1)

                def exponential(mc):
                    wait(act, pe_D[mc], V(1))
                    wait(act, dv_P[(mc + 2) % NC], V(0) if mc < 2 else V(1))
                    s.activation(E[:, mc % 2, :], AT_BANK[mc % 2][:, :], ACT.Exp, scale=2.0).then_inc(ac_E[mc], 1)

                def rounded(mc):
                    wait(act, dv_P[mc], V(1))
                    wait(act, pe_N, V(0))
                    s.activation(P_hi[:, mc, :], P[:, mc % 2, :], ACT.Identity).then_inc(ac_Phi[mc], 1)
                if cur:
                    exponential(0)
                    exponential(1)
                    rounded(0)
                    exponential(2)
                    rounded(1)
                    exponential(3)
                    rounded(2)
                    rounded(3)
                    wait(act, pe_Q, V(1))
                    wait(act, dv_conv, V(0))
                    s.activation(P0s, CV_BANK[:, 0:HALF], ACT.Identity).then_inc(ac_P0s, 1)
                if nxt:
                    wait(act, dv_ef, V(2))
                    wait(act, dv_dq, V(1))
                    s.activation(pef[:, 0, :], ef[:, 0, :], ACT.Exp, bias=c12[:, 0:1])
                    s.activation(pef[:, 1, :], ef[:, 1, :], ACT.Exp, bias=c12[:, 1:2]).then_inc(ac_pef, 1)
                if cur:
                    wait(act, dv_conv, V(1))
                    wait(act, pe_gn, V(0))
                    s.activation(xc_hi[:, :], conv, ACT.Relu).then_inc(ac_xchi, 1)
                    wait(act, pe_N, V(1))
                    s.activation(nmp_hi[:, :], X_BANK[:, :], ACT.Identity).then_inc(ac_nmphi, 1)
                if nxt:
                    wait(act, pe_agg2, V(2))
                    s.activation(agg_sb[:, :], AG_BANK[:, :], ACT.Identity).then_inc(ac_agg2, 1)
                    wait(act, pe_den, V(2))
                    wait(act, pe_dcol, V(1))
                    s.activation(den_sb[:, :], SQ_BANK[0:2, :], ACT.Identity).then_inc(ac_den, 1)
                if cur:
                    wait(act, pe_z, V(1))
                    s.activation(th_z, MS_BANK[:, :], ACT.Tanh, bias=gate_bias[:, 1:2], scale=0.5).then_inc(ac_thz, 1)
                    wait(act, pe_r, V(1))
                    s.activation(th_r, CV_BANK[:, :], ACT.Tanh, bias=gate_bias[:, 0:1], scale=0.5).then_inc(ac_thr, 1)
                    wait(act, dv_t, V(1))
                    wait(act, po_g, V(0))
                    s.activation(nn, gh, ACT.Tanh, bias=cols[:, BIH + 2:BIH + 3]).then_inc(ac_nn, 1)

            over_graphs(act, turn)

        @block.vector
        def _(dve):
            v = nc.vector
            def statistics(i, V, k, src):
                for c in range(NC):
                    last = v.bn_stats(st[i][:, c, :], src(c))
                last.then_inc(dv_st[i], 1)
                hold(dve, dv_st[i], V(k))
                for c in range(NC):
                    last = v.bn_aggr(mv[i][:, c, :], st[i][:, c, :])
                last.then_inc(dv_mv[i], 1)

            def normalise(i, V, k, dst, src, done):
                hold(dve, po_rs[i], V(k))
                for c in range(NC):
                    last = v.tensor_scalar(dst[:, c, :], src[:, c, :], mv[i][:, c, 0:1], rs[i][:, c:c + 1],
                                           ALU.subtract, ALU.mult)
                last.then_inc(done, 1)

            def turn(V, dma, par, graph, has, outs):
                cur, nxt, prev = has(0), has(1), has(-1)

                def split_rest(mc):
                    wait(dve, ac_aT[mc], V(2))
                    wait(dve, pe_den, V(1))
                    v.tensor_tensor(aT_lo[:, mc, :], aT[1 - par][:, mc, :], f(aT_hi[:, mc, :]),
                                    ALU.subtract).then_inc(dv_aTlo[mc], 1)

                def weigh(mc):
                    wait(dve, ac_E[mc], V(1))
                    wait(dve, ac_aT[mc], V(1))
                    k = 0 if mc < 2 else 1
                    wait(dve, ac_Phi[(mc + 2) % NC], V(k))
                    wait(dve, po_Plo[(mc + 2) % NC], V(k))
                    v.tensor_tensor(P[:, mc % 2, :], E[:, mc % 2, :], aT[par][:, mc, :], ALU.mult).then_inc(dv_P[mc], 1)

                if cur:
                    wait(dve, ac_x3T, V(1))
                    wait(dve, pe_gn, V(0))
                    v.tensor_tensor(x3T_lo[:, :], x3T[:, :], f(x3T_hi[:, :]), ALU.subtract).then_inc(dv_x3Tlo, 1)
                if nxt:
                    split_rest(0)
                    split_rest(1)
                if cur:
                    wait(dve, ac_c1, V(1))
                    wait(dve, pe_Q, V(0))
                    v.tensor_copy(c1_hi[:, :, :], c1[:, :, :]).then_inc(dv_c1h, 1)
                    v.tensor_tensor(cs[:, :], c1[:, 0, :], c1[:, 1, :], ALU.add).then_inc(dv_cs, 1)
                    wait(dve, dv_c1h, V(1))
                    v.tensor_tensor(c1_lo[:, :, :], c1[:, :, :], f(c1_hi[:, :, :]), ALU.subtract).then_inc(dv_c1, 1)
                    wait(dve, pe_msg, V(1))
                    wait(dve, ac_msghi, V(1))
                    wait(dve, pe_N, V(0))
                    v.scalar_tensor_tensor(msg_lo[:, :], MS_BANK[:, :], 0.0, f(msg_hi[:, :]), ALU.max,
                                           ALU.subtract).then_inc(dv_msglo, 1)
                if nxt:
                    wait(dve, ac_xhi, V(2))
                    wait(dve, x_in[1 - par], dma(1))
                    wait(dve, pe_agg2, V(1))
                    v.tensor_tensor(x_lo[:, :, :], x_nat[1 - par][:, :, :], f(x_hi[:, :, :]),
                                    ALU.subtract).then_inc(dv_xlo, 1)
                    split_rest(2)
                    split_rest(3)
                if cur:
                    wait(dve, dv_cs, V(1))
                    v.tensor_copy(cs_hi[:, :], cs[:, :]).then_inc(dv_csh, 1)
                if prev:
                    hold(dve, pe_yT, V(0))
                    statistics(3, V, 0, lambda c: X_BANK[:, ch(c)])
                if cur:
                    wait(dve, dv_csh, V(1))
                    v.tensor_tensor(cs_lo[:, :], cs[:, :], f(cs_hi[:, :]), ALU.subtract).then_inc(dv_csp, 1)
                    wait(dve, ac_H, V(1))
                    wait(dve, pe_D[NC - 1], V(0))
                    v.scalar_tensor_tensor(Lf[0:64, :], f(sH[0:64, :]), part_mask[0:64, 0:1], sC[0:64, :],
                                           ALU.mult, ALU.add).then_inc(dv_L, 1)
                    v.scalar_tensor_tensor(Rf[0:32, :], f(sH[0:32, :]), part_mask[0:32, 1:2], sC[0:32, :],
                                           ALU.mult, ALU.add)
                    v.scalar_tensor_tensor(Rf[64:96, :], f(sH[64:96, :]), part_mask[64:96, 1:2], sC[64:96, :],
                                           ALU.mult, ALU.add).then_inc(dv_R, 1)
                if nxt:
                    wait(dve, pe_out0, V(2))
                    wait(dve, po_xb, V(2))
                    v.tensor_tensor(x1[:, :, :], AG_BANK[:, :].rearrange("p (c d) -> p c d", c=NC), x1[:, :, :],
                                    ALU.add).then_inc(dv_y1, 1)
                    hold(dve, dv_y1, V(2))
                    statistics(0, V, 2, lambda c: x1[:, c, :])
                if cur:
                    weigh(0)
                    weigh(1)
                if nxt:
                    normalise(0, V, 2, x1, x1, dv_x1)
                    wait(dve, dv_x1, V(2))
                    wait(dve, f_in[1 - par], dma(1))
                    v.tensor_tensor(x1[0:NODES, 0, :], x1[0:NODES, 0, :], fused_in[1 - par][:, :],
                                    ALU.add).then_inc(dv_fused, 1)
                    hold(dve, dv_fused, V(2))
                    statistics(1, V, 2, lambda c: x1[:, c, :])
                if cur:
                    weigh(2)
                    weigh(3)
                if nxt:
                    hold(dve, po_x2b, V(1))
                    normalise(1, V, 2, x2, x1, dv_x2)
                    hold(dve, po_v, V(2))
                    hold(dve, ac_pef, V(1))
                    v.reduce_sum(ef[:, :, :], tv[:, :, :, :], X).then_inc(dv_ef, 1)
                if cur:
                    even, odd = (conv.rearrange("p (i r) -> p r i", r=2)[:, r, :] for r in range(2))
                    xe, xo = (x3T[:, :].rearrange("p (i r) -> p r i", r=2)[:, r, :] for r in range(2))
                    wait(dve, pe_P1, V(1))
                    wait(dve, ac_x3T, V(1))
                    wait(dve, ac_xchi, V(0))
                    wait(dve, dv_xclo, V(0))
                    v.scalar_tensor_tensor(even, MS_BANK[:, 0:HALF], bn_bias[:, 1:2], xe, ALU.add, ALU.add)
                    v.scalar_tensor_tensor(odd, xo, bn_bias[:, 1:2], MS_BANK[:, 1:HALF + 1], ALU.add,
                                           ALU.subtract).then_inc(dv_ab, 1)
                if nxt:
                    hold(dve, ac_pef, V(2))
                    wait(dve, pe_agg1, V(2))
                    dve.nop(nofuse=True)
                    for c in range(NC):
                        last = v.tensor_scalar(x_hi[:, c, :], x2[:, c, :], pef[:, 1, c:c + 1], None, ALU.mult)
                    last.then_inc(dv_xshi, 1)
                    hold(dve, pe_den, V(1))
                    v.tensor_copy(pf2[:, :, 0], pef[:, 1, :]).then_inc(dv_pfh, 1)
                    wait(dve, dv_xshi, V(2))
                    for c in range(NC):
                        last = v.scalar_tensor_tensor(x_lo[:, c, :], x2[:, c, :], pef[:, 1, c:c + 1], f(x_hi[:, c, :]),
                                                      ALU.mult, ALU.subtract)
                    last.then_inc(dv_xslo, 1)
                    wait(dve, dv_pfh, V(2))
                    v.tensor_tensor(pf2[:, :, 1], pef[:, 1, :], f(pf2[:, :, 0]), ALU.subtract).then_inc(dv_pf, 1)
                if cur:
                    wait(dve, dv_ab, V(1))
                    wait(dve, ac_P0s, V(1))
                    v.tensor_tensor(odd, CV_BANK[:, HALF:N], odd, ALU.add).then_inc(dv_q, 1)
                    v.tensor_tensor(even, even, P0s, ALU.add)
                    wait(dve, dv_q, V(1))
                    v.tensor_tensor(odd, odd, P0s, ALU.subtract).then_inc(dv_conv, 1)
                    wait(dve, ac_xchi, V(1))
                    wait(dve, pe_gn, V(0))
                    v.scalar_tensor_tensor(xc_lo[:, :], conv, 0.0, f(xc_hi[:, :]), ALU.max,
                                           ALU.subtract).then_inc(dv_xclo, 1)
                    wait(dve, ac_nmphi, V(1))
                    v.tensor_tensor(nmp_lo[:, :], X_BANK[:, :], f(nmp_hi[:, :]), ALU.subtract).then_inc(dv_nmplo, 1)
                if nxt:
                    wait(dve, pe_dcol, V(2))
                    v.tensor_tensor(dq[:, 0, :], SQ_BANK[:, 0:NC], pef[:, 0, :], ALU.mult).then_inc(dv_q0, 1)
                    hold(dve, dv_q0, V(2))
                    v.reciprocal(dq[:, 1, :], dq[:, 0, :]).then_inc(dv_q1, 1)
                    wait(dve, dv_q1, V(2))
                    v.tensor_tensor(dq[:, 2, :], dq[:, 1, :], pef[:, 0, :], ALU.mult).then_inc(dv_dq, 1)
                    wait(dve, pe_out2, V(2))
                    wait(dve, po_x2b, V(2))
                    wait(dve, dv_dq, V(2))
                    for c in range(NC):
                        last = v.scalar_tensor_tensor(y3[:, c, :], AG_BANK[:, ch(c)], dq[:, 2, c:c + 1], y3[:, c, :],
                                                      ALU.mult, ALU.add)
                    last.then_inc(dv_y3, 1)
                    hold(dve, dv_y3, V(2))
                    statistics(2, V, 2, lambda c: y3[:, c, :])
                    hold(dve, pe_x3T, V(1))
                    normalise(2, V, 2, x3, y3, dv_x3)
                if cur:
                    wait(dve, ac_thr, V(1))
                    wait(dve, ac_gh, V(1))
                    v.scalar_tensor_tensor(gh, th_r, 1.0, gh, ALU.add, ALU.mult).then_inc(dv_t0, 1)
                    wait(dve, dv_t0, V(1))
                    wait(dve, pe_gn, V(1))
                    v.tensor_tensor(gh, SQ_BANK[:, :], gh, ALU.add).then_inc(dv_t, 1)
                    wait(dve, po_g, V(1))
                    wait(dve, ac_thz, V(1))
                    v.scalar_tensor_tensor(gd, th_z, 1.0, gd, ALU.add, ALU.mult).then_inc(dv_m, 1)
                    wait(dve, dv_m, V(1))
                    v.scalar_tensor_tensor(ga, gd, 0.5, ga, ALU.mult, ALU.add).then_inc(dv_y4, 1)

            over_graphs(dve, turn)

        @block.tensor
        def _(pe):
            t_ = nc.tensor
            def turn(V, dma, par, graph, has, outs):
                cur, nxt, prev = has(0), has(1), has(-1)

                def transpose_adjacency(mc):
                    for c in range(NC):
                        last = t_.transpose(AT_BANK[mc % 2][:, ch(c)], adj_nat[1 - par][:, c, ch(mc)], ident[:, :])
                    last.then_inc(pe_aT[mc], 1)

                def distances(mc):
                    t_.matmul(AT_BANK[mc % 2][:, :], Lf[:, ch(mc)], Rf[:, :], start=True, stop=True
                              ).then_inc(pe_D[mc], 1)

                def taps(o, first, count, hi, lo, start_col, width, done):
                    for k, blk in enumerate(range(first, first + count)):
                        w = range(start_col + k, start_col + k + width)
                        last = three(pe, o, w_hi[:, tapblk(blk), :], w_lo[:, tapblk(blk), :],
                                     hi[:, w.start:w.stop], lo[:, w.start:w.stop], k == 0, k == count - 1)
                    last.then_inc(done, 1)

                if nxt:
                    wait(pe, adj_in[1 - par], dma(1))
                    for mc in range(2):
                        wait(pe, ac_E[mc + 2], V(0))
                        transpose_adjacency(mc)
                if cur:
                    wait(pe, dv_x3, V(1))
                    wait(pe, dv_nmplo, V(0))
                    for c in range(NC):
                        last = t_.transpose(X_BANK[:, ch(c)], x3[:, c, :], ident[:, :])
                    last.then_inc(pe_x3T, 1)
                    wait(pe, ac_x3Thi, V(1))
                    wait(pe, dv_x3Tlo, V(1))
                    wait(pe, dv_t, V(0))
                    three(pe, SQ_BANK[:, :], w_hi[:, SE, :], w_lo[:, SE, :], x3T_hi[:, :], x3T_lo[:, :],
                          True, True).then_inc(pe_s, 1)
                    wait(pe, ac_thr, V(0))
                    three(pe, CV_BANK[:, :], w_hi[:, CONV1, :], w_lo[:, CONV1, :], x3T_hi[:, :], x3T_lo[:, :],
                          True, True).then_inc(pe_c1, 1)
                    wait(pe, ac_thz, V(0))
                    wait(pe, ac_x3T, V(1))
                    t_.matmul(MS_BANK[:, :], ones_r[:, :], msg_bias[:, :, :].rearrange("p c d -> p (c d)"),
                              start=True, stop=False)
                    for c in range(NC):
                        last = t_.matmul(MS_BANK[:, ch(c)], x3T[:, ch(c)], wmsgT, start=False, stop=(c == NC - 1))
                    last.then_inc(pe_msg, 1)
                    wait(pe, ac_gh, V(0))
                    three(pe, HN_BANK[:, :], w_hi[:, HH + 2, :], w_lo[:, HH + 2, :], x3T_hi[:, :], x3T_lo[:, :],
                          True, True).then_inc(pe_hn, 1)
                if nxt:
                    for mc in range(2, NC):
                        wait(pe, ac_aT[mc - 2], V(2))
                        transpose_adjacency(mc)
                if prev:
                    wait(pe, dv_y4, V(0))
                    if cur:
                        wait(pe, ac_x3T, V(1))
                    for c in range(NC):
                        last = t_.transpose(X_BANK[:, ch(c)], ga[:, ch(c)], ident[:, :])
                    last.then_inc(pe_yT, 1)
                if nxt:
                    wait(pe, ac_xhi, V(2))
                    wait(pe, dv_xlo, V(2))
                    wait(pe, dv_y3, V(1))
                    for mc in range(NC):
                        wait(pe, dv_aTlo[mc], V(2))
                        last = three(pe, AG_BANK[:, :], x_hi[:, mc, :], x_lo[:, mc, :], aT_hi[:, mc, :],
                                     aT_lo[:, mc, :], mc == 0, mc == NC - 1)
                    last.then_inc(pe_agg1, 1)
                if cur:
                    wait(pe, ac_s2, V(1))
                    t_.matmul(SQ_BANK[:, :], sq_pick[0:32, :], sC[0:32, :], start=False, stop=True,
                              skip_group_check=True).then_inc(pe_sq, 1)
                if nxt:
                    wait(pe, ac_agg1, V(2))
                    for c in range(NC):
                        last = t_.matmul(AG_BANK[:, ch(c)], agg_sb[:, ch(c)], w0[:, :], start=True, stop=True)
                    last.then_inc(pe_out0, 1)
                if cur:
                    wait(pe, dv_c1, V(1))
                    wait(pe, dv_msglo, V(1))
                    taps(MS_BANK[:, 0:P1W], EVEN, ODD, c1_hi[:, 1, :], c1_lo[:, 1, :], 0, P1W, pe_P1)
                    wait(pe, dv_R, V(1))
                    for mc in range(2):
                        if nxt:
                            wait(pe, ac_aT[mc + 2], V(2))
                        else:
                            wait(pe, ac_E[mc + 2], V(0))
                        distances(mc)
                    taps(CV_BANK[:, 0:HALF], 0, EVEN, c1_hi[:, 0, :], c1_lo[:, 0, :], 0, HALF, pe_P0)
                    for mc in range(2, NC):
                        wait(pe, ac_E[mc - 2], V(1))
                        distances(mc)
                    wait(pe, dv_csp, V(1))
                    taps(CV_BANK[:, HALF:N], EVEN + ODD, EVEN, cs_hi, cs_lo, 0, HALF, pe_Q)
                    if prev:
                        wait(pe, ac_out, V(0))
                    for mc in range(NC):
                        wait(pe, ac_Phi[mc], V(1))
                        wait(pe, po_Plo[mc], V(1))
                        last = three(pe, X_BANK[:, :], msg_hi[:, ch(mc)], msg_lo[:, ch(mc)], P_hi[:, mc, :],
                                     P_lo[:, mc, :], mc == 0, mc == NC - 1)
                    last.then_inc(pe_N, 1)
                if nxt:
                    wait(pe, dv_xslo, V(2))
                    for mc in range(NC):
                        last = three(pe, AG_BANK[:, :], x_hi[:, mc, :], x_lo[:, mc, :], aT_hi[:, mc, :],
                                     aT_lo[:, mc, :], mc == 0, mc == NC - 1)
                    last.then_inc(pe_agg2, 1)
                    wait(pe, dv_pf, V(2))
                    for mc in range(NC):
                        t_.matmul(SQ_BANK[0:2, :], pf2[:, mc, :], aT_hi[:, mc, :], start=(mc == 0), stop=False)
                        last = t_.matmul(SQ_BANK[0:2, :], pf2[:, mc, :], aT_lo[:, mc, :], start=False,
                                         stop=(mc == NC - 1))
                    last.then_inc(pe_den, 1)

                def gate(o, g, parts, done):
                    for i, (blk, hi, lo) in enumerate(parts):
                        last = three(pe, o, w_hi[:, blk, :], w_lo[:, blk, :], hi, lo, i == 0, i == len(parts) - 1)
                    last.then_inc(done, 1)

                def gate_parts(g):
                    parts = [(IH + 2 * g, xc_hi[:, :], xc_lo[:, :]), (IH + 2 * g + 1, nmp_hi[:, :], nmp_lo[:, :])]
                    return parts if g == 2 else [(HH + g, x3T_hi[:, :], x3T_lo[:, :])] + parts
                if cur:
                    wait(pe, dv_xclo, V(1))
                    wait(pe, dv_nmplo, V(1))
                    gate(MS_BANK[:, :], 1, gate_parts(1), pe_z)
                if nxt:
                    wait(pe, ac_agg2, V(2))
                    for c in range(NC):
                        last = t_.matmul(AG_BANK[:, ch(c)], agg_sb[:, ch(c)], wwT, start=True, stop=True)
                    last.then_inc(pe_out2, 1)
                    wait(pe, ac_den, V(2))
                    for c in range(NC):
                        last = t_.matmul(SQ_BANK[:, c:c + 1], den_sb[0:2, ch(c)], ones[0:2, 0:1], start=True, stop=True)
                    last.then_inc(pe_dcol, 1)
                if cur:
                    gate(CV_BANK[:, :], 0, gate_parts(0), pe_r)
                    if nxt:
                        wait(pe, dv_q0, V(2))
                    gate(SQ_BANK[:, :], 2, gate_parts(2), pe_gn)

            over_graphs(pe, turn)


def kernel(**inputs):
    import numpy as _np
    import concourse.bacc as _bacc
    from concourse import mybir as _mybir
    from concourse.bass_utils import run_bass_kernel_spmd as _run

    nc = _bacc.Bacc("TRN2", target_bir_lowering=False, num_devices=1)
    arrays, aps = {}, {}
    for name, value in inputs.items():
        value = _np.ascontiguousarray(value)
        arrays[f"in_{name}_dram"] = value
        aps[name] = nc.dram_tensor(f"in_{name}_dram", value.shape, _mybir.dt.from_np(value.dtype),
                                   kind="ExternalInput").ap()
    out = nc.dram_tensor("out_0_dram", (B, N, D), _mybir.dt.float32, kind="ExternalOutput").ap()
    network_kernel(nc, aps, out)
    r = _run(nc, [arrays], core_ids=[0])
    return r.results[0]["out_0_dram"]
```

```python
import concourse.bass as bass
from concourse import mybir
from contextlib import ExitStack

B, N, D = 16, 512, 128
NC = N // 128
HID = 256
GROUPS = [[(0, 25)], [(0, 9)], [(0, 1), (9, 15)], [(6, 9), (12, 15)], [(3, 6), (9, 12)]]
NG = len(GROUPS)
NODES = 25
SLOT = 32
GT = B // 4
TAPS = 17
PAD = TAPS // 2
EVEN, ODD = TAPS // 2 + 1, TAPS // 2
HALF = N // 2
HP = PAD // 2
PH = HALF + 2 * HP + 2
P1W = HALF + 2
EPS = 1e-5
SE, CONV1, IH, HH, TAP, SUMTAP = 0, 1, 2, 8, 11, 28
NW = SUMTAP + EVEN - 1
A1, A2, WB, G1, BB1, M1, V1, G2, BB2, M2, V2, BIH, BHH, HB = 0, 1, 2, 3, 4, 5, 6, 7, 8, 9, 10, 11, 14, 17
NROWS = HB + NG * HID // 128
NCST = 6 + 2 * NC + 4


def network_kernel(nc, a, out):
    f32 = mybir.dt.float32
    f32r = mybir.dt.float32r
    ALU = mybir.AluOpType
    ACT = mybir.ActivationFunctionType
    X = mybir.AxisListType.X

    ctx = ExitStack()
    with ctx:
        def sb(name, shape, dt=f32):
            return ctx.enter_context(nc.sbuf_tensor(name, shape, dt))

        def sem(name):
            return ctx.enter_context(nc.semaphore(name))

        def sems(name, n):
            return [sem(f"{name}{i}") for i in range(n)]

        def f(ap):
            return ap.bitcast(f32)

        fused_dram = nc.dram_tensor("fused_dram", (B, SLOT, D), f32, kind="Internal").ap()

        bank = [ctx.enter_context(nc.psum_tensor(f"bank{i}", [128, 512], f32)) for i in range(8)]
        AT_BANK = [bank[0], bank[1]]
        X_BANK = bank[2]
        CV_BANK = bank[3]
        MS_BANK = bank[4]
        AG_BANK = bank[5]
        SQ_BANK = bank[6]
        HN_BANK = bank[7]

        ident = sb("ident", [128, 128])
        ones = sb("ones", [128, 128])
        neg_half = sb("neg_half", [128, NG])
        bias0 = sb("bias0", [128, D])
        w0 = sb("w0", [128, D])
        wb_bc = sb("wb_bc", [128, D])
        v12 = sb("v12", [128, 2, D])
        c12 = sb("c12", [128, 2])
        ab_col = sb("ab_col", [128, 1])
        plainT = sb("plainT", [128, 2, 128])
        wwT, wmsgT = plainT[:, 0, :], plainT[:, 1, :]
        w_hi = sb("w_hi", [128, NW, 128], f32r)
        w_lo = sb("w_lo", [128, NW, 128], f32r)
        msg_bias_f = sb("msg_bias_f", [64, NC, D])
        msg_bias = sb("msg_bias", [64, NC, D], f32r)
        ones_r = sb("ones_r", [64, 128], f32r)
        cols = sb("cols", [128, NROWS])
        bn_scale = sb("bn_scale", [128, 2])
        bn_bias = sb("bn_bias", [128, 2])
        gate_bias = sb("gate_bias", [128, 3])
        se_bias = sb("se_bias", [128, 1])
        part_mask = sb("part_mask", [128, 2])
        sq_pick = sb("sq_pick", [128, 128])

        adj_nat = [sb(f"adj_nat{i}", [128, NC, N]) for i in range(2)]
        x_nat = [sb(f"x_nat{i}", [128, NC, D]) for i in range(2)]
        fused_in = [sb(f"fused_in{i}", [NODES, D]) for i in range(2)]
        aT_hi = sb("aT_hi", [128, NC, N], f32r)
        aT_lo = sb("aT_lo", [128, NC, N], f32r)
        x_hi = sb("x_hi", [128, NC, D], f32r)
        x_lo = sb("x_lo", [128, NC, D], f32r)
        x1 = sb("x1", [128, NC, D])
        x2 = sb("x2", [128, NC, D])
        y3 = sb("y3", [128, NC, D])
        agg_sb = sb("agg_sb", [128, N])
        ef = sb("ef", [128, 2, NC])
        pef = sb("pef", [128, 2, NC])
        pf2 = sb("pf2", [128, NC, 2], f32r)
        den_sb = sb("den_sb", [2, N])
        dq = sb("dq", [128, 3, NC])
        x3 = sb("x3", [128, NC, D])
        st = [sb(f"st{i}", [128, NC, 6]) for i in range(4)]
        mv = [sb(f"mv{i}", [128, NC, 2]) for i in range(4)]
        ve = [sb(f"ve{i}", [128, NC]) for i in range(4)]
        rs = [sb(f"rs{i}", [128, NC]) for i in range(4)]
        nmr = sb("nmr", [128, NC])
        nms = sb("nms", [128, NC])
        x3T = [sb(f"x3T{i}", [128, N]) for i in range(2)]
        x3T_hi = sb("x3T_hi", [128, N], f32r)
        x3T_lo = sb("x3T_lo", [128, N], f32r)
        c1 = sb("c1", [128, 2, PH])
        c1_hi = sb("c1_hi", [128, 2, PH], f32r)
        c1_lo = sb("c1_lo", [128, 2, PH], f32r)
        cs = sb("cs", [128, PH])
        cs_hi = sb("cs_hi", [128, PH], f32r)
        cs_lo = sb("cs_lo", [128, PH], f32r)
        msg_hi = sb("msg_hi", [128, N], f32r)
        msg_lo = sb("msg_lo", [128, N], f32r)
        sC = sb("sC", [128, N])
        sH = sb("sH", [96, N], f32r)
        Lf = sb("Lf", [96, N], f32r)
        Rf = sb("Rf", [96, N], f32r)
        xc_hi = sb("xc_hi", [128, N], f32r)
        xc_lo = sb("xc_lo", [128, N], f32r)
        nmp_hi = sb("nmp_hi", [128, N], f32r)
        nmp_lo = sb("nmp_lo", [128, N], f32r)
        P_hi = sb("P_hi", [128, NC, N], f32r)
        P_lo = sb("P_lo", [128, NC, N], f32r)
        y_out = sb("y_out", [128, NC, D])
        tv = sb("tv", [128, 2, NC, D])
        x1P = sb("x1P", [128, GT, D])

        ARENA = 10240
        arena = sb("arena", [128, ARENA])

        def carver(flat):
            used = [0]

            def carve(*shape):
                size = 1
                for s in shape:
                    size *= s
                ap = flat[:, used[0]:used[0] + size]
                used[0] += size
                if len(shape) == 2:
                    return ap.rearrange("p (a b) -> p a b", a=shape[0])
                if len(shape) == 3:
                    return ap.rearrange("p (a b c) -> p a b c", a=shape[0], b=shape[1])
                return ap
            return carve

        carve = carver(arena)
        aT = [carve(NC, N) for _ in range(2)]
        E = carve(2, N)
        P = carve(2, N)
        P0s = carve(HALF)
        conv = carve(N)
        gh, th_r, th_z, nn, gd, ga = [carve(N) for _ in range(6)]
        carve = carver(arena)
        adjP = carve(GT, N)
        nadjT = carve(GT, NG, 128)
        U = carve(NG, GT, 128)
        hw1 = carve(NG, HID)
        hw2 = carve(NG, 2, D)
        carve = carver(arena[:, GT * N:])
        nat_ww = carve(2, 128)
        nat_se = carve(128)
        nat_c1 = carve(128)
        nat_ih = carve(3, 2, 128)
        nat_hh = carve(3, 128)
        nat_c2 = carve(D, TAPS)
        nat_sum = carve(D, ODD)
        abc = carve(2, 128)
        carve = carver(adj_nat[0][:, :, :].rearrange("p c n -> p (c n)"))
        CM = carve(NG, 128)
        GM = carve(NG, 128)
        A5 = carve(NG, 128)
        A0 = carve(128)
        carve = carver(adj_nat[1][:, :, :].rearrange("p c n -> p (c n)"))
        hT = carve(2, N)
        S2 = carve(N)
        R2 = carve(N)
        xr = [x1, x2, y3, x3]
        xP = y_out
        aPT = [agg_sb[:, :], x3T[0][:, :]]
        TTs = sC
        fusedP = x3
        mb_rest = tv[0:64, 0]
        vrows = sb("vrows", [32, 128])
        fw = sb("fw", [128, 4, NG])
        fmx = sb("fmx", [128, 3])
        rm = sb("rm", [128, NG])
        wm = sb("wm", [128, NG])
        mk = sb("mk", [128, 2, 128])
        deg = sb("deg", [128, 4, NG])
        hb2 = sb("hb2", [1, NG, D])
        b2row = sb("b2row", [1, N])
        stP = sb("stP", [128, 6])
        mvP = sb("mvP", [128, 2])
        veP = sb("veP", [128, 1])
        rsP = sb("rsP", [128, 1])

        def wait(eng, s, count):
            if not (isinstance(count, int) and count <= 0):
                eng.wait_ge(s, count)

        def hold(eng, s, count):
            if not (isinstance(count, int) and count <= 0):
                eng.wait_ge(s, count)
                eng.nop(nofuse=True)

        def over_graphs(eng, step, start=-2):
            end = B - 3
            def fixed(b):
                step(lambda k: b + k, lambda k: 16 * ((b + k) // 2 + 1), b % 2, lambda k: b + k,
                     lambda k: 0 <= b + k < B, 16 * b)
            for b in range(start, 1):
                fixed(b)
            with eng.Fori(1, end, 2) as b:
                v = [eng.snap(b + k) for k in range(0, 5)]
                d = [eng.snap(b * 8 + k) for k in (8, 24, 40)]
                o = [eng.snap(b * 16 + k) for k in (0, 16)]
                for h in range(2):
                    step(lambda k, h=h: v[h + k], lambda k, h=h: d[(h + k + 1) // 2], (1 + h) % 2,
                         lambda k, h=h: b + (h + k), lambda k: True, o[h])
            for b in range(end, B + 1):
                fixed(b)

        def three(pe, o, lh, ll, rh, rl, start, stop):
            nc.tensor.matmul(o, lh, rh, start=start, stop=False)
            nc.tensor.matmul(o, lh, rl, start=False, stop=False)
            return nc.tensor.matmul(o, ll, rh, start=False, stop=stop)

        def ch(c):
            return slice(c * 128, (c + 1) * 128)

        def bc(ap, n):
            return ap.unsqueeze(1).to_broadcast([128, n, ap.shape[-1]])

        def spread(ap, n):
            return ap.unsqueeze(2).to_broadcast([128, ap.shape[-1], n])

        x_v = a["x"].rearrange("b (c p) d -> b p c d", p=128)
        adj_v = a["adj"].rearrange("b (c p) m -> b p c m", p=128)
        out_v = out.rearrange("b (c p) d -> b p c d", p=128)
        four = "(t j) n d -> j n t d"

        x_in, adj_in, f_in = sems("x_in", 2), sems("adj_in", 2), sems("f_in", 2)

        before = [nc.alloc_semaphore(name=f"before{i}") for i in range(71)]
        (q_zero, q_ident, q_mask, q_row, q_cols, q_colsb, q_wt, q_cst, q_adjP, q_xP, q_h, q_bnv, q_bnr, q_bns,
         q_sc, q_sum, q_abc, q_mt, q_gm, q_v, q_vsb, q_c12, q_wps, q_whi, q_wlo, q_fm, q_fs, q_fe, q_fd, q_fr,
         q_wm, q_aP, q_aPT, q_TT, q_TTs, q_o, q_xPb, q_yP, q_stP, q_mvP, q_veP, q_rsP, q_x1P, q_A0, q_A1, q_A5,
         q_dg, q_dg1, q_dg2, q_dgp, q_dgz, q_dgi, q_B, q_BT, q_nT, q_U, q_Us, q_h2, q_hT, q_S2, q_S2s, q_o2, q_R2,
         q_fu, q_fout, q_mb, q_gb) = before[:67]
        q_xr = before[67:]

        blocks = ([nat_ww[:, 0, :], nat_ww[:, 1, :]], [nat_se, nat_c1[:, :]]
                  + [nat_ih[:, g, h, :] for g in range(3) for h in range(2)] + [nat_hh[:, g, :] for g in range(3)]
                  + [nat_c2[:, :, k] for k in range(TAPS)] + [nat_sum[:, :, k] for k in range(ODD)])
        WG = NW // 4

        def tapblk(i):
            if i < EVEN:
                return TAP + 2 * i
            if i < TAPS:
                return TAP + 2 * (i - EVEN) + 1
            return TAP if i == TAPS else SUMTAP + i - TAPS - 1

        with nc.Block() as block:
            @block.sync
            def _(sp):
                sp.dma_start(nat_ww[:, 0, :], a["L2_gnn_W_w"]).then_inc(q_wt, 16)
                sp.dma_start(nat_ww[:, 1, :], a["L3_gnn_w_msg"]).then_inc(q_wt, 16)
                sp.dma_start(nat_c1, a["L3_gnn_conv1_w"].rearrange("o i k -> o (i k)")).then_inc(q_wt, 16)
                sp.dma_start(nat_ih, a["L3_gnn_w_ih"].rearrange("(g o) (h k) -> o g h k", g=3, h=2)).then_inc(q_wt, 16)
                sp.dma_start(nat_hh, a["L3_gnn_w_hh"].rearrange("(g o) k -> o g k", g=3)).then_inc(q_wt, 16)
                sp.dma_start(nat_c2, a["L3_gnn_conv2_w"]).then_inc(q_wt, 16)
                for j in range(4):
                    if j == 0:
                        sp.wait_ge(q_zero, 1)
                    sp.dma_start(nat_se[3 * j:3 * j + 3, :], a["L3_gnn_w_se"]).then_inc(q_wt, 16)
                for j in range(4):
                    sp.dma_start(adjP[SLOT * j:SLOT * (j + 1), :, :],
                                 a["adj"].rearrange("(t j) n m -> j n t m", j=4)[j, 0:SLOT]).then_inc(q_adjP, 16)
                    sp.dma_start(xP[SLOT * j:SLOT * (j + 1), :, :],
                                 a["x"].rearrange(four, j=4)[j, 0:SLOT]).then_inc(q_xP, 16)
                for t in range(GT):
                    for j in range(4):
                        if t > 0:
                            sp.wait_ge(q_TT, t)
                        sp.dma_start(xr[j][:, :, :], x_v[4 * t + j]).then_inc(q_xr[j], 16)
                    if t == 0:
                        sp.dma_start(hw1, a["L1_gnn_W1"].rearrange("g i h -> i g h")).then_inc(q_h, 16)
                        sp.dma_start(hw2, a["L1_gnn_W2"].rearrange("g (h p) o -> p g h o", h=2)).then_inc(q_h, 16)
                sp.dma_start(x_nat[0][:, :, :], x_v[0]).then_inc(x_in[0], 16)
                sp.wait_ge(q_nT, GT)
                sp.dma_start(adj_nat[0][:, :, :], adj_v[0]).then_inc(adj_in[0], 16)
                sp.wait_ge(q_fu, NG)
                for j in range(4):
                    sp.dma_start(fused_dram.rearrange(four, j=4)[j],
                                 fusedP[SLOT * j:SLOT * (j + 1), :, :]).then_inc(q_fout, 16)
                sp.wait_ge(q_fout, 16 * 4)
                sp.dma_start(fused_in[0][:, :], fused_dram[0, 0:NODES]).then_inc(f_in[0], 16)

            @block.gpsimd
            def _(pool):
                g = nc.gpsimd
                g.memset(ident[:, :], 0.0)
                g.memset(nat_se, 0.0)
                g.memset(se_bias[:, :], 0.0)
                g.memset(msg_bias_f[:, :, :], 0.0).then_inc(q_zero, 1)
                for tile_, value in ((ones[:, :], 1.0), (neg_half[:, :], -0.5), (f(ones_r[:, :]), 1.0), (c1[:, :, :], 0.0),
                                     (sq_pick[:, :], 0.0),
                                     (mk[:, :, :], 0.0), (CM, 0.0)):
                    g.memset(tile_, value)
                g.memset(A0, 0.0).then_inc(q_zero, 1)
                pool.wait_ge(q_zero, 2)
                g.affine_select(out=ident[:, :], in_=ident[:, :], compare_op=ALU.not_equal, fill=1.0, base=0,
                                pattern=[[-1, 128]], channel_multiplier=1).then_inc(q_ident, 1)
                pool.wait_ge(q_colsb, 1)
                pool.nop(nofuse=True)
                g.tensor_scalar(bn_bias[:, :], cols[:, V1:V2 + 1:V2 - V1], EPS, None, ALU.add).then_inc(q_bnv, 1)
                pool.wait_ge(q_bnv, 1)
                g.tensor_tensor(bn_scale[:, :], bn_bias[:, :], neg_half[:, 0:2], ALU.pow).then_inc(q_bnr, 1)
                pool.wait_ge(q_xP, 16 * 4)
                pool.wait_ge(q_cst, 16 * NCST)
                g.tensor_tensor(xP[:, :, :], xP[:, :, :], bc(bias0[:, :], GT), ALU.add).then_inc(q_xPb, 1)
                for t in range(GT):
                    pool.wait_ge(q_dg2, t + 1)
                    g.tensor_tensor(deg[:, 2, :], deg[:, 0, :], neg_half[:, :], ALU.pow).then_inc(q_dgp, 1)
                    pool.wait_ge(q_mvP, t + 1)
                    g.tensor_scalar(veP[:, :], mvP[:, 1:2], EPS, None, ALU.add).then_inc(q_veP, 1)
                    pool.wait_ge(q_veP, t + 1)
                    g.tensor_tensor(rsP[:, :], veP[:, :], neg_half[:, 0:1], ALU.pow).then_inc(q_rsP, 1)

            @block.scalar
            def _(act):
                s = nc.scalar

                def copy_U(t):
                    act.wait_ge(q_U, t + 1)
                    s.activation(U[:, 0:4, t, :], bank[2 + t % 2][:, :].rearrange("p (a b) -> p a b", a=4), ACT.Identity)
                    s.activation(U[:, 4, t, :], bank[4 + t % 2][:, 128:256], ACT.Identity).then_inc(q_Us, 1)

                for row, name, n in ((A1, "L2_gnn_a_w", 2), (WB, "L2_gnn_W_b", 1), (G1, "L3_gnn_bn1_g", 1),
                                     (BB1, "L3_gnn_bn1_b", 1), (M1, "L3_gnn_bn1_m", 1), (V1, "L3_gnn_bn1_v", 1),
                                     (G2, "L3_gnn_bn2_g", 1), (BB2, "L3_gnn_bn2_b", 1), (M2, "L3_gnn_bn2_m", 1),
                                     (V2, "L3_gnn_bn2_v", 1), (BIH, "L3_gnn_b_ih", 3), (BHH, "L3_gnn_b_hh", 3)):
                    act.dma_start(vrows[row:row + n, :], a[name].rearrange("(n d) -> n d", n=n)).then_inc(q_row, 16)
                act.dma_start(vrows[HB:NROWS, :], a["L1_gnn_b1"].rearrange("g (h d) -> (g h) d", h=2)).then_inc(q_row, 16)
                for dst, src in ((w0[:, :], a["L0_gnn_weight"]),
                                 (bias0[:, :], a["L0_gnn_bias"].partition_broadcast(128)),
                                 (wb_bc[:, :], a["L2_gnn_W_b"].partition_broadcast(128)),
                                 (ab_col[:, :], a["L2_gnn_a_b"].partition_broadcast(128)),
                                 (fw[:, 0, :], a["L1_gnn_fusion_w"].partition_broadcast(128)),
                                 (hb2[:, :, :], a["L1_gnn_b2"].rearrange("g o -> (g o)").unsqueeze(0))):
                    act.dma_start(dst, src).then_inc(q_cst, 16)
                act.wait_ge(q_zero, 1)
                for row in (0, 32):
                    for c in range(NC):
                        act.dma_start(msg_bias_f[row:row + 1, c, :], a["L3_gnn_b_msg"].unsqueeze(0)).then_inc(q_cst, 16)
                for j in range(4):
                    act.dma_start(se_bias[3 * j:3 * j + 3, :], a["L3_gnn_b_se"].unsqueeze(1)).then_inc(q_cst, 16)

                act.wait_ge(q_cols, 1)
                s.activation(cols[:, :], bank[7][:, 0:NROWS], ACT.Identity).then_inc(q_colsb, 1)
                act.wait_ge(q_wps, 1)
                s.activation(plainT[:, :, :], bank[0][:, 0:256].rearrange("p (a b) -> p a b", a=2),
                             ACT.Identity).then_inc(q_whi, 1)
                act.wait_ge(q_v, 1)
                s.activation(v12[:, :, :], bank[7][:, 128:384].rearrange("p (a b) -> p a b", a=2),
                             ACT.Identity).then_inc(q_vsb, 1)
                act.wait_ge(q_cst, 16 * NCST)
                s.activation(msg_bias[:, :, :], msg_bias_f[:, :, :], ACT.Identity).then_inc(q_mb, 1)
                for k in range(WG):
                    act.wait_ge(q_wps, k + 2)
                    s.activation(w_hi[:, 4 * k:4 * k + 4, :], bank[(k + 1) % 5][:, :].rearrange("p (a b) -> p a b", a=4),
                                 ACT.Identity).then_inc(q_whi, 1)
                act.wait_ge(q_fs, 1)
                s.activation(fw[:, 2, :], fw[:, 1, :], ACT.Exp).then_inc(q_fe, 1)
                for t in range(GT):
                    act.wait_ge(q_aP, t + 1)
                    if t > 1:
                        act.wait_ge(q_TT, t - 1)
                    s.activation(aPT[t % 2], bank[t % 2][:, :], ACT.Identity).then_inc(q_aPT, 1)
                    act.wait_ge(q_TT, t + 1)
                    s.activation(TTs[:, ch(t)], bank[2 + t % 2][:, 0:128], ACT.Identity).then_inc(q_TTs, 1)
                    if t > 0:
                        copy_U(t - 1)
                copy_U(GT - 1)
                for gi in range(NG):
                    for h in range(2):
                        act.wait_ge(q_h2, 2 * gi + h + 1)
                        if gi > 0:
                            act.wait_ge(q_S2, gi)
                        s.activation(hT[:, h, :], bank[h][:, :], ACT.Relu,
                                     bias=cols[:, HB + 2 * gi + h:HB + 2 * gi + h + 1]).then_inc(q_hT, 1)
                    act.wait_ge(q_S2, gi + 1)
                    if gi > 0:
                        act.wait_ge(q_o2, gi)
                    s.activation(S2, bank[2][:, :], ACT.Identity).then_inc(q_S2s, 1)
                    act.wait_ge(q_o2, gi + 1)
                    act.wait_ge(q_wm, 1)
                    if gi > 0:
                        act.wait_ge(q_fu, gi)
                    s.activation(R2, bank[3][:, :], ACT.Relu, scale=wm[:, gi:gi + 1]).then_inc(q_R2, 1)

            @block.vector
            def _(dve):
                v = nc.vector
                v.memset(f(Lf[64:96, :]), 1.0)
                v.memset(f(Rf[32:64, :]), 1.0)
                dve.wait_ge(q_zero, 2)
                for lo, hi in ((6, 12), (33, 34)):
                    v.memset(mk[:, 0, lo:hi], -1.0)
                for lo, hi in ((3, 6), (9, 12), (65, 66)):
                    v.memset(mk[:, 1, lo:hi], -1.0)
                for lo in (32, 64):
                    v.memset(sq_pick[0:3, lo:lo + 2], -0.5)
                for gi, spans in enumerate(GROUPS):
                    for j in range(4):
                        for lo, hi in spans:
                            last = v.memset(CM[SLOT * j:SLOT * (j + 1), gi, SLOT * j + lo:SLOT * j + hi], 1.0)
                last.then_inc(q_mask, 1)
                dve.wait_ge(q_cst, 16 * NCST)
                v.reduce_max(fmx[:, 0:1], fw[:, 0, :], X).then_inc(q_fm, 1)
                dve.wait_ge(q_fm, 1)
                v.tensor_scalar(fw[:, 1, :], fw[:, 0, :], fmx[:, 0:1], None, ALU.subtract).then_inc(q_fs, 1)
                dve.wait_ge(q_bnr, 1)
                v.tensor_tensor(bn_scale[:, :], bn_scale[:, :], cols[:, G1:G2 + 1:G2 - G1], ALU.mult).then_inc(q_bns, 1)
                dve.wait_ge(q_bns, 1)
                v.tensor_tensor(bn_bias[:, :], cols[:, M1:M2 + 1:M2 - M1], bn_scale[:, :], ALU.mult).then_inc(q_bns, 1)
                dve.wait_ge(q_bns, 2)
                v.tensor_tensor(bn_bias[:, :], cols[:, BB1:BB2 + 1:BB2 - BB1], bn_bias[:, :], ALU.subtract)
                dve.wait_ge(q_wt, 16 * 10)
                v.tensor_scalar(nat_c1, nat_c1, bn_scale[:, 0:1], None, ALU.mult)
                v.tensor_scalar(nat_c2, nat_c2, bn_scale[:, 1:2], None, ALU.mult).then_inc(q_sc, 1)
                dve.wait_ge(q_sc, 1)
                v.tensor_tensor(nat_sum, nat_c2[:, :, 2:TAPS:2], nat_c2[:, :, 1:TAPS:2], ALU.add).then_inc(q_sum, 1)
                for j in range(2):
                    last = v.tensor_scalar(abc[:, j, :], ones[:, :], cols[:, A1 + j:A1 + j + 1], None, ALU.mult)
                last.then_inc(q_abc, 1)
                v.tensor_tensor(gate_bias[:, 0:2], cols[:, BIH:BIH + 2], cols[:, BHH:BHH + 2], ALU.add).then_inc(q_gb, 1)
                dve.wait_ge(q_gb, 1)
                v.tensor_scalar(gate_bias[:, 0:2], gate_bias[:, 0:2], 0.5, None, ALU.mult)
                v.tensor_scalar(gate_bias[:, 2:3], cols[:, BHH + 2:BHH + 3], 0.5, None, ALU.mult)
                dve.wait_ge(q_mt, 1)
                v.tensor_tensor(GM[:, 0:4, :], bank[5][:, :].rearrange("p (a b) -> p a b", a=4), CM[:, 0:4, :], ALU.mult)
                v.tensor_tensor(GM[:, 4, :], bank[6][:, 0:128], CM[:, 4, :], ALU.mult)
                v.reduce_max(rm[:, 0:4], bank[5][:, :].rearrange("p (a b) -> p a b", a=4), X)
                v.reduce_max(rm[:, 4:5], bank[6][:, 0:128], X)
                v.tensor_copy(part_mask[:, :], bank[6][:, 128:384:128]).then_inc(q_gm, 1)
                dve.wait_ge(q_vsb, 1)
                v.tensor_copy(c12[:, :], bank[7][:, 384:386]).then_inc(q_c12, 1)
                dve.wait_ge(q_c12, 1)
                v.tensor_tensor(c12[:, 0:1], c12[:, 0:1], ab_col[:, :], ALU.add)
                dve.wait_ge(q_mb, 1)
                v.tensor_tensor(mb_rest[:, :, :], msg_bias_f[:, :, :], f(msg_bias[:, :, :]), ALU.subtract).then_inc(q_mb, 1)
                dve.wait_ge(q_mb, 2)
                v.tensor_copy(msg_bias[32:64, :, :], mb_rest[32:64, :, :]).then_inc(q_mb, 1)
                for k in range(WG):
                    dve.wait_ge(q_whi, k + 2)
                    v.tensor_tensor(w_lo[:, 4 * k:4 * k + 4, :], bank[(k + 1) % 5][:, :].rearrange("p (a b) -> p a b", a=4),
                                    f(w_hi[:, 4 * k:4 * k + 4, :]), ALU.subtract).then_inc(q_wlo, 1)
                dve.wait_ge(q_fe, 1)
                v.reduce_sum(fmx[:, 1:2], fw[:, 2, :], X).then_inc(q_fd, 1)
                dve.wait_ge(q_fd, 1)
                v.reciprocal(fmx[:, 2:3], fmx[:, 1:2]).then_inc(q_fr, 1)
                dve.wait_ge(q_fr, 1)
                dve.wait_ge(q_gm, 1)
                v.scalar_tensor_tensor(wm[:, :], fw[:, 2, :], fmx[:, 2:3], rm[:, :], ALU.mult, ALU.mult).then_inc(q_wm, 1)
                dve.wait_ge(q_adjP, 16 * 4)
                dve.wait_ge(q_zero, 2)
                dve.wait_ge(q_ident, 1)
                for t in range(GT):
                    if t > 0:
                        dve.wait_ge(q_A5, t)
                    for j in range(4):
                        last = v.tensor_copy(A0[SLOT * j:SLOT * (j + 1), SLOT * j:SLOT * (j + 1)],
                                             adjP[SLOT * j:SLOT * (j + 1), t, 0:SLOT])
                    last.then_inc(q_A0, 1)
                    dve.wait_ge(q_A0, t + 1)
                    v.tensor_tensor(A0, A0, ident[:, :], ALU.add).then_inc(q_A1, 1)
                    dve.wait_ge(q_A1, t + 1)
                    if t > 0:
                        dve.wait_ge(q_BT, t)
                    v.tensor_tensor(A5, bc(A0, NG), GM, ALU.mult).then_inc(q_A5, 1)
                    dve.wait_ge(q_A5, t + 1)
                    v.reduce_sum(deg[:, 3, :], A5, X).then_inc(q_dg, 1)
                    dve.wait_ge(q_dg, t + 1)
                    v.tensor_scalar(deg[:, 1, :], deg[:, 3, :], 0.0, None, ALU.is_equal).then_inc(q_dg1, 1)
                    dve.wait_ge(q_dg1, t + 1)
                    v.tensor_tensor(deg[:, 0, :], deg[:, 3, :], deg[:, 1, :], ALU.add).then_inc(q_dg2, 1)
                    v.tensor_scalar(deg[:, 1, :], deg[:, 1, :], -1.0, 1.0, ALU.mult, ALU.add).then_inc(q_dgz, 1)
                    dve.wait_ge(q_dgz, t + 1)
                    dve.wait_ge(q_dgp, t + 1)
                    v.tensor_tensor(deg[:, 3, :], deg[:, 2, :], deg[:, 1, :], ALU.mult).then_inc(q_dgi, 1)
                    dve.wait_ge(q_dgi, t + 1)
                    v.tensor_tensor(A5, A5, spread(deg[:, 3, :], 128), ALU.mult).then_inc(q_B, 1)
                    dve.wait_ge(q_o, t + 1)
                    dve.wait_ge(q_xPb, 1)
                    v.tensor_tensor(x1P[:, t, :], bank[4 + t % 2][:, 0:128], xP[:, t, :], ALU.add).then_inc(q_yP, 1)
                    dve.wait_ge(q_yP, t + 1)
                    v.bn_stats(stP[:, :], x1P[:, t, :]).then_inc(q_stP, 1)
                    dve.wait_ge(q_stP, t + 1)
                    v.bn_aggr(mvP[:, :], stP[:, :]).then_inc(q_mvP, 1)
                    dve.wait_ge(q_BT, t + 1)
                    v.tensor_tensor(nadjT[:, t, 0:4, :], bank[6][:, :].rearrange("p (a b) -> p a b", a=4),
                                    spread(deg[:, 3, 0:4], 128), ALU.mult)
                    v.tensor_scalar(nadjT[:, t, 4, :], bank[7][:, 0:128], deg[:, 3, 4:5], None, ALU.mult).then_inc(q_nT, 1)
                    dve.wait_ge(q_rsP, t + 1)
                    v.tensor_scalar(x1P[:, t, :], x1P[:, t, :], mvP[:, 0:1], rsP[:, :], ALU.subtract,
                                    ALU.mult).then_inc(q_x1P, 1)
                fusedF = fusedP[:, :, :].rearrange("p t d -> p (t d)")
                for gi in range(NG):
                    dve.wait_ge(q_R2, gi + 1)
                    if gi == 0:
                        v.tensor_copy(fusedF, R2).then_inc(q_fu, 1)
                    else:
                        dve.wait_ge(q_fu, gi)
                        v.tensor_tensor(fusedF, fusedF, R2, ALU.add).then_inc(q_fu, 1)

            @block.tensor
            def _(pe):
                t_ = nc.tensor
                pe.wait_ge(q_ident, 1)
                pe.wait_ge(q_row, 16 * 13)
                t_.transpose(bank[7][:, 0:NROWS], vrows[0:NROWS, :], ident[0:NROWS, 0:NROWS]).then_inc(q_cols, 1)
                pe.wait_ge(q_mask, 1)
                for gi in range(NG):
                    t_.transpose(bank[5 + gi // 4][:, ch(gi % 4)], CM[:, gi, :], ident[:, :])
                t_.transpose(bank[6][:, ch(1)], mk[:, 0, :], ident[:, :])
                t_.transpose(bank[6][:, ch(2)], mk[:, 1, :], ident[:, :]).then_inc(q_mt, 1)
                pe.wait_ge(q_wt, 16 * 10)
                for i, w in enumerate(blocks[0]):
                    last = t_.transpose(bank[0][:, ch(i)], w, ident[:, :])
                last.then_inc(q_wps, 1)
                pe.wait_ge(q_abc, 1)
                pe.wait_ge(q_colsb, 1)
                for j in range(2):
                    t_.matmul(bank[7][:, ch(1 + j)], abc[:, j, :], nat_ww[:, 0, :], start=True, stop=True)
                    last = t_.matmul(bank[7][:, 384 + j:385 + j], abc[:, j, :], cols[:, WB:WB + 1], start=True, stop=True)
                last.then_inc(q_v, 1)
                pe.wait_ge(q_sum, 1)
                for k in range(WG):
                    if k >= 4:
                        pe.wait_ge(q_whi, k - 3)
                        if k >= 5:
                            pe.wait_ge(q_wlo, k - 4)
                    for i in range(4):
                        last = t_.transpose(bank[(k + 1) % 5][:, ch(i)], blocks[1][4 * k + i], ident[:, :])
                    last.then_inc(q_wps, 1)
                pe.wait_ge(q_adjP, 16 * 4)
                pe.wait_ge(q_whi, WG + 1)
                pe.wait_ge(q_wlo, WG)
                pe.wait_ge(q_gm, 1)
                pe.wait_ge(q_c12, 1)
                pe.wait_ge(q_vsb, 1)
                pe.wait_ge(q_cst, 16 * NCST)

                def transpose_rows(t):
                    for mc in range(NC):
                        last = t_.transpose(bank[t % 2][:, ch(mc)], adjP[:, t, ch(mc)], ident[:, :])
                    last.then_inc(q_aP, 1)
                transpose_rows(0)
                for t in range(GT):
                    pe.wait_ge(q_aPT, t + 1)
                    if t > 1:
                        pe.wait_ge(q_Us, t - 1)
                    for j in range(4):
                        pe.wait_ge(q_xr[j], 16 * (t + 1))
                        for mc in range(NC):
                            last = t_.matmul(bank[2 + t % 2][:, SLOT * j:SLOT * (j + 1)], xr[j][:, mc, :],
                                             aPT[t % 2][:, 128 * mc + SLOT * j:128 * mc + SLOT * (j + 1)],
                                             start=(mc == 0), stop=(mc == NC - 1))
                    last.then_inc(q_TT, 1)
                    if t + 1 < GT:
                        transpose_rows(t + 1)
                    pe.wait_ge(q_B, t + 1)
                    if t > 0:
                        pe.wait_ge(q_nT, t)
                    for gi in range(NG):
                        last = t_.transpose(bank[6 + gi // 4][:, ch(gi % 4)], A5[:, gi, :], ident[:, :])
                    last.then_inc(q_BT, 1)
                    pe.wait_ge(q_TTs, t + 1)
                    t_.matmul(bank[4 + t % 2][:, 0:128], TTs[:, ch(t)], w0[:, :], start=True, stop=True).then_inc(q_o, 1)
                    pe.wait_ge(q_x1P, t + 1)
                    pe.wait_ge(q_nT, t + 1)
                    for gi in range(NG):
                        o = bank[2 + t % 2][:, ch(gi)] if gi < 4 else bank[4 + t % 2][:, 128:256]
                        last = t_.matmul(o, x1P[:, t, :], nadjT[:, t, gi, :], start=True, stop=True)
                    last.then_inc(q_U, 1)
                pe.wait_ge(q_h, 16 * 2)
                pe.wait_ge(q_Us, GT)

                def hidden(gi):
                    for h in range(2):
                        if gi > 0:
                            pe.wait_ge(q_hT, 2 * gi - 1 + h)
                        t_.matmul(bank[h][:, :], hw1[:, gi, ch(h)], U[:, gi, :, :].rearrange("p t n -> p (t n)"),
                                  start=True, stop=True).then_inc(q_h2, 1)
                hidden(0)
                for gi in range(NG):
                    pe.wait_ge(q_hT, 2 * gi + 2)
                    if gi > 0:
                        pe.wait_ge(q_S2s, gi)
                    for t in range(GT):
                        for h in range(2):
                            last = t_.matmul(bank[2][:, ch(t)], hT[:, h, ch(t)], hw2[:, gi, h, :],
                                             start=(h == 0), stop=(h == 1))
                    last.then_inc(q_S2, 1)
                    if gi + 1 < NG:
                        hidden(gi + 1)
                    pe.wait_ge(q_S2s, gi + 1)
                    if gi > 0:
                        pe.wait_ge(q_R2, gi)
                    for t in range(GT):
                        t_.matmul(bank[3][:, ch(t)], ones[0:1, :], hb2[0:1, gi, :], start=True, stop=False)
                        last = t_.matmul(bank[3][:, ch(t)], nadjT[:, t, gi, :], S2[:, ch(t)], start=False, stop=True)
                    last.then_inc(q_o2, 1)
                pe.wait_ge(q_mb, 3)
                pe.wait_ge(q_R2, NG)

        nc.clear_and_free_semaphores(before)
        nc.all_engine_barrier()

        pe_aT, ac_aThi, ac_aT, aTlo = sems("pe_aT", NC), sems("ac_aThi", NC), sems("ac_aT", NC), sems("aTlo", NC)
        ac_xhi, dv_xlo, po_xb = sem("ac_xhi"), sem("dv_xlo"), sem("po_xb")
        pe_agg1, ac_agg1, pe_out0, dv_y1 = sem("pe_agg1"), sem("ac_agg1"), sem("pe_out0"), sem("dv_y1")
        dv_st, dv_mv, po_ve, po_rs = sems("dv_st", 4), sems("dv_mv", 4), sems("po_ve", 4), sems("po_rs", 4)
        dv_x1, dv_fused, dv_x2, po_x2b, po_v = sem("dv_x1"), sem("dv_fused"), sem("dv_x2"), sem("po_x2b"), sem("po_v")
        dv_f, dv_e, ac_pf, ac_pe, dv_xshi, dv_xslo, dv_pf = sem("dv_f"), sem("dv_e"), sem("ac_pf"), sem("ac_pe"), sem("dv_xshi"), sem("dv_xslo"), sem("dv_pf")
        pe_agg2, pe_den, ac_agg2, ac_den = sem("pe_agg2"), sem("pe_den"), sem("ac_agg2"), sem("ac_den")
        pe_dcol, pe_out2, dv_dq, dv_y3, dv_x3 = sem("pe_dcol"), sem("pe_out2"), sem("dv_dq"), sem("dv_y3"), sem("dv_x3")
        pe_x3T, ac_x3Thi, ac_x3T, dv_x3Tlo = sem("pe_x3T"), sem("ac_x3Thi"), sem("ac_x3T"), sem("dv_x3Tlo")
        pe_s, pe_c1, pe_hn, pe_msg, pe_sq = sem("pe_s"), sem("pe_c1"), sem("pe_hn"), sem("pe_msg"), sem("pe_sq")
        ac_s2, ac_c1, ac_gh, ac_msghi, ac_C, ac_H = [sem(n) for n in ("ac_s2", "ac_c1", "ac_gh", "ac_msghi", "ac_C", "ac_H")]
        dv_c1, po_cs, dv_csp, dv_msglo, po_L, dv_R = [sem(n) for n in ("dv_c1", "po_cs", "dv_csp", "dv_msglo", "po_L", "dv_R")]
        pe_D, ac_E, dv_P, ac_Phi, po_Plo = sems("pe_D", NC), sems("ac_E", NC), sems("dv_P", NC), sems("ac_Phi", NC), sems("po_Plo", NC)
        pe_P1, pe_P0, pe_Q, ac_P0s, dv_ab, dv_conv = [sem(n) for n in ("pe_P1", "pe_P0", "pe_Q", "ac_P0s", "dv_ab", "dv_conv")]
        ac_xchi, dv_xclo, pe_N, ac_nmphi, dv_nmplo = [sem(n) for n in ("ac_xchi", "dv_xclo", "pe_N", "ac_nmphi", "dv_nmplo")]
        pe_z, pe_r, pe_gn, ac_thz, ac_thr, ac_nn = [sem(n) for n in ("pe_z", "pe_r", "pe_gn", "ac_thz", "ac_thr", "ac_nn")]
        dv_t, po_g, po_y4, pe_yT = [sem(n) for n in ("dv_t", "po_g", "po_y4", "pe_yT")]
        po_nms, dv_c1h, ac_csh, dv_q0, dv_q1, dv_q, dv_pfh, dv_t0, dv_m, dv_d, dv_v = [sem(n) for n in (
            "po_nms", "dv_c1h", "ac_csh", "dv_q0", "dv_q1", "dv_q", "dv_pfh", "dv_t0", "dv_m", "dv_d", "dv_v")]
        ac_L, ac_half = sem("ac_L"), sem("ac_half")
        po_nm, ac_out, o_out = sem("po_nm"), sem("ac_out"), sem("o_out")

        block = ctx.enter_context(nc.Block())

        @block.sync
        def _(sp):
            sp.sem_inc(o_out, 16)
            def turn(V, dma, par, graph, has, outs):
                if has(2):
                    wait(sp, ac_xhi, V(1))
                    wait(sp, dv_xlo, V(1))
                    wait(sp, po_xb, V(1))
                    sp.dma_start(x_nat[par][:, :, :], x_v[bass.ds(graph(2), 1)].rearrange("a p c d -> p (a c) d")
                                 ).then_inc(x_in[par], 16)
                    wait(sp, pe_aT[NC - 1], V(1))
                    sp.dma_start(adj_nat[par][:, :, :], adj_v[bass.ds(graph(2), 1)].rearrange("a p c m -> p (a c) m")
                                 ).then_inc(adj_in[par], 16)
                    wait(sp, dv_fused, V(1))
                    sp.dma_start(fused_in[par][:, :],
                                 fused_dram[bass.ds(graph(2), 1), 0:NODES].rearrange("a p d -> p (a d)")
                                 ).then_inc(f_in[par], 16)
                if has(-1):
                    sp.wait_ge(ac_out, V(0))
                    sp.dma_start(out_v[bass.ds(graph(-1), 1)].rearrange("a p c d -> p (a c) d"),
                                 y_out[:, :, :]).then_inc(o_out, 16)

            over_graphs(sp, turn, -1)
            sp.wait_ge(o_out, 16 * (B + 1))

        @block.gpsimd
        def _(pool):
            g = nc.gpsimd
            def inverse_root(V, k, i, chunks=NC):
                hold(pool, dv_mv[i], V(k))
                g.tensor_scalar(ve[i][:, :], mv[i][:, :, 1], EPS, None, ALU.add).then_inc(po_ve[i], 1)
                wait(pool, po_ve[i], V(k))
                g.tensor_tensor(rs[i][:, :], ve[i][:, :], neg_half[:, 0:NC], ALU.pow).then_inc(po_rs[i], 1)

            def turn(V, dma, par, graph, has, outs):
                cur, nxt, prev, new = has(0), has(1), has(-1), has(2)

                def split_rest(mc):
                    wait(pool, ac_aT[mc], V(3))
                    wait(pool, pe_agg2, V(2))
                    g.tensor_tensor(aT_lo[:, mc, :], aT[par][:, mc, :], f(aT_hi[:, mc, :]),
                                    ALU.subtract).then_inc(aTlo[mc], 1)

                def rest(mc):
                    wait(pool, ac_Phi[mc], V(1))
                    wait(pool, pe_N, V(0))
                    g.tensor_tensor(P_lo[:, mc, :], P[:, mc % 2, :], f(P_hi[:, mc, :]),
                                    ALU.subtract).then_inc(po_Plo[mc], 1)

                if nxt:
                    wait(pool, x_in[1 - par], dma(1))
                    wait(pool, dv_x2, V(1))
                    g.tensor_tensor(x1[:, :, :], x_nat[1 - par][:, :, :], bc(bias0[:, :], NC),
                                    ALU.add).then_inc(po_xb, 1)
                if cur:
                    wait(pool, ac_c1, V(1))
                    wait(pool, pe_Q, V(0))
                    g.tensor_tensor(cs[:, :], c1[:, 0, :], c1[:, 1, :], ALU.add).then_inc(po_cs, 1)
                if nxt:
                    inverse_root(V, 2, 0)
                if prev:
                    wait(pool, ac_nn, V(0))
                    g.tensor_tensor(ga, x3T[1 - par][:, :], nn, ALU.add).then_inc(po_g, 1)
                if nxt:
                    inverse_root(V, 2, 1)
                if cur:
                    wait(pool, ac_L, V(1))
                    g.tensor_tensor(Lf[0:64, :], f(Lf[0:64, :]), sC[0:64, :], ALU.add).then_inc(po_L, 1)
                if nxt:
                    wait(pool, dv_x2, V(2))
                    wait(pool, dv_e, V(1))
                    g.tensor_tensor(tv[:, 0], x2[:, :, :], bc(v12[:, 0, :], NC), ALU.mult).then_inc(po_v, 1)
                if prev:
                    wait(pool, ac_half, V(0))
                    wait(pool, po_g, V(0))
                    g.tensor_tensor(ga, gd, ga, ALU.add).then_inc(po_y4, 1)
                if cur:
                    rest(0)
                    rest(1)
                if nxt:
                    wait(pool, dv_x3, V(1))
                    g.tensor_tensor(y3[:, :, :], x2[:, :, :], bc(wb_bc[:, :], NC), ALU.add).then_inc(po_x2b, 1)
                if prev:
                    inverse_root(V, 0, 3)
                    wait(pool, po_rs[3], V(0))
                    g.tensor_tensor(nms[:, :], mv[3][:, :, 0], rs[3][:, :], ALU.mult).then_inc(po_nms, 1)
                    hold(pool, po_nms, V(0))
                    g.tensor_scalar(nmr[:, :], nms[:, :], -1.0, None, ALU.mult).then_inc(po_nm, 1)
                if cur:
                    rest(2)
                    rest(3)
                if nxt:
                    inverse_root(V, 2, 2)
                if new:
                    split_rest(1)
                    split_rest(3)
            over_graphs(pool, turn)

        @block.scalar
        def _(act):
            s = nc.scalar
            def turn(V, dma, par, graph, has, outs):
                cur, nxt, prev, new = has(0), has(1), has(-1), has(2)

                def split_adjacency(mc):
                    wait(act, pe_aT[mc], V(3))
                    wait(act, pe_agg2, V(2))
                    s.activation(aT_hi[:, mc, :], AT_BANK[mc % 2][:, :], ACT.Identity).then_inc(ac_aThi[mc], 1)
                    wait(act, dv_P[NC - 1], V(1))
                    s.activation(aT[par][:, mc, :], AT_BANK[mc % 2][:, :], ACT.Identity).then_inc(ac_aT[mc], 1)

                def exponential(mc):
                    wait(act, pe_D[mc], V(1))
                    wait(act, dv_P[(mc + 2) % NC], V(0) if mc < 2 else V(1))
                    s.activation(E[:, mc % 2, :], AT_BANK[mc % 2][:, :], ACT.Exp, scale=2.0).then_inc(ac_E[mc], 1)

                def rounded(mc):
                    wait(act, dv_P[mc], V(1))
                    wait(act, pe_N, V(0))
                    s.activation(P_hi[:, mc, :], P[:, mc % 2, :], ACT.Identity).then_inc(ac_Phi[mc], 1)

                if cur:
                    wait(act, pe_x3T, V(1))
                    wait(act, pe_r, V(0))
                    s.activation(x3T_hi[:, :], X_BANK[:, :], ACT.Identity).then_inc(ac_x3Thi, 1)
                    s.activation(x3T[par][:, :], X_BANK[:, :], ACT.Identity).then_inc(ac_x3T, 1)
                if nxt:
                    wait(act, pe_agg1, V(2))
                    wait(act, pe_out2, V(1))
                    s.activation(agg_sb[:, :], AG_BANK[:, :], ACT.Identity).then_inc(ac_agg1, 1)
                if cur:
                    wait(act, pe_c1, V(1))
                    wait(act, po_cs, V(0))
                    wait(act, dv_c1, V(0))
                    s.activation(c1[:, :, HP:HP + HALF], CV_BANK[:, :].rearrange("p (i r) -> p r i", r=2), ACT.Relu,
                                 bias=bn_bias[:, 0:1]).then_inc(ac_c1, 1)
                if prev:
                    wait(act, dv_t, V(0))
                    s.activation(nn, gh, ACT.Tanh, bias=cols[:, BIH + 2:BIH + 3]).then_inc(ac_nn, 1)
                if cur:
                    wait(act, po_cs, V(1))
                    wait(act, pe_Q, V(0))
                    s.activation(cs_hi[:, :], cs[:, :], ACT.Identity).then_inc(ac_csh, 1)
                    wait(act, pe_s, V(1))
                    wait(act, dv_R, V(0))
                    s.activation(sC[0:32, :], SQ_BANK[0:32, :], ACT.Square, bias=se_bias[0:32, :]).then_inc(ac_s2, 1)
                    wait(act, pe_msg, V(1))
                    wait(act, pe_N, V(0))
                    s.activation(msg_hi[:, :], MS_BANK[:, :], ACT.Relu).then_inc(ac_msghi, 1)
                    wait(act, pe_sq, V(1))
                    s.activation(sC[0:96, :], SQ_BANK[0:96, :], ACT.Identity, bias=se_bias[0:96, :]).then_inc(ac_C, 1)
                    wait(act, ac_C, V(1))
                    s.activation(sH[:, :], sC[0:96, :], ACT.Identity).then_inc(ac_H, 1)
                    wait(act, ac_H, V(1))
                    wait(act, pe_D[NC - 1], V(0))
                    s.activation(Lf[0:64, :], f(sH[0:64, :]), ACT.Identity, scale=part_mask[0:64, 0:1]).then_inc(ac_L, 1)
                if cur:
                    wait(act, pe_hn, V(1))
                    wait(act, ac_nn, V(0))
                    s.activation(gh, HN_BANK[:, :], ACT.Identity, bias=gate_bias[:, 2:3], scale=0.5).then_inc(ac_gh, 1)
                if prev:
                    wait(act, dv_m, V(0))
                    s.activation(gd, gd, ACT.Identity, scale=0.5).then_inc(ac_half, 1)
                if cur:
                    exponential(0)
                if nxt:
                    wait(act, dv_f, V(2))
                    wait(act, dv_pf, V(1))
                    s.activation(pef[:, 1, :], ef[:, 1, :], ACT.Exp, bias=c12[:, 1:2]).then_inc(ac_pf, 1)
                if cur:
                    exponential(1)
                    rounded(0)
                    rounded(1)
                    exponential(2)
                    exponential(3)
                if cur:
                    wait(act, pe_Q, V(1))
                    wait(act, dv_conv, V(0))
                    s.activation(P0s, CV_BANK[:, 0:HALF], ACT.Identity).then_inc(ac_P0s, 1)
                if nxt:
                    wait(act, pe_den, V(2))
                    wait(act, pe_dcol, V(1))
                    s.activation(den_sb[:, :], SQ_BANK[0:2, :], ACT.Identity).then_inc(ac_den, 1)
                    wait(act, dv_e, V(2))
                    wait(act, dv_dq, V(1))
                    s.activation(pef[:, 0, :], ef[:, 0, :], ACT.Exp, bias=c12[:, 0:1]).then_inc(ac_pe, 1)
                if cur:
                    rounded(2)
                if nxt:
                    wait(act, pe_agg2, V(2))
                    s.activation(agg_sb[:, :], AG_BANK[:, :], ACT.Identity).then_inc(ac_agg2, 1)
                if cur:
                    rounded(3)
                if prev:
                    hold(act, po_nm, V(0))
                    hold(act, o_out, outs)
                    for c in range(NC):
                        last = s.activation(y_out[:, c, :], X_BANK[:, ch(c)], ACT.Identity, bias=nmr[:, c:c + 1],
                                            scale=rs[3][:, c:c + 1])
                    last.then_inc(ac_out, 1)
                if cur:
                    wait(act, dv_conv, V(1))
                    wait(act, pe_gn, V(0))
                    s.activation(xc_hi[:, :], conv, ACT.Relu).then_inc(ac_xchi, 1)
                if new:
                    wait(act, x_in[par], dma(2))
                    s.activation(x_hi[:, :, :], x_nat[par][:, :, :], ACT.Identity).then_inc(ac_xhi, 1)
                if cur:
                    wait(act, pe_N, V(1))
                    s.activation(nmp_hi[:, :], X_BANK[:, :], ACT.Identity).then_inc(ac_nmphi, 1)
                if new:
                    split_adjacency(0)
                    split_adjacency(1)
                if cur:
                    wait(act, pe_z, V(1))
                    wait(act, po_y4, V(0))
                    s.activation(th_z, MS_BANK[:, :], ACT.Tanh, bias=gate_bias[:, 1:2], scale=0.5).then_inc(ac_thz, 1)
                if new:
                    split_adjacency(2)
                    split_adjacency(3)
                if cur:
                    wait(act, pe_r, V(1))
                    s.activation(th_r, CV_BANK[:, :], ACT.Tanh, bias=gate_bias[:, 0:1], scale=0.5).then_inc(ac_thr, 1)

            over_graphs(act, turn)

        @block.vector
        def _(dve):
            v = nc.vector
            def statistics(i, V, k, src, meanwhile=None):
                for c in range(NC):
                    last = v.bn_stats(st[i][:, c, :], src(c))
                last.then_inc(dv_st[i], 1)
                if meanwhile:
                    meanwhile()
                hold(dve, dv_st[i], V(k))
                for c in range(NC):
                    last = v.bn_aggr(mv[i][:, c, :], st[i][:, c, :])
                last.then_inc(dv_mv[i], 1)

            def normalise(i, V, k, dst, src, done):
                hold(dve, po_rs[i], V(k))
                for c in range(NC):
                    last = v.tensor_scalar(dst[:, c, :], src[:, c, :], mv[i][:, c, 0:1], rs[i][:, c:c + 1],
                                           ALU.subtract, ALU.mult)
                last.then_inc(done, 1)

            def turn(V, dma, par, graph, has, outs):
                cur, nxt, prev, new = has(0), has(1), has(-1), has(2)

                def split_rest(mc):
                    wait(dve, ac_aT[mc], V(3))
                    wait(dve, pe_agg2, V(2))
                    v.tensor_tensor(aT_lo[:, mc, :], aT[par][:, mc, :], f(aT_hi[:, mc, :]),
                                    ALU.subtract).then_inc(aTlo[mc], 1)

                def weigh(mc):
                    wait(dve, ac_E[mc], V(1))
                    wait(dve, ac_aT[mc], V(1))
                    k = 0 if mc < 2 else 1
                    wait(dve, ac_Phi[(mc + 2) % NC], V(k))
                    wait(dve, po_Plo[(mc + 2) % NC], V(k))
                    v.tensor_tensor(P[:, mc % 2, :], E[:, mc % 2, :], aT[par][:, mc, :], ALU.mult).then_inc(dv_P[mc], 1)

                if cur:
                    wait(dve, ac_x3T, V(1))
                    wait(dve, pe_r, V(0))
                    v.tensor_tensor(x3T_lo[:, :], x3T[par][:, :], f(x3T_hi[:, :]), ALU.subtract).then_inc(dv_x3Tlo, 1)
                if prev:
                    wait(dve, ac_thr, V(0))
                    wait(dve, ac_gh, V(0))
                    v.scalar_tensor_tensor(gh, th_r, 1.0, gh, ALU.add, ALU.mult).then_inc(dv_t0, 1)
                    wait(dve, dv_t0, V(0))
                    wait(dve, pe_gn, V(0))
                    v.tensor_tensor(gh, SQ_BANK[:, :], gh, ALU.add).then_inc(dv_t, 1)

                def round_c1():
                    wait(dve, ac_c1, V(1))
                    wait(dve, pe_Q, V(0))
                    wait(dve, pe_P1, V(0))
                    v.tensor_copy(c1_hi[:, :, :], c1[:, :, :]).then_inc(dv_c1h, 1)

                if nxt:
                    wait(dve, pe_out0, V(2))
                    wait(dve, po_xb, V(2))
                    v.tensor_tensor(x1[:, :, :], AG_BANK[:, :].rearrange("p (c d) -> p c d", c=NC), x1[:, :, :],
                                    ALU.add).then_inc(dv_y1, 1)
                    hold(dve, dv_y1, V(2))
                    statistics(0, V, 2, lambda c: x1[:, c, :], round_c1 if cur else None)
                elif cur:
                    round_c1()
                if cur:
                    wait(dve, dv_c1h, V(1))
                    v.tensor_tensor(c1_lo[:, :, :], c1[:, :, :], f(c1_hi[:, :, :]), ALU.subtract).then_inc(dv_c1, 1)
                if prev:
                    wait(dve, ac_nn, V(0))
                    v.tensor_tensor(gd, x3T[1 - par][:, :], nn, ALU.subtract).then_inc(dv_d, 1)
                if nxt:
                    normalise(0, V, 2, x1, x1, dv_x1)
                if cur:
                    wait(dve, ac_csh, V(1))
                    v.tensor_tensor(cs_lo[:, :], cs[:, :], f(cs_hi[:, :]), ALU.subtract).then_inc(dv_csp, 1)
                if nxt:
                    wait(dve, dv_x1, V(2))
                    wait(dve, f_in[1 - par], dma(1))
                    v.tensor_tensor(x1[0:NODES, 0, :], x1[0:NODES, 0, :], fused_in[1 - par][:, :],
                                    ALU.add).then_inc(dv_fused, 1)
                    hold(dve, dv_fused, V(2))
                    statistics(1, V, 2, lambda c: x1[:, c, :])
                if cur:
                    wait(dve, ac_H, V(1))
                    wait(dve, pe_D[NC - 1], V(0))
                    v.scalar_tensor_tensor(Rf[0:32, :], f(sH[0:32, :]), part_mask[0:32, 1:2], sC[0:32, :],
                                           ALU.mult, ALU.add)
                    v.scalar_tensor_tensor(Rf[64:96, :], f(sH[64:96, :]), part_mask[64:96, 1:2], sC[64:96, :],
                                           ALU.mult, ALU.add).then_inc(dv_R, 1)
                if nxt:
                    hold(dve, po_x2b, V(1))
                    normalise(1, V, 2, x2, x1, dv_x2)
                if cur:
                    wait(dve, pe_msg, V(1))
                    wait(dve, ac_msghi, V(1))
                    wait(dve, pe_N, V(0))
                    v.scalar_tensor_tensor(msg_lo[:, :], MS_BANK[:, :], 0.0, f(msg_hi[:, :]), ALU.max,
                                           ALU.subtract).then_inc(dv_msglo, 1)
                if nxt:
                    wait(dve, dv_x2, V(2))
                    v.tensor_tensor(tv[:, 1], x2[:, :, :], bc(v12[:, 1, :], NC), ALU.mult).then_inc(dv_v, 1)
                if prev:
                    wait(dve, dv_d, V(0))
                    wait(dve, ac_thz, V(0))
                    v.scalar_tensor_tensor(gd, th_z, 1.0, gd, ALU.add, ALU.mult).then_inc(dv_m, 1)
                if nxt:
                    hold(dve, dv_v, V(2))
                    hold(dve, ac_pf, V(1))
                    v.reduce_sum(ef[:, 1, :], tv[:, 1], X).then_inc(dv_f, 1)
                if cur:
                    weigh(0)
                if nxt:
                    hold(dve, ac_pf, V(2))
                    hold(dve, pe_den, V(1))
                    v.tensor_copy(pf2[:, :, 0], pef[:, 1, :]).then_inc(dv_pfh, 1)
                    hold(dve, pe_agg1, V(2))
                    for c in range(NC):
                        last = v.tensor_scalar(x_hi[:, c, :], x2[:, c, :], pef[:, 1, c:c + 1], None, ALU.mult)
                    last.then_inc(dv_xshi, 1)
                    wait(dve, dv_pfh, V(2))
                    v.tensor_tensor(pf2[:, :, 1], pef[:, 1, :], f(pf2[:, :, 0]), ALU.subtract).then_inc(dv_pf, 1)
                if cur:
                    weigh(1)
                if nxt:
                    wait(dve, dv_xshi, V(2))
                    for c in range(NC):
                        last = v.scalar_tensor_tensor(x_lo[:, c, :], x2[:, c, :], pef[:, 1, c:c + 1], f(x_hi[:, c, :]),
                                                      ALU.mult, ALU.subtract)
                    last.then_inc(dv_xslo, 1)
                if prev:
                    hold(dve, pe_yT, V(0))
                    statistics(3, V, 0, lambda c: X_BANK[:, ch(c)])
                if nxt:
                    hold(dve, po_v, V(2))
                    hold(dve, ac_pe, V(1))
                    v.reduce_sum(ef[:, 0, :], tv[:, 0], X).then_inc(dv_e, 1)
                if cur:
                    weigh(2)
                    weigh(3)
                    even, odd = (conv.rearrange("p (i r) -> p r i", r=2)[:, r, :] for r in range(2))
                    xe, xo = (x3T[par][:, :].rearrange("p (i r) -> p r i", r=2)[:, r, :] for r in range(2))
                    wait(dve, pe_P1, V(1))
                    wait(dve, ac_x3T, V(1))
                    wait(dve, ac_xchi, V(0))
                    wait(dve, dv_xclo, V(0))
                    v.scalar_tensor_tensor(even, MS_BANK[:, 0:HALF], bn_bias[:, 1:2], xe, ALU.add, ALU.add)
                    v.scalar_tensor_tensor(odd, xo, bn_bias[:, 1:2], MS_BANK[:, 1:HALF + 1], ALU.add,
                                           ALU.subtract).then_inc(dv_ab, 1)
                    wait(dve, dv_ab, V(1))
                    wait(dve, ac_P0s, V(1))
                    v.tensor_tensor(odd, CV_BANK[:, HALF:N], odd, ALU.add).then_inc(dv_q, 1)
                    v.tensor_tensor(even, even, P0s, ALU.add)
                    wait(dve, dv_q, V(1))
                    v.tensor_tensor(odd, odd, P0s, ALU.subtract).then_inc(dv_conv, 1)
                if nxt:
                    wait(dve, pe_dcol, V(2))
                    wait(dve, ac_pe, V(2))
                    v.tensor_tensor(dq[:, 0, :], SQ_BANK[:, 0:NC], pef[:, 0, :], ALU.mult).then_inc(dv_q0, 1)
                    hold(dve, dv_q0, V(2))
                    v.reciprocal(dq[:, 1, :], dq[:, 0, :]).then_inc(dv_q1, 1)
                    wait(dve, dv_q1, V(2))
                    v.tensor_tensor(dq[:, 2, :], dq[:, 1, :], pef[:, 0, :], ALU.mult).then_inc(dv_dq, 1)
                    wait(dve, pe_out2, V(2))
                    wait(dve, po_x2b, V(2))
                    wait(dve, dv_dq, V(2))
                    for c in range(NC):
                        last = v.scalar_tensor_tensor(y3[:, c, :], AG_BANK[:, ch(c)], dq[:, 2, c:c + 1], y3[:, c, :],
                                                      ALU.mult, ALU.add)
                    last.then_inc(dv_y3, 1)
                if cur:
                    wait(dve, ac_xchi, V(1))
                    wait(dve, pe_gn, V(0))
                    v.scalar_tensor_tensor(xc_lo[:, :], conv, 0.0, f(xc_hi[:, :]), ALU.max,
                                           ALU.subtract).then_inc(dv_xclo, 1)
                if nxt:
                    hold(dve, dv_y3, V(2))
                    statistics(2, V, 2, lambda c: y3[:, c, :])
                if cur:
                    wait(dve, ac_nmphi, V(1))
                    wait(dve, pe_gn, V(0))
                    v.tensor_tensor(nmp_lo[:, :], X_BANK[:, :], f(nmp_hi[:, :]), ALU.subtract).then_inc(dv_nmplo, 1)
                if nxt:
                    hold(dve, pe_x3T, V(1))
                    normalise(2, V, 2, x3, y3, dv_x3)
                if new:
                    wait(dve, ac_xhi, V(3))
                    wait(dve, x_in[par], dma(2))
                    v.tensor_tensor(x_lo[:, :, :], x_nat[par][:, :, :], f(x_hi[:, :, :]),
                                    ALU.subtract).then_inc(dv_xlo, 1)
                    split_rest(0)
                    split_rest(2)

            over_graphs(dve, turn)

        @block.tensor
        def _(pe):
            t_ = nc.tensor
            def turn(V, dma, par, graph, has, outs):
                cur, nxt, prev, new = has(0), has(1), has(-1), has(2)

                def transpose_adjacency(mc):
                    for c in range(NC):
                        last = t_.transpose(AT_BANK[mc % 2][:, ch(c)], adj_nat[par][:, c, ch(mc)], ident[:, :])
                    last.then_inc(pe_aT[mc], 1)

                def distances(mc):
                    t_.matmul(AT_BANK[mc % 2][:, :], Lf[:, ch(mc)], Rf[:, :], start=True, stop=True
                              ).then_inc(pe_D[mc], 1)

                def taps(o, first, count, hi, lo, start_col, width, done):
                    for k, blk in enumerate(range(first, first + count)):
                        w = range(start_col + k, start_col + k + width)
                        last = three(pe, o, w_hi[:, tapblk(blk), :], w_lo[:, tapblk(blk), :],
                                     hi[:, w.start:w.stop], lo[:, w.start:w.stop], k == 0, k == count - 1)
                    last.then_inc(done, 1)

                def gate(o, parts, done, k):
                    for i, (blk, hi, lo) in enumerate(parts):
                        if i == len(parts) - 1:
                            wait(pe, dv_nmplo, V(k))
                        last = three(pe, o, w_hi[:, blk, :], w_lo[:, blk, :], hi, lo, i == 0, i == len(parts) - 1)
                    last.then_inc(done, 1)

                def of_inputs(g):
                    return [(IH + 2 * g, xc_hi[:, :], xc_lo[:, :]), (IH + 2 * g + 1, nmp_hi[:, :], nmp_lo[:, :])]

                def of_state(g):
                    return [(HH + g, x3T_hi[:, :], x3T_lo[:, :])]

                if cur:
                    wait(pe, dv_x3, V(1))
                    wait(pe, dv_nmplo, V(0))
                    for c in range(NC):
                        last = t_.transpose(X_BANK[:, ch(c)], x3[:, c, :], ident[:, :])
                    last.then_inc(pe_x3T, 1)
                if nxt:
                    wait(pe, ac_xhi, V(2))
                    wait(pe, dv_xlo, V(2))
                    wait(pe, dv_y3, V(1))
                    for mc in range(NC):
                        wait(pe, aTlo[mc], V(2))
                        last = three(pe, AG_BANK[:, :], x_hi[:, mc, :], x_lo[:, mc, :], aT_hi[:, mc, :],
                                     aT_lo[:, mc, :], mc == 0, mc == NC - 1)
                    last.then_inc(pe_agg1, 1)
                if prev:
                    if cur:
                        wait(pe, dv_q0, V(1))
                    gate(SQ_BANK[:, :], of_inputs(2), pe_gn, 0)
                if nxt:
                    wait(pe, ac_agg1, V(2))
                    for c in range(NC):
                        last = t_.matmul(AG_BANK[:, ch(c)], agg_sb[:, ch(c)], w0[:, :], start=True, stop=True)
                    last.then_inc(pe_out0, 1)
                if cur:
                    wait(pe, ac_x3T, V(1))
                    wait(pe, dv_x3Tlo, V(1))
                    wait(pe, ac_thr, V(0))
                    three(pe, CV_BANK[:, :], w_hi[:, CONV1, :], w_lo[:, CONV1, :], x3T_hi[:, :], x3T_lo[:, :],
                          True, True).then_inc(pe_c1, 1)
                    wait(pe, ac_gh, V(0))
                    three(pe, HN_BANK[:, :], w_hi[:, HH + 2, :], w_lo[:, HH + 2, :], x3T_hi[:, :], x3T_lo[:, :],
                          True, True).then_inc(pe_hn, 1)
                if cur:
                    wait(pe, dv_t, V(0))
                    three(pe, SQ_BANK[:, :], w_hi[:, SE, :], w_lo[:, SE, :], x3T_hi[:, :], x3T_lo[:, :],
                          True, True).then_inc(pe_s, 1)
                    wait(pe, ac_thz, V(0))
                    t_.matmul(MS_BANK[:, :], ones_r[:, :], msg_bias[:, :, :].rearrange("p c d -> p (c d)"),
                              start=True, stop=False)
                    for c in range(NC):
                        last = t_.matmul(MS_BANK[:, ch(c)], x3T[par][:, ch(c)], wmsgT, start=False, stop=(c == NC - 1))
                    last.then_inc(pe_msg, 1)
                    wait(pe, ac_s2, V(1))
                    t_.matmul(SQ_BANK[:, :], sq_pick[0:32, :], sC[0:32, :], start=False, stop=True,
                              skip_group_check=True).then_inc(pe_sq, 1)
                    wait(pe, dv_c1, V(1))
                    taps(CV_BANK[:, 0:HALF], 0, EVEN, c1_hi[:, 0, :], c1_lo[:, 0, :], 0, HALF, pe_P0)
                    wait(pe, dv_csp, V(1))
                    taps(CV_BANK[:, HALF:N], EVEN + ODD, EVEN, cs_hi, cs_lo, 0, HALF, pe_Q)
                    wait(pe, dv_R, V(1))
                    wait(pe, po_L, V(1))
                    for mc in range(2):
                        wait(pe, ac_E[mc + 2], V(0))
                        if nxt:
                            wait(pe, ac_aT[mc + 2], V(2))
                        distances(mc)
                    wait(pe, dv_msglo, V(1))
                    taps(MS_BANK[:, 0:P1W], EVEN, ODD, c1_hi[:, 1, :], c1_lo[:, 1, :], 0, P1W, pe_P1)
                    for mc in range(2, NC):
                        wait(pe, ac_E[mc - 2], V(1))
                        distances(mc)
                if prev:
                    wait(pe, po_y4, V(0))
                    if cur:
                        wait(pe, ac_x3T, V(1))
                    for c in range(NC):
                        last = t_.transpose(X_BANK[:, ch(c)], ga[:, ch(c)], ident[:, :])
                    last.then_inc(pe_yT, 1)
                if nxt:
                    wait(pe, dv_pf, V(2))
                    for mc in range(NC):
                        t_.matmul(SQ_BANK[0:2, :], pf2[:, mc, :], aT_hi[:, mc, :], start=(mc == 0), stop=False)
                        last = t_.matmul(SQ_BANK[0:2, :], pf2[:, mc, :], aT_lo[:, mc, :], start=False,
                                         stop=(mc == NC - 1))
                    last.then_inc(pe_den, 1)
                    wait(pe, dv_xslo, V(2))
                    for mc in range(NC):
                        last = three(pe, AG_BANK[:, :], x_hi[:, mc, :], x_lo[:, mc, :], aT_hi[:, mc, :],
                                     aT_lo[:, mc, :], mc == 0, mc == NC - 1)
                    last.then_inc(pe_agg2, 1)
                    wait(pe, ac_den, V(2))
                    for c in range(NC):
                        last = t_.matmul(SQ_BANK[:, c:c + 1], den_sb[0:2, ch(c)], ones[0:2, 0:1], start=True, stop=True)
                    last.then_inc(pe_dcol, 1)
                    wait(pe, ac_agg2, V(2))
                    for c in range(NC):
                        last = t_.matmul(AG_BANK[:, ch(c)], agg_sb[:, ch(c)], wwT, start=True, stop=True)
                    last.then_inc(pe_out2, 1)
                if new:
                    wait(pe, adj_in[par], dma(2))
                    for mc in range(2):
                        wait(pe, ac_E[mc + 2], V(1))
                        transpose_adjacency(mc)
                if cur:
                    if prev:
                        wait(pe, ac_out, V(0))
                    for mc in range(NC):
                        wait(pe, ac_Phi[mc], V(1))
                        wait(pe, po_Plo[mc], V(1))
                        last = three(pe, X_BANK[:, :], msg_hi[:, ch(mc)], msg_lo[:, ch(mc)], P_hi[:, mc, :],
                                     P_lo[:, mc, :], mc == 0, mc == NC - 1)
                    last.then_inc(pe_N, 1)
                if cur:
                    wait(pe, dv_xclo, V(1))
                    gate(MS_BANK[:, :], of_state(1) + of_inputs(1), pe_z, 1)
                if new:
                    for mc in range(2, NC):
                        wait(pe, ac_aT[mc - 2], V(3))
                        transpose_adjacency(mc)
                if cur:
                    gate(CV_BANK[:, :], of_state(0) + of_inputs(0), pe_r, 1)

            over_graphs(pe, turn)


def kernel(**inputs):
    import numpy as _np
    import concourse.bacc as _bacc
    from concourse import mybir as _mybir
    from concourse.bass_utils import run_bass_kernel_spmd as _run

    nc = _bacc.Bacc("TRN2", target_bir_lowering=False, num_devices=1)
    arrays, aps = {}, {}
    for name, value in inputs.items():
        value = _np.ascontiguousarray(value)
        arrays[f"in_{name}_dram"] = value
        aps[name] = nc.dram_tensor(f"in_{name}_dram", value.shape, _mybir.dt.from_np(value.dtype),
                                   kind="ExternalInput").ap()
    out = nc.dram_tensor("out_0_dram", (B, N, D), _mybir.dt.float32, kind="ExternalOutput").ap()
    network_kernel(nc, aps, out)
    r = _run(nc, [arrays], core_ids=[0])
    return r.results[0]["out_0_dram"]
```

```python
import concourse.bass as bass
from concourse import mybir
from contextlib import ExitStack

B, N, D = 16, 512, 128
NC = N // 128
HID = 256
GROUPS = [[(0, 25)], [(0, 9)], [(0, 1), (9, 15)], [(6, 9), (12, 15)], [(3, 6), (9, 12)]]
NG = len(GROUPS)
NODES = 25
SLOT = 32
GT = B // 4
TAPS = 17
PAD = TAPS // 2
EVEN, ODD = TAPS // 2 + 1, TAPS // 2
HALF = N // 2
HP = PAD // 2
PH = HALF + 2 * HP + 2
P1W = HALF + 2
EPS = 1e-5
SE, CONV1, IH, HH, TAP, SUMTAP = 0, 1, 2, 8, 11, 28
NW = SUMTAP + EVEN - 1
A1, A2, WB, G1, BB1, M1, V1, G2, BB2, M2, V2, BIH, BHH, HB = 0, 1, 2, 3, 4, 5, 6, 7, 8, 9, 10, 11, 14, 17
NROWS = HB + NG * HID // 128
NCST2 = 4 + 2 * NC + 4


def network_kernel(nc, a, out):
    f32 = mybir.dt.float32
    f32r = mybir.dt.float32r
    ALU = mybir.AluOpType
    ACT = mybir.ActivationFunctionType
    X = mybir.AxisListType.X

    ctx = ExitStack()
    with ctx:
        def sb(name, shape, dt=f32):
            return ctx.enter_context(nc.sbuf_tensor(name, shape, dt))

        def sem(name):
            return ctx.enter_context(nc.semaphore(name))

        def sems(name, n):
            return [sem(f"{name}{i}") for i in range(n)]

        def f(ap):
            return ap.bitcast(f32)

        fused_dram = nc.dram_tensor("fused_dram", (B, SLOT, D), f32, kind="Internal").ap()

        bank = [ctx.enter_context(nc.psum_tensor(f"bank{i}", [128, 512], f32)) for i in range(8)]
        AT_BANK = [bank[0], bank[1]]
        X_BANK = bank[2]
        CV_BANK = bank[3]
        MS_BANK = bank[4]
        AG_BANK = bank[5]
        SQ_BANK = bank[6]
        HN_BANK = bank[7]

        ident = sb("ident", [128, 128])
        ones = sb("ones", [128, 128])
        neg_half = sb("neg_half", [128, GT * NG])
        bias0 = sb("bias0", [128, D])
        w0 = sb("w0", [128, D])
        wb_bc = sb("wb_bc", [128, D])
        v12 = sb("v12", [128, 2, D])
        c12 = sb("c12", [128, 2])
        ab_col = sb("ab_col", [128, 1])
        plainT = sb("plainT", [128, 2, 128])
        wwT, wmsgT = plainT[:, 0, :], plainT[:, 1, :]
        w_hi = sb("w_hi", [128, NW, 128], f32r)
        w_lo = sb("w_lo", [128, NW, 128], f32r)
        msg_bias_f = sb("msg_bias_f", [64, NC, D])
        msg_bias = sb("msg_bias", [64, NC, D], f32r)
        ones_r = sb("ones_r", [64, 128], f32r)
        cols = sb("cols", [128, NROWS])
        bn_scale = sb("bn_scale", [128, 2])
        bn_bias = sb("bn_bias", [128, 2])
        gate_bias = sb("gate_bias", [128, 3])
        se_bias = sb("se_bias", [128, 1])
        part_mask = sb("part_mask", [128, 2])
        sq_pick = sb("sq_pick", [128, 128])

        adj_nat = [sb(f"adj_nat{i}", [128, NC, N]) for i in range(2)]
        x_nat = [sb(f"x_nat{i}", [128, NC, D]) for i in range(2)]
        fused_in = [sb(f"fused_in{i}", [NODES, D]) for i in range(2)]
        Lf = sb("Lf", [96, N], f32r)
        Rf = sb("Rf", [96, N], f32r)
        c1 = sb("c1", [128, 2, PH])

        before_loop = ExitStack()

        def early(name, shape):
            return before_loop.enter_context(nc.sbuf_tensor(name, shape, f32))

        adjP = early("adjP", [128, GT, N])
        xP = early("xP", [128, GT, D])
        x_all = early("x_all", [128, B, NC, D])
        aPT = [early(f"aPT{i}", [128, N]) for i in range(2)]
        aggP = early("aggP", [128, N])
        TTs = early("TTs", [128, N])
        x1P = early("x1P", [128, GT, D])
        A0 = early("A0", [128, GT, 128])
        CM, GM = [early(name, [128, NG, 128]) for name in ("CM", "GM")]
        A5 = early("A5", [128, GT, NG, 128])
        nadjT = early("nadjT", [128, GT, NG, 128])
        U = early("U", [128, NG, GT, 128])
        hw1 = early("hw1", [128, NG, HID])
        hw2 = early("hw2", [128, NG, 2, D])
        hT, S2, R2 = adj_nat[1][:, 0:2, :], adj_nat[1][:, 2, :], adj_nat[1][:, 3, :]
        o2b = [early(f"o2b{i}", [128, N]) for i in range(2)]
        fusedP = early("fusedP", [128, GT, D])
        nat_c2 = early("nat_c2", [128, D, TAPS])
        nat_sum = early("nat_sum", [128, D, ODD])
        nat_ih = early("nat_ih", [128, 3, 2, 128])
        nat_hh = early("nat_hh", [128, 3, 128])
        nat_ww = early("nat_ww", [128, 2, 128])
        nat_se = early("nat_se", [128, 128])
        nat_c1 = early("nat_c1", [128, 128])
        abc = early("abc", [128, 2, 128])
        mb_rest = early("mb_rest", [64, NC, D])
        vrows = early("vrows", [32, 128])
        fw = early("fw", [128, 4, NG])
        fmx = early("fmx", [128, 3])
        rm = early("rm", [128, NG])
        wm = early("wm", [128, NG])
        mk = early("mk", [128, 2, 128])
        deg = early("deg", [128, 4, GT * NG])
        hb2 = early("hb2", [128, NG, D])
        stP = early("stP", [128, GT, 6])
        mvP = early("mvP", [128, GT, 2])
        veP = early("veP", [128, GT])
        rsP = early("rsP", [128, GT])

        def wait(eng, s, count):
            if not (isinstance(count, int) and count <= 0):
                eng.wait_ge(s, count)

        def hold(eng, s, count):
            if not (isinstance(count, int) and count <= 0):
                eng.wait_ge(s, count)
                eng.nop(nofuse=True)

        def over_graphs(eng, step, start=-2):
            end = B - 3
            def fixed(b):
                step(lambda k: b + k, lambda k: 16 * ((b + k) // 2 + 1), b % 2, lambda k: b + k,
                     lambda k: 0 <= b + k < B, 16 * b)
            for b in range(start, 1):
                fixed(b)
            with eng.Fori(1, end, 2) as b:
                v = [eng.snap(b + k) for k in range(0, 5)]
                d = [eng.snap(b * 8 + k) for k in (8, 24, 40)]
                o = [eng.snap(b * 16 + k) for k in (0, 16)]
                for h in range(2):
                    step(lambda k, h=h: v[h + k], lambda k, h=h: d[(h + k + 1) // 2], (1 + h) % 2,
                         lambda k, h=h: b + (h + k), lambda k: True, o[h])
            for b in range(end, B + 1):
                fixed(b)

        def three(pe, o, lh, ll, rh, rl, start, stop):
            nc.tensor.matmul(o, lh, rh, start=start, stop=False)
            nc.tensor.matmul(o, lh, rl, start=False, stop=False)
            return nc.tensor.matmul(o, ll, rh, start=False, stop=stop)

        def ch(c):
            return slice(c * 128, (c + 1) * 128)

        def bc(ap, n):
            return ap.unsqueeze(1).to_broadcast([128, n, ap.shape[-1]])

        def spread(ap, n):
            return ap.unsqueeze(2).to_broadcast([128, ap.shape[-1], n])

        x_v = a["x"].rearrange("b (c p) d -> b p c d", p=128)
        adj_v = a["adj"].rearrange("b (c p) m -> b p c m", p=128)
        out_v = out.rearrange("b (c p) d -> b p c d", p=128)
        four = "(t j) n d -> j n t d"

        x_in, adj_in, f_in = sems("x_in", 2), sems("adj_in", 2), sems("f_in", 2)
        fused_out = sem("fused_out")

        before = []

        def ready(names):
            made = [nc.alloc_semaphore(name=name) for name in names.split()]
            before.extend(made)
            return made

        q_zero, q_ident, q_mask, q_mt, q_gm = ready("q_zero q_ident q_mask q_mt q_gm")
        q_wt, q_cst, q_cst2, q_row, q_adjP, q_xP, q_h = ready("q_wt q_cst q_cst2 q_row q_adjP q_xP q_h")
        q_cols, q_colsb, q_bnv, q_bnr, q_bns, q_sc, q_sum = ready("q_cols q_colsb q_bnv q_bnr q_bns q_sc q_sum")
        q_abc, q_v, q_vsb, q_c12, q_gb, q_mb = ready("q_abc q_v q_vsb q_c12 q_gb q_mb")
        q_wps, q_whi, q_wlo = ready("q_wps q_whi q_wlo")
        q_fm, q_fs, q_fe, q_fd, q_fr, q_wm = ready("q_fm q_fs q_fe q_fd q_fr q_wm")
        q_aP, q_aPT, q_TT, q_ag, q_agT, q_TTs, q_o = ready("q_aP q_aPT q_TT q_ag q_agT q_TTs q_o")
        q_xPb, q_yP, q_stP, q_mvP, q_veP, q_rsP, q_x1P = ready("q_xPb q_yP q_stP q_mvP q_veP q_rsP q_x1P")
        (q_A0, q_A1, q_A5, q_dg, q_dg1, q_dg2, q_dgz, q_dgp, q_dgi, q_B, q_BT, q_nT) = ready(
            "q_A0 q_A1 q_A5 q_dg q_dg1 q_dg2 q_dgz q_dgp q_dgi q_B q_BT q_nT")
        (q_U, q_Us, q_h2, q_hT, q_S2, q_S2s, q_o2, q_ob, q_R2, q_fu) = ready(
            "q_U q_Us q_h2 q_hT q_S2 q_S2s q_o2 q_ob q_R2 q_fu")
        q_xr = ready(" ".join(f"q_xr{t}" for t in range(GT)))

        blocks = ([nat_ww[:, 0, :], nat_ww[:, 1, :]], [nat_se[:, :], nat_c1[:, :]]
                  + [nat_ih[:, g, h, :] for g in range(3) for h in range(2)] + [nat_hh[:, g, :] for g in range(3)]
                  + [nat_c2[:, :, k] for k in range(TAPS)] + [nat_sum[:, :, k] for k in range(ODD)])
        WG = NW // 4
        W_BANK = bank[5:8]
        U_BANK = [bank[i] for i in (2, 3, 5, 6, 7)]
        WEIGHTS_AT = [[-1], [0, 1, 2], [3, 4], [5, 6], [7, 8]]

        def tapblk(i):
            if i < EVEN:
                return TAP + 2 * i
            if i < TAPS:
                return TAP + 2 * (i - EVEN) + 1
            return TAP if i == TAPS else SUMTAP + i - TAPS - 1

        with nc.Block() as block:
            @block.sync
            def _(sp):
                for j in range(4):
                    sp.dma_start(adjP[SLOT * j:SLOT * (j + 1), :, :],
                                 a["adj"].rearrange("(t j) n m -> j n t m", j=4)[j, 0:SLOT]).then_inc(q_adjP, 16)
                for t in range(GT):
                    sp.dma_start(x_all[:, 4 * t:4 * t + 4, :, :].rearrange("p j c d -> p (j c) d"),
                                 x_v[4 * t:4 * t + 4].rearrange("j p c d -> p j c d")).then_inc(q_xr[t], 16)
                    if t == 0:
                        for j in range(4):
                            sp.dma_start(xP[SLOT * j:SLOT * (j + 1), :, :],
                                         a["x"].rearrange(four, j=4)[j, 0:SLOT]).then_inc(q_xP, 16)
                sp.dma_start(hw1[:, :, :], a["L1_gnn_W1"].rearrange("g i h -> i g h")).then_inc(q_h, 16)
                sp.dma_start(hw2[:, :, :, :], a["L1_gnn_W2"].rearrange("g (h p) o -> p g h o", h=2)).then_inc(q_h, 16)
                for row, name, n in ((A1, "L2_gnn_a_w", 2), (WB, "L2_gnn_W_b", 1), (G1, "L3_gnn_bn1_g", 1),
                                     (BB1, "L3_gnn_bn1_b", 1), (M1, "L3_gnn_bn1_m", 1), (V1, "L3_gnn_bn1_v", 1),
                                     (G2, "L3_gnn_bn2_g", 1), (BB2, "L3_gnn_bn2_b", 1), (M2, "L3_gnn_bn2_m", 1),
                                     (V2, "L3_gnn_bn2_v", 1), (BIH, "L3_gnn_b_ih", 3), (BHH, "L3_gnn_b_hh", 3)):
                    sp.dma_start(vrows[row:row + n, :], a[name].rearrange("(n d) -> n d", n=n)).then_inc(q_row, 16)
                sp.dma_start(vrows[HB:NROWS, :], a["L1_gnn_b1"].rearrange("g (h d) -> (g h) d", h=2)).then_inc(q_row, 16)
                for dst, src in ((fw[:, 0, :], a["L1_gnn_fusion_w"].partition_broadcast(128)),
                                 (hb2[:, :, :], a["L1_gnn_b2"].partition_broadcast(128)),
                                 (ab_col[:, :], a["L2_gnn_a_b"].partition_broadcast(128)),
                                 (wb_bc[:, :], a["L2_gnn_W_b"].partition_broadcast(128))):
                    sp.dma_start(dst, src).then_inc(q_cst2, 16)
                sp.wait_ge(q_zero, 1)
                for row in (0, 32):
                    for c in range(NC):
                        sp.dma_start(msg_bias_f[row:row + 1, c, :], a["L3_gnn_b_msg"].unsqueeze(0)).then_inc(q_cst2, 16)
                for j in range(4):
                    sp.dma_start(se_bias[3 * j:3 * j + 3, :], a["L3_gnn_b_se"].unsqueeze(1)).then_inc(q_cst2, 16)
                sp.dma_start(nat_ww[:, 0, :], a["L2_gnn_W_w"]).then_inc(q_wt, 16)
                sp.dma_start(nat_ww[:, 1, :], a["L3_gnn_w_msg"]).then_inc(q_wt, 16)
                sp.dma_start(nat_c1[:, :], a["L3_gnn_conv1_w"].rearrange("o i k -> o (i k)")).then_inc(q_wt, 16)
                sp.dma_start(nat_c2[:, :, :], a["L3_gnn_conv2_w"]).then_inc(q_wt, 16)
                sp.dma_start(nat_ih[:, :, :, :], a["L3_gnn_w_ih"].rearrange("(g o) (h k) -> o g h k", g=3, h=2)).then_inc(q_wt, 16)
                sp.dma_start(nat_hh[:, :, :], a["L3_gnn_w_hh"].rearrange("(g o) k -> o g k", g=3)).then_inc(q_wt, 16)
                for j in range(4):
                    sp.dma_start(nat_se[3 * j:3 * j + 3, :], a["L3_gnn_w_se"]).then_inc(q_wt, 16)
                sp.dma_start(x_nat[0][:, :, :], x_v[0]).then_inc(x_in[0], 16)
                sp.wait_ge(q_nT, GT)
                sp.dma_start(adj_nat[0][:, :, :], adj_v[0]).then_inc(adj_in[0], 16)
                sp.wait_ge(q_fu, NG)
                for j in range(4):
                    sp.dma_start(fused_dram.rearrange(four, j=4)[j],
                                 fusedP[SLOT * j:SLOT * (j + 1), :, :]).then_inc(fused_out, 16)

            @block.gpsimd
            def _(pool):
                g = nc.gpsimd
                g.memset(ident[:, :], 0.0)
                g.memset(nat_se[:, :], 0.0)
                g.memset(se_bias[:, :], 0.0)
                g.memset(msg_bias_f[:, :, :], 0.0).then_inc(q_zero, 1)
                for tile_, value in ((ones[:, :], 1.0), (neg_half[:, :], -0.5), (f(ones_r[:, :]), 1.0), (c1[:, :, :], 0.0),
                                     (sq_pick[:, :], 0.0),
                                     (mk[:, :, :], 0.0), (CM[:, :, :], 0.0)):
                    g.memset(tile_, value)
                g.memset(A0[:, :, :], 0.0).then_inc(q_zero, 1)
                pool.wait_ge(q_zero, 2)
                g.affine_select(out=ident[:, :], in_=ident[:, :], compare_op=ALU.not_equal, fill=1.0, base=0,
                                pattern=[[-1, 128]], channel_multiplier=1).then_inc(q_ident, 1)
                pool.wait_ge(q_xP, 16 * 4)
                pool.wait_ge(q_cst, 16 * 2)
                g.tensor_tensor(xP[:, :, :], xP[:, :, :], bc(bias0[:, :], GT), ALU.add).then_inc(q_xPb, 1)
                pool.wait_ge(q_dg2, 1)
                g.tensor_tensor(deg[:, 2, :], deg[:, 0, :], neg_half[:, :], ALU.pow).then_inc(q_dgp, 1)
                pool.wait_ge(q_mvP, 1)
                pool.nop(nofuse=True)
                g.tensor_scalar(veP[:, :], mvP[:, :, 1], EPS, None, ALU.add).then_inc(q_veP, 1)
                pool.wait_ge(q_veP, 1)
                g.tensor_tensor(rsP[:, :], veP[:, :], neg_half[:, 0:GT], ALU.pow).then_inc(q_rsP, 1)
                pool.wait_ge(q_colsb, 1)
                pool.nop(nofuse=True)
                g.tensor_scalar(bn_bias[:, :], cols[:, V1:V2 + 1:V2 - V1], EPS, None, ALU.add).then_inc(q_bnv, 1)
                pool.wait_ge(q_bnv, 1)
                g.tensor_tensor(bn_scale[:, :], bn_bias[:, :], neg_half[:, 0:2], ALU.pow).then_inc(q_bnr, 1)

            @block.scalar
            def _(act):
                s = nc.scalar

                for dst, name in ((w0[:, :], "L0_gnn_weight"), (bias0[:, :], "L0_gnn_bias")):
                    act.dma_start(dst, a[name] if name == "L0_gnn_weight" else a[name].partition_broadcast(128)
                                  ).then_inc(q_cst, 16)

                def own_sums(t):
                    act.wait_ge(q_TT, t + 1)
                    for j in range(4):
                        last = s.activation(aggP[SLOT * j:SLOT * (j + 1), ch(t)],
                                            bank[2 + t % 2][SLOT * j:SLOT * (j + 1), ch(j)], ACT.Identity)
                    last.then_inc(q_ag, 1)

                for t in range(GT):
                    act.wait_ge(q_aP, t + 1)
                    if t > 1:
                        act.wait_ge(q_TT, t - 1)
                    s.activation(aPT[t % 2][:, :], bank[t % 2][:, :], ACT.Identity).then_inc(q_aPT, 1)
                    if t > 0:
                        own_sums(t - 1)
                own_sums(GT - 1)
                act.wait_ge(q_agT, 1)
                s.activation(TTs[:, :], bank[2][:, :], ACT.Identity).then_inc(q_TTs, 1)
                act.wait_ge(q_cols, 1)
                s.activation(cols[:, :], bank[4][:, 0:NROWS], ACT.Identity).then_inc(q_colsb, 1)
                act.wait_ge(q_v, 1)
                s.activation(v12[:, :, :], bank[4][:, 128:384].rearrange("p (a b) -> p a b", a=2),
                             ACT.Identity).then_inc(q_vsb, 1)
                act.wait_ge(q_cst2, 16 * NCST2)
                s.activation(msg_bias[:, :, :], msg_bias_f[:, :, :], ACT.Identity).then_inc(q_mb, 1)
                for gi in range(NG):
                    act.wait_ge(q_U, gi + 1)
                    s.activation(U[:, gi, :, :], U_BANK[gi][:, :].rearrange("p (t n) -> p t n", t=GT),
                                 ACT.Identity).then_inc(q_Us, 1)

                def split_weights(k):
                    act.wait_ge(q_wps, k + 2)
                    if k < 0:
                        s.activation(plainT[:, :, :], W_BANK[0][:, 0:256].rearrange("p (a b) -> p a b", a=2),
                                     ACT.Identity).then_inc(q_whi, 1)
                    else:
                        s.activation(w_hi[:, 4 * k:4 * k + 4, :], W_BANK[(k + 1) % 3][:, :].rearrange("p (a b) -> p a b", a=4),
                                     ACT.Identity).then_inc(q_whi, 1)

                def relu_hidden(gi):
                    act.wait_ge(q_colsb, 1)
                    for h in range(2):
                        act.wait_ge(q_h2, 2 * gi + h + 1)
                        if gi > 0:
                            act.wait_ge(q_S2, gi)
                        s.activation(hT[:, h, :], bank[h][:, :], ACT.Relu,
                                     bias=cols[:, HB + 2 * gi + h:HB + 2 * gi + h + 1]).then_inc(q_hT, 1)

                act.wait_ge(q_fs, 1)
                s.activation(fw[:, 2, :], fw[:, 1, :], ACT.Exp).then_inc(q_fe, 1)
                relu_hidden(0)
                for gi in range(NG):
                    act.wait_ge(q_S2, gi + 1)
                    if gi > 0:
                        act.wait_ge(q_o2, gi)
                    s.activation(S2, bank[2][:, :], ACT.Identity).then_inc(q_S2s, 1)
                    if gi + 1 < NG:
                        relu_hidden(gi + 1)
                    for k in WEIGHTS_AT[gi]:
                        split_weights(k)
                    act.wait_ge(q_ob, gi + 1)
                    act.wait_ge(q_wm, 1)
                    if gi > 0:
                        act.wait_ge(q_fu, gi)
                    s.activation(R2, o2b[gi % 2][:, :], ACT.Relu, scale=wm[:, gi:gi + 1]).then_inc(q_R2, 1)

            @block.vector
            def _(dve):
                v = nc.vector
                v.memset(f(Lf[64:96, :]), 1.0)
                v.memset(f(Rf[32:64, :]), 1.0)
                dve.wait_ge(q_zero, 2)
                for lo, hi in ((6, 12), (33, 34)):
                    v.memset(mk[:, 0, lo:hi], -1.0)
                for lo, hi in ((3, 6), (9, 12), (65, 66)):
                    v.memset(mk[:, 1, lo:hi], -1.0)
                for lo in (32, 64):
                    v.memset(sq_pick[0:3, lo:lo + 2], -0.5)
                for gi, spans in enumerate(GROUPS):
                    for j in range(4):
                        for lo, hi in spans:
                            last = v.memset(CM[SLOT * j:SLOT * (j + 1), gi, SLOT * j + lo:SLOT * j + hi], 1.0)
                last.then_inc(q_mask, 1)
                dve.wait_ge(q_mt, 1)
                v.tensor_tensor(GM[:, 0:4, :], bank[5][:, :].rearrange("p (a b) -> p a b", a=4), CM[:, 0:4, :], ALU.mult)
                v.tensor_tensor(GM[:, 4, :], bank[6][:, 0:128], CM[:, 4, :], ALU.mult)
                v.reduce_max(rm[:, 0:4], bank[5][:, :].rearrange("p (a b) -> p a b", a=4), X)
                v.reduce_max(rm[:, 4:5], bank[6][:, 0:128], X)
                v.tensor_copy(part_mask[:, :], bank[6][:, 128:384:128]).then_inc(q_gm, 1)
                dve.wait_ge(q_gm, 1)
                dve.wait_ge(q_adjP, 16 * 4)
                dve.wait_ge(q_zero, 2)
                dve.wait_ge(q_ident, 1)

                for j in range(4):
                    last = v.tensor_copy(A0[SLOT * j:SLOT * (j + 1), :, SLOT * j:SLOT * (j + 1)],
                                         adjP[SLOT * j:SLOT * (j + 1), :, 0:SLOT])
                last.then_inc(q_A0, 1)
                dve.wait_ge(q_A0, 1)
                v.tensor_tensor(A0[:, :, :], A0[:, :, :], bc(ident[:, :], GT), ALU.add).then_inc(q_A1, 1)
                dve.wait_ge(q_A1, 1)
                for t in range(GT):
                    v.tensor_tensor(A5[:, t], bc(A0[:, t, :], NG), GM[:, :, :], ALU.mult).then_inc(q_A5, 1)
                for t in range(GT):
                    dve.wait_ge(q_A5, t + 1)
                    last = v.reduce_sum(deg[:, 3, NG * t:NG * (t + 1)], A5[:, t], X)
                last.then_inc(q_dg, 1)
                dve.wait_ge(q_dg, 1)
                v.tensor_scalar(deg[:, 1, :], deg[:, 3, :], 0.0, None, ALU.is_equal).then_inc(q_dg1, 1)
                dve.wait_ge(q_dg1, 1)
                v.tensor_tensor(deg[:, 0, :], deg[:, 3, :], deg[:, 1, :], ALU.add).then_inc(q_dg2, 1)
                v.tensor_scalar(deg[:, 1, :], deg[:, 1, :], -1.0, 1.0, ALU.mult, ALU.add).then_inc(q_dgz, 1)
                dve.wait_ge(q_dgz, 1)
                dve.wait_ge(q_dgp, 1)
                v.tensor_tensor(deg[:, 3, :], deg[:, 2, :], deg[:, 1, :], ALU.mult).then_inc(q_dgi, 1)
                dve.wait_ge(q_dgi, 1)
                for t in range(GT):
                    v.tensor_tensor(A5[:, t], A5[:, t], spread(deg[:, 3, NG * t:NG * (t + 1)], 128), ALU.mult).then_inc(q_B, 1)

                def scale_columns(t):
                    dve.wait_ge(q_BT, t + 1)
                    v.tensor_tensor(nadjT[:, t, 0:4, :], bank[4 + t][:, :].rearrange("p (a b) -> p a b", a=4),
                                    spread(deg[:, 3, NG * t:NG * t + 4], 128), ALU.mult).then_inc(q_nT, 1)
                scale_columns(0)
                scale_columns(1)
                dve.wait_ge(q_o, 1)
                dve.wait_ge(q_xPb, 1)
                v.tensor_tensor(x1P[:, :, :], bank[3][:, :].rearrange("p (t d) -> p t d", t=GT), xP[:, :, :],
                                ALU.add).then_inc(q_yP, 1)
                dve.wait_ge(q_yP, 1)
                for t in range(GT):
                    last = v.bn_stats(stP[:, t, :], x1P[:, t, :])
                last.then_inc(q_stP, 1)
                dve.wait_ge(q_stP, 1)
                for t in range(GT):
                    last = v.bn_aggr(mvP[:, t, :], stP[:, t, :])
                last.then_inc(q_mvP, 1)
                dve.wait_ge(q_colsb, 1)
                for j in range(2):
                    last = v.tensor_scalar(abc[:, j, :], ones[:, :], cols[:, A1 + j:A1 + j + 1], None, ALU.mult)
                last.then_inc(q_abc, 1)
                scale_columns(2)
                scale_columns(3)
                v.tensor_tensor(nadjT[:, :, 4, :], bank[0][:, :].rearrange("p (a b) -> p a b", a=GT),
                                spread(deg[:, 3, 4:GT * NG:NG], 128), ALU.mult).then_inc(q_nT, 1)
                dve.wait_ge(q_rsP, 1)
                for t in range(GT):
                    last = v.tensor_scalar(x1P[:, t, :], x1P[:, t, :], mvP[:, t, 0:1], rsP[:, t:t + 1], ALU.subtract,
                                           ALU.mult)
                last.then_inc(q_x1P, 1)
                dve.wait_ge(q_cst2, 16 * NCST2)
                v.reduce_max(fmx[:, 0:1], fw[:, 0, :], X).then_inc(q_fm, 1)
                dve.wait_ge(q_fm, 1)
                v.tensor_scalar(fw[:, 1, :], fw[:, 0, :], fmx[:, 0:1], None, ALU.subtract).then_inc(q_fs, 1)
                dve.wait_ge(q_bnr, 1)
                v.tensor_tensor(bn_scale[:, :], bn_scale[:, :], cols[:, G1:G2 + 1:G2 - G1], ALU.mult).then_inc(q_bns, 1)
                dve.wait_ge(q_bns, 1)
                v.tensor_tensor(bn_bias[:, :], cols[:, M1:M2 + 1:M2 - M1], bn_scale[:, :], ALU.mult).then_inc(q_bns, 1)
                dve.wait_ge(q_bns, 2)
                v.tensor_tensor(bn_bias[:, :], cols[:, BB1:BB2 + 1:BB2 - BB1], bn_bias[:, :], ALU.subtract)
                dve.wait_ge(q_wt, 16 * 10)
                v.tensor_scalar(nat_c1[:, :], nat_c1[:, :], bn_scale[:, 0:1], None, ALU.mult)
                v.tensor_scalar(nat_c2[:, :, :], nat_c2[:, :, :], bn_scale[:, 1:2], None, ALU.mult).then_inc(q_sc, 1)
                dve.wait_ge(q_sc, 1)
                v.tensor_tensor(nat_sum[:, :, :], nat_c2[:, :, 2:TAPS:2], nat_c2[:, :, 1:TAPS:2], ALU.add).then_inc(q_sum, 1)
                dve.wait_ge(q_fe, 1)
                v.reduce_sum(fmx[:, 1:2], fw[:, 2, :], X).then_inc(q_fd, 1)
                dve.wait_ge(q_fd, 1)
                v.reciprocal(fmx[:, 2:3], fmx[:, 1:2]).then_inc(q_fr, 1)
                dve.wait_ge(q_fr, 1)
                v.scalar_tensor_tensor(wm[:, :], fw[:, 2, :], fmx[:, 2:3], rm[:, :], ALU.mult, ALU.mult).then_inc(q_wm, 1)
                v.tensor_tensor(gate_bias[:, 0:2], cols[:, BIH:BIH + 2], cols[:, BHH:BHH + 2], ALU.add).then_inc(q_gb, 1)
                dve.wait_ge(q_gb, 1)
                v.tensor_scalar(gate_bias[:, 0:2], gate_bias[:, 0:2], 0.5, None, ALU.mult)
                v.tensor_scalar(gate_bias[:, 2:3], cols[:, BHH + 2:BHH + 3], 0.5, None, ALU.mult)
                dve.wait_ge(q_vsb, 1)
                v.tensor_copy(c12[:, :], bank[4][:, 384:386]).then_inc(q_c12, 1)
                dve.wait_ge(q_c12, 1)
                v.tensor_tensor(c12[:, 0:1], c12[:, 0:1], ab_col[:, :], ALU.add)
                dve.wait_ge(q_mb, 1)
                v.tensor_tensor(mb_rest[:, :, :], msg_bias_f[:, :, :], f(msg_bias[:, :, :]), ALU.subtract).then_inc(q_mb, 1)
                dve.wait_ge(q_mb, 2)
                v.tensor_copy(msg_bias[32:64, :, :], mb_rest[32:64, :, :]).then_inc(q_mb, 1)
                fusedF = fusedP[:, :, :].rearrange("p t d -> p (t d)")
                for gi in range(NG):
                    for k in WEIGHTS_AT[gi]:
                        if k >= 0:
                            dve.wait_ge(q_whi, k + 2)
                            v.tensor_tensor(w_lo[:, 4 * k:4 * k + 4, :],
                                            W_BANK[(k + 1) % 3][:, :].rearrange("p (a b) -> p a b", a=4),
                                            f(w_hi[:, 4 * k:4 * k + 4, :]), ALU.subtract).then_inc(q_wlo, 1)
                    dve.wait_ge(q_o2, gi + 1)
                    if gi > 1:
                        dve.wait_ge(q_R2, gi - 1)
                    v.tensor_tensor(o2b[gi % 2][:, :].rearrange("p (t d) -> p t d", t=GT),
                                    bank[3][:, :].rearrange("p (t d) -> p t d", t=GT), bc(hb2[:, gi, :], GT),
                                    ALU.add).then_inc(q_ob, 1)
                    dve.wait_ge(q_R2, gi + 1)
                    if gi == 0:
                        v.tensor_copy(fusedF, R2).then_inc(q_fu, 1)
                    else:
                        dve.wait_ge(q_fu, gi)
                        v.tensor_tensor(fusedF, fusedF, R2, ALU.add).then_inc(q_fu, 1)

            @block.tensor
            def _(pe):
                t_ = nc.tensor
                pe.wait_ge(q_ident, 1)
                pe.wait_ge(q_mask, 1)
                for gi in range(NG):
                    t_.transpose(bank[5 + gi // 4][:, ch(gi % 4)], CM[:, gi, :], ident[:, :])
                t_.transpose(bank[6][:, ch(1)], mk[:, 0, :], ident[:, :])
                t_.transpose(bank[6][:, ch(2)], mk[:, 1, :], ident[:, :]).then_inc(q_mt, 1)
                pe.wait_ge(q_adjP, 16 * 4)

                def transpose_rows(t):
                    if t > 1:
                        pe.wait_ge(q_aPT, t - 1)
                    for mc in range(NC):
                        last = t_.transpose(bank[t % 2][:, ch(mc)], adjP[:, t, ch(mc)], ident[:, :])
                    last.then_inc(q_aP, 1)

                def block_rows(t):
                    pe.wait_ge(q_B, t + 1)
                    for gi in range(NG):
                        o = bank[4 + t][:, ch(gi)] if gi < 4 else bank[0][:, ch(t)]
                        last = t_.transpose(o, A5[:, t, gi, :], ident[:, :])
                    last.then_inc(q_BT, 1)

                transpose_rows(0)
                transpose_rows(1)
                for t in range(GT):
                    pe.wait_ge(q_aPT, t + 1)
                    pe.wait_ge(q_xr[t], 16)
                    if t > 1:
                        pe.wait_ge(q_ag, t - 1)
                    for mc in range(NC):
                        last = t_.matmul(bank[2 + t % 2][:, :], aPT[t % 2][:, ch(mc)], x_all[:, 4 * t:4 * t + 4, mc, :],
                                         start=(mc == 0), stop=(mc == NC - 1))
                    last.then_inc(q_TT, 1)
                    if t + 2 < GT:
                        transpose_rows(t + 2)
                pe.wait_ge(q_gm, 1)
                block_rows(0)
                block_rows(1)
                pe.wait_ge(q_ag, GT)
                for t in range(GT):
                    last = t_.transpose(bank[2][:, ch(t)], aggP[:, ch(t)], ident[:, :])
                last.then_inc(q_agT, 1)
                block_rows(2)
                pe.wait_ge(q_TTs, 1)
                pe.wait_ge(q_cst, 16 * 2)
                for t in range(GT):
                    last = t_.matmul(bank[3][:, ch(t)], TTs[:, ch(t)], w0[:, :], start=True, stop=True)
                last.then_inc(q_o, 1)
                block_rows(3)
                pe.wait_ge(q_row, 16 * 13)
                pe.wait_ge(q_nT, 1)
                t_.transpose(bank[4][:, 0:NROWS], vrows[0:NROWS, :], ident[0:NROWS, 0:NROWS]).then_inc(q_cols, 1)
                pe.wait_ge(q_abc, 1)
                pe.wait_ge(q_wt, 16 * 10)
                for j in range(2):
                    t_.matmul(bank[4][:, ch(1 + j)], abc[:, j, :], nat_ww[:, 0, :], start=True, stop=True)
                    last = t_.matmul(bank[4][:, 384 + j:385 + j], abc[:, j, :], cols[:, WB:WB + 1],
                                     start=True, stop=True)
                last.then_inc(q_v, 1)
                pe.wait_ge(q_x1P, 1)
                pe.wait_ge(q_nT, GT + 1)
                for gi in range(NG):
                    for t in range(GT):
                        last = t_.matmul(U_BANK[gi][:, ch(t)], x1P[:, t, :], nadjT[:, t, gi, :], start=True, stop=True)
                    last.then_inc(q_U, 1)
                pe.wait_ge(q_h, 16 * 2)

                def hidden(gi):
                    pe.wait_ge(q_Us, gi + 1)
                    for h in range(2):
                        if gi > 0:
                            pe.wait_ge(q_hT, 2 * gi - 1 + h)
                        t_.matmul(bank[h][:, :], hw1[:, gi, ch(h)], U[:, gi, :, :].rearrange("p t n -> p (t n)"),
                                  start=True, stop=True).then_inc(q_h2, 1)

                def transpose_weights(k):
                    for i, w in enumerate(blocks[0] if k < 0 else blocks[1][4 * k:4 * k + 4]):
                        last = t_.transpose(W_BANK[(k + 1) % 3][:, ch(i)], w, ident[:, :])
                    last.then_inc(q_wps, 1)

                hidden(0)
                for gi in range(NG):
                    pe.wait_ge(q_hT, 2 * gi + 2)
                    if gi > 0:
                        pe.wait_ge(q_S2s, gi)
                    for t in range(GT):
                        for h in range(2):
                            last = t_.matmul(bank[2][:, ch(t)], hT[:, h, ch(t)], hw2[:, gi, h, :],
                                             start=(h == 0), stop=(h == 1))
                    last.then_inc(q_S2, 1)
                    if gi + 1 < NG:
                        hidden(gi + 1)
                    for k in WEIGHTS_AT[gi]:
                        if k >= 0:
                            pe.wait_ge(q_sum, 1)
                            if k >= 2:
                                pe.wait_ge(q_whi, k - 1)
                            if k >= 3:
                                pe.wait_ge(q_wlo, k - 2)
                        if k < 0:
                            pe.wait_ge(q_Us, NG)
                        transpose_weights(k)
                    pe.wait_ge(q_S2s, gi + 1)
                    pe.wait_ge(q_Us, 2)
                    pe.wait_ge(q_cst2, 16 * NCST2)
                    if gi > 0:
                        pe.wait_ge(q_ob, gi)
                    for t in range(GT):
                        last = t_.matmul(bank[3][:, ch(t)], nadjT[:, t, gi, :], S2[:, ch(t)], start=True, stop=True)
                    last.then_inc(q_o2, 1)
                pe.wait_ge(q_mb, 3)
                pe.wait_ge(q_R2, NG)

        before_loop.close()
        aT_hi = sb("aT_hi", [128, NC, N], f32r)
        aT_lo = sb("aT_lo", [128, NC, N], f32r)
        x_hi = sb("x_hi", [128, NC, D], f32r)
        x_lo = sb("x_lo", [128, NC, D], f32r)
        x1 = sb("x1", [128, NC, D])
        x2 = sb("x2", [128, NC, D])
        y3 = sb("y3", [128, NC, D])
        agg_sb = sb("agg_sb", [128, N])
        ef = sb("ef", [128, 2, NC])
        pef = sb("pef", [128, 2, NC])
        pf2 = sb("pf2", [128, NC, 2], f32r)
        den_sb = sb("den_sb", [2, N])
        dq = sb("dq", [128, 3, NC])
        x3 = sb("x3", [128, NC, D])
        st = [sb(f"st{i}", [128, NC, 6]) for i in range(4)]
        mv = [sb(f"mv{i}", [128, NC, 2]) for i in range(4)]
        ve = [sb(f"ve{i}", [128, NC]) for i in range(4)]
        rs = [sb(f"rs{i}", [128, NC]) for i in range(4)]
        nmr = sb("nmr", [128, NC])
        nms = sb("nms", [128, NC])
        x3T = [sb(f"x3T{i}", [128, N]) for i in range(2)]
        x3T_hi = sb("x3T_hi", [128, N], f32r)
        x3T_lo = sb("x3T_lo", [128, N], f32r)
        c1_hi = sb("c1_hi", [128, 2, PH], f32r)
        c1_lo = sb("c1_lo", [128, 2, PH], f32r)
        cs = sb("cs", [128, PH])
        cs_hi = sb("cs_hi", [128, PH], f32r)
        cs_lo = sb("cs_lo", [128, PH], f32r)
        msg_hi = sb("msg_hi", [128, N], f32r)
        msg_lo = sb("msg_lo", [128, N], f32r)
        sC = sb("sC", [128, N])
        sH = sb("sH", [96, N], f32r)
        xc_hi = sb("xc_hi", [128, N], f32r)
        xc_lo = sb("xc_lo", [128, N], f32r)
        nmp_hi = sb("nmp_hi", [128, N], f32r)
        nmp_lo = sb("nmp_lo", [128, N], f32r)
        P_hi = sb("P_hi", [128, NC, N], f32r)
        P_lo = sb("P_lo", [128, NC, N], f32r)
        y_out = sb("y_out", [128, NC, D])
        tv = sb("tv", [128, 2, NC, D])
        aT = [sb(f"aT{i}", [128, NC, N]) for i in range(2)]
        E = sb("E", [128, 2, N])
        P = sb("P", [128, 2, N])
        P0s = sb("P0s", [128, HALF])
        conv, gh, th_r, th_z, nn, gd, ga = [sb(name, [128, N])[:, :] for name in (
            "conv", "gh", "th_r", "th_z", "nn", "gd", "ga")]

        nc.clear_and_free_semaphores(before)
        nc.all_engine_barrier()

        pe_aT, ac_aThi, ac_aT, aTlo = sems("pe_aT", NC), sems("ac_aThi", NC), sems("ac_aT", NC), sems("aTlo", NC)
        ac_xhi, dv_xlo, po_xb = sem("ac_xhi"), sem("dv_xlo"), sem("po_xb")
        pe_agg1, ac_agg1, pe_out0, dv_y1 = sem("pe_agg1"), sem("ac_agg1"), sem("pe_out0"), sem("dv_y1")
        dv_st, dv_mv, po_ve, po_rs = sems("dv_st", 4), sems("dv_mv", 4), sems("po_ve", 4), sems("po_rs", 4)
        dv_x1, dv_fused, dv_x2, po_x2b, po_v = sem("dv_x1"), sem("dv_fused"), sem("dv_x2"), sem("po_x2b"), sem("po_v")
        dv_f, dv_e, ac_pf, ac_pe, dv_xshi, dv_xslo, dv_pf = [sem(n) for n in (
            "dv_f", "dv_e", "ac_pf", "ac_pe", "dv_xshi", "dv_xslo", "dv_pf")]
        pe_agg2, pe_den, ac_agg2, ac_den = sem("pe_agg2"), sem("pe_den"), sem("ac_agg2"), sem("ac_den")
        pe_dcol, pe_out2, dv_dq, dv_y3, dv_x3 = sem("pe_dcol"), sem("pe_out2"), sem("dv_dq"), sem("dv_y3"), sem("dv_x3")
        pe_x3T, ac_x3Thi, ac_x3T, dv_x3Tlo = sem("pe_x3T"), sem("ac_x3Thi"), sem("ac_x3T"), sem("dv_x3Tlo")
        pe_s, pe_c1, pe_hn, pe_msg, pe_sq = sem("pe_s"), sem("pe_c1"), sem("pe_hn"), sem("pe_msg"), sem("pe_sq")
        ac_s2, ac_c1, ac_gh, ac_msghi, ac_C, ac_H = [sem(n) for n in (
            "ac_s2", "ac_c1", "ac_gh", "ac_msghi", "ac_C", "ac_H")]
        dv_c1, po_cs, dv_csp, dv_msglo, po_L, dv_R = [sem(n) for n in (
            "dv_c1", "po_cs", "dv_csp", "dv_msglo", "po_L", "dv_R")]
        pe_D, ac_E, dv_P, ac_Phi, po_Plo = [sems(n, NC) for n in ("pe_D", "ac_E", "dv_P", "ac_Phi", "po_Plo")]
        pe_P1, pe_P0, pe_Q, ac_P0s, dv_ab, dv_conv = [sem(n) for n in (
            "pe_P1", "pe_P0", "pe_Q", "ac_P0s", "dv_ab", "dv_conv")]
        ac_xchi, dv_xclo, pe_N, ac_nmphi, dv_nmplo = [sem(n) for n in (
            "ac_xchi", "dv_xclo", "pe_N", "ac_nmphi", "dv_nmplo")]
        pe_z, pe_r, pe_gn, ac_thz, ac_thr, ac_nn = [sem(n) for n in ("pe_z", "pe_r", "pe_gn", "ac_thz", "ac_thr", "ac_nn")]
        dv_t, po_g, po_y4, pe_yT = [sem(n) for n in ("dv_t", "po_g", "po_y4", "pe_yT")]
        po_nms, dv_c1h, ac_csh, dv_q0, dv_q1, dv_q, dv_pfh, dv_t0, dv_m, dv_d, dv_v = [sem(n) for n in (
            "po_nms", "dv_c1h", "ac_csh", "dv_q0", "dv_q1", "dv_q", "dv_pfh", "dv_t0", "dv_m", "dv_d", "dv_v")]
        ac_L, ac_half = sem("ac_L"), sem("ac_half")
        po_nm, ac_out, o_out = sem("po_nm"), sem("ac_out"), sem("o_out")

        block = ctx.enter_context(nc.Block())

        @block.sync
        def _(sp):
            sp.sem_inc(o_out, 16)
            sp.wait_ge(fused_out, 16 * 4)
            sp.dma_start(fused_in[0][:, :], fused_dram[0, 0:NODES]).then_inc(f_in[0], 16)
            def turn(V, dma, par, graph, has, outs):
                if has(2):
                    wait(sp, ac_xhi, V(1))
                    wait(sp, dv_xlo, V(1))
                    wait(sp, po_xb, V(1))
                    sp.dma_start(x_nat[par][:, :, :], x_v[bass.ds(graph(2), 1)].rearrange("a p c d -> p (a c) d")
                                 ).then_inc(x_in[par], 16)
                    wait(sp, pe_aT[NC - 1], V(1))
                    sp.dma_start(adj_nat[par][:, :, :], adj_v[bass.ds(graph(2), 1)].rearrange("a p c m -> p (a c) m")
                                 ).then_inc(adj_in[par], 16)
                    wait(sp, dv_fused, V(1))
                    sp.dma_start(fused_in[par][:, :],
                                 fused_dram[bass.ds(graph(2), 1), 0:NODES].rearrange("a p d -> p (a d)")
                                 ).then_inc(f_in[par], 16)
                if has(-1):
                    sp.wait_ge(ac_out, V(0))
                    sp.dma_start(out_v[bass.ds(graph(-1), 1)].rearrange("a p c d -> p (a c) d"),
                                 y_out[:, :, :]).then_inc(o_out, 16)

            over_graphs(sp, turn, -1)
            sp.wait_ge(o_out, 16 * (B + 1))

        @block.gpsimd
        def _(pool):
            g = nc.gpsimd
            def inverse_root(V, k, i):
                hold(pool, dv_mv[i], V(k))
                g.tensor_scalar(ve[i][:, :], mv[i][:, :, 1], EPS, None, ALU.add).then_inc(po_ve[i], 1)
                wait(pool, po_ve[i], V(k))
                g.tensor_tensor(rs[i][:, :], ve[i][:, :], neg_half[:, 0:NC], ALU.pow).then_inc(po_rs[i], 1)

            def turn(V, dma, par, graph, has, outs):
                cur, nxt, prev, new = has(0), has(1), has(-1), has(2)

                def split_rest(mc):
                    wait(pool, ac_aT[mc], V(3))
                    wait(pool, pe_agg2, V(2))
                    g.tensor_tensor(aT_lo[:, mc, :], aT[par][:, mc, :], f(aT_hi[:, mc, :]),
                                    ALU.subtract).then_inc(aTlo[mc], 1)

                def rest(mc):
                    wait(pool, ac_Phi[mc], V(1))
                    wait(pool, pe_N, V(0))
                    g.tensor_tensor(P_lo[:, mc, :], P[:, mc % 2, :], f(P_hi[:, mc, :]),
                                    ALU.subtract).then_inc(po_Plo[mc], 1)

                if nxt:
                    wait(pool, x_in[1 - par], dma(1))
                    wait(pool, dv_x2, V(1))
                    g.tensor_tensor(x1[:, :, :], x_nat[1 - par][:, :, :], bc(bias0[:, :], NC),
                                    ALU.add).then_inc(po_xb, 1)
                if cur:
                    wait(pool, ac_c1, V(1))
                    wait(pool, pe_Q, V(0))
                    g.tensor_tensor(cs[:, :], c1[:, 0, :], c1[:, 1, :], ALU.add).then_inc(po_cs, 1)
                if nxt:
                    inverse_root(V, 2, 0)
                if prev:
                    wait(pool, ac_nn, V(0))
                    g.tensor_tensor(ga, x3T[1 - par][:, :], nn, ALU.add).then_inc(po_g, 1)
                if cur:
                    wait(pool, ac_L, V(1))
                    g.tensor_tensor(Lf[0:64, :], f(Lf[0:64, :]), sC[0:64, :], ALU.add).then_inc(po_L, 1)
                if nxt:
                    inverse_root(V, 2, 1)
                if prev:
                    wait(pool, ac_half, V(0))
                    wait(pool, po_g, V(0))
                    g.tensor_tensor(ga, gd, ga, ALU.add).then_inc(po_y4, 1)
                if nxt:
                    wait(pool, dv_x2, V(2))
                    wait(pool, dv_e, V(1))
                    g.tensor_tensor(tv[:, 0], x2[:, :, :], bc(v12[:, 0, :], NC), ALU.mult).then_inc(po_v, 1)
                if cur:
                    rest(0)
                    rest(1)
                if prev:
                    inverse_root(V, 0, 3)
                    wait(pool, po_rs[3], V(0))
                    g.tensor_tensor(nms[:, :], mv[3][:, :, 0], rs[3][:, :], ALU.mult).then_inc(po_nms, 1)
                    hold(pool, po_nms, V(0))
                    g.tensor_scalar(nmr[:, :], nms[:, :], -1.0, None, ALU.mult).then_inc(po_nm, 1)
                if cur:
                    rest(2)
                if nxt:
                    wait(pool, dv_x3, V(1))
                    g.tensor_tensor(y3[:, :, :], x2[:, :, :], bc(wb_bc[:, :], NC), ALU.add).then_inc(po_x2b, 1)
                if cur:
                    rest(3)
                if nxt:
                    inverse_root(V, 2, 2)
                if new:
                    split_rest(1)
                    split_rest(3)
            over_graphs(pool, turn)

        @block.scalar
        def _(act):
            s = nc.scalar
            def turn(V, dma, par, graph, has, outs):
                cur, nxt, prev, new = has(0), has(1), has(-1), has(2)

                def split_adjacency(mc):
                    wait(act, pe_aT[mc], V(3))
                    wait(act, pe_agg2, V(2))
                    s.activation(aT_hi[:, mc, :], AT_BANK[mc % 2][:, :], ACT.Identity).then_inc(ac_aThi[mc], 1)
                    wait(act, dv_P[NC - 1], V(1))
                    s.activation(aT[par][:, mc, :], AT_BANK[mc % 2][:, :], ACT.Identity).then_inc(ac_aT[mc], 1)

                def exponential(mc):
                    wait(act, pe_D[mc], V(1))
                    wait(act, dv_P[(mc + 2) % NC], V(0) if mc < 2 else V(1))
                    s.activation(E[:, mc % 2, :], AT_BANK[mc % 2][:, :], ACT.Exp, scale=2.0).then_inc(ac_E[mc], 1)

                def rounded(mc):
                    wait(act, dv_P[mc], V(1))
                    wait(act, pe_N, V(0))
                    s.activation(P_hi[:, mc, :], P[:, mc % 2, :], ACT.Identity).then_inc(ac_Phi[mc], 1)

                if cur:
                    wait(act, pe_x3T, V(1))
                    wait(act, pe_r, V(0))
                    s.activation(x3T_hi[:, :], X_BANK[:, :], ACT.Identity).then_inc(ac_x3Thi, 1)
                    s.activation(x3T[par][:, :], X_BANK[:, :], ACT.Identity).then_inc(ac_x3T, 1)
                if nxt:
                    wait(act, pe_agg1, V(2))
                    wait(act, pe_out2, V(1))
                    s.activation(agg_sb[:, :], AG_BANK[:, :], ACT.Identity).then_inc(ac_agg1, 1)
                if cur:
                    wait(act, pe_c1, V(1))
                    wait(act, po_cs, V(0))
                    wait(act, dv_c1, V(0))
                    s.activation(c1[:, :, HP:HP + HALF], CV_BANK[:, :].rearrange("p (i r) -> p r i", r=2), ACT.Relu,
                                 bias=bn_bias[:, 0:1]).then_inc(ac_c1, 1)
                if prev:
                    wait(act, dv_t, V(0))
                    s.activation(nn, gh, ACT.Tanh, bias=cols[:, BIH + 2:BIH + 3]).then_inc(ac_nn, 1)
                if cur:
                    wait(act, pe_s, V(1))
                    wait(act, dv_R, V(0))
                    s.activation(sC[0:32, :], SQ_BANK[0:32, :], ACT.Square, bias=se_bias[0:32, :]).then_inc(ac_s2, 1)
                    wait(act, po_cs, V(1))
                    wait(act, pe_Q, V(0))
                    s.activation(cs_hi[:, :], cs[:, :], ACT.Identity).then_inc(ac_csh, 1)
                    wait(act, pe_msg, V(1))
                    wait(act, pe_N, V(0))
                    s.activation(msg_hi[:, :], MS_BANK[:, :], ACT.Relu).then_inc(ac_msghi, 1)
                    wait(act, pe_sq, V(1))
                    s.activation(sC[0:96, :], SQ_BANK[0:96, :], ACT.Identity, bias=se_bias[0:96, :]).then_inc(ac_C, 1)
                    wait(act, ac_C, V(1))
                    s.activation(sH[:, :], sC[0:96, :], ACT.Identity).then_inc(ac_H, 1)
                    wait(act, ac_H, V(1))
                    wait(act, pe_D[NC - 1], V(0))
                    s.activation(Lf[0:64, :], f(sH[0:64, :]), ACT.Identity, scale=part_mask[0:64, 0:1]).then_inc(ac_L, 1)
                if prev:
                    wait(act, dv_m, V(0))
                    s.activation(gd, gd, ACT.Identity, scale=0.5).then_inc(ac_half, 1)
                if cur:
                    wait(act, pe_hn, V(1))
                    wait(act, ac_nn, V(0))
                    s.activation(gh, HN_BANK[:, :], ACT.Identity, bias=gate_bias[:, 2:3], scale=0.5).then_inc(ac_gh, 1)
                if cur:
                    exponential(0)
                    exponential(1)
                if nxt:
                    wait(act, dv_f, V(2))
                    wait(act, dv_pf, V(1))
                    s.activation(pef[:, 1, :], ef[:, 1, :], ACT.Exp, bias=c12[:, 1:2]).then_inc(ac_pf, 1)
                if cur:
                    rounded(0)
                    rounded(1)
                    exponential(2)
                    exponential(3)
                if cur:
                    wait(act, pe_Q, V(1))
                    wait(act, dv_conv, V(0))
                    s.activation(P0s[:, :], CV_BANK[:, 0:HALF], ACT.Identity).then_inc(ac_P0s, 1)
                if nxt:
                    wait(act, pe_den, V(2))
                    wait(act, pe_dcol, V(1))
                    s.activation(den_sb[:, :], SQ_BANK[0:2, :], ACT.Identity).then_inc(ac_den, 1)
                    wait(act, dv_e, V(2))
                    wait(act, dv_dq, V(1))
                    s.activation(pef[:, 0, :], ef[:, 0, :], ACT.Exp, bias=c12[:, 0:1]).then_inc(ac_pe, 1)
                if cur:
                    rounded(2)
                if nxt:
                    wait(act, pe_agg2, V(2))
                    s.activation(agg_sb[:, :], AG_BANK[:, :], ACT.Identity).then_inc(ac_agg2, 1)
                if prev:
                    hold(act, po_nm, V(0))
                    hold(act, o_out, outs)
                    for c in range(NC):
                        last = s.activation(y_out[:, c, :], X_BANK[:, ch(c)], ACT.Identity, bias=nmr[:, c:c + 1],
                                            scale=rs[3][:, c:c + 1])
                    last.then_inc(ac_out, 1)
                if cur:
                    rounded(3)
                if cur:
                    wait(act, dv_conv, V(1))
                    wait(act, pe_gn, V(0))
                    s.activation(xc_hi[:, :], conv, ACT.Relu).then_inc(ac_xchi, 1)
                if new:
                    wait(act, x_in[par], dma(2))
                    s.activation(x_hi[:, :, :], x_nat[par][:, :, :], ACT.Identity).then_inc(ac_xhi, 1)
                if cur:
                    wait(act, pe_N, V(1))
                    s.activation(nmp_hi[:, :], X_BANK[:, :], ACT.Identity).then_inc(ac_nmphi, 1)
                if new:
                    split_adjacency(0)
                    split_adjacency(1)
                if cur:
                    wait(act, pe_z, V(1))
                    wait(act, po_y4, V(0))
                    s.activation(th_z, MS_BANK[:, :], ACT.Tanh, bias=gate_bias[:, 1:2], scale=0.5).then_inc(ac_thz, 1)
                if new:
                    split_adjacency(2)
                    split_adjacency(3)
                if cur:
                    wait(act, pe_r, V(1))
                    s.activation(th_r, CV_BANK[:, :], ACT.Tanh, bias=gate_bias[:, 0:1], scale=0.5).then_inc(ac_thr, 1)

            over_graphs(act, turn)

        @block.vector
        def _(dve):
            v = nc.vector
            def statistics(i, V, k, src, meanwhile=None):
                for c in range(NC):
                    last = v.bn_stats(st[i][:, c, :], src(c))
                last.then_inc(dv_st[i], 1)
                if meanwhile:
                    meanwhile()
                hold(dve, dv_st[i], V(k))
                for c in range(NC):
                    last = v.bn_aggr(mv[i][:, c, :], st[i][:, c, :])
                last.then_inc(dv_mv[i], 1)

            def normalise(i, V, k, dst, src, done):
                hold(dve, po_rs[i], V(k))
                for c in range(NC):
                    last = v.tensor_scalar(dst[:, c, :], src[:, c, :], mv[i][:, c, 0:1], rs[i][:, c:c + 1],
                                           ALU.subtract, ALU.mult)
                last.then_inc(done, 1)

            def turn(V, dma, par, graph, has, outs):
                cur, nxt, prev, new = has(0), has(1), has(-1), has(2)

                def split_rest(mc):
                    wait(dve, ac_aT[mc], V(3))
                    wait(dve, pe_agg2, V(2))
                    v.tensor_tensor(aT_lo[:, mc, :], aT[par][:, mc, :], f(aT_hi[:, mc, :]),
                                    ALU.subtract).then_inc(aTlo[mc], 1)

                def weigh(mc):
                    wait(dve, ac_E[mc], V(1))
                    wait(dve, ac_aT[mc], V(1))
                    k = 0 if mc < 2 else 1
                    wait(dve, ac_Phi[(mc + 2) % NC], V(k))
                    wait(dve, po_Plo[(mc + 2) % NC], V(k))
                    v.tensor_tensor(P[:, mc % 2, :], E[:, mc % 2, :], aT[par][:, mc, :], ALU.mult).then_inc(dv_P[mc], 1)

                if cur:
                    wait(dve, ac_x3T, V(1))
                    wait(dve, pe_r, V(0))
                    v.tensor_tensor(x3T_lo[:, :], x3T[par][:, :], f(x3T_hi[:, :]), ALU.subtract).then_inc(dv_x3Tlo, 1)
                if prev:
                    wait(dve, ac_thr, V(0))
                    wait(dve, ac_gh, V(0))
                    v.scalar_tensor_tensor(gh, th_r, 1.0, gh, ALU.add, ALU.mult).then_inc(dv_t0, 1)
                    wait(dve, dv_t0, V(0))
                    wait(dve, pe_gn, V(0))
                    v.tensor_tensor(gh, SQ_BANK[:, :], gh, ALU.add).then_inc(dv_t, 1)

                def round_c1():
                    wait(dve, ac_c1, V(1))
                    wait(dve, pe_Q, V(0))
                    wait(dve, pe_P1, V(0))
                    v.tensor_copy(c1_hi[:, :, :], c1[:, :, :]).then_inc(dv_c1h, 1)

                if nxt:
                    wait(dve, pe_out0, V(2))
                    wait(dve, po_xb, V(2))
                    v.tensor_tensor(x1[:, :, :], AG_BANK[:, :].rearrange("p (c d) -> p c d", c=NC), x1[:, :, :],
                                    ALU.add).then_inc(dv_y1, 1)
                    hold(dve, dv_y1, V(2))
                    statistics(0, V, 2, lambda c: x1[:, c, :], round_c1 if cur else None)
                elif cur:
                    round_c1()
                if prev:
                    wait(dve, ac_nn, V(0))
                    v.tensor_tensor(gd, x3T[1 - par][:, :], nn, ALU.subtract).then_inc(dv_d, 1)
                if cur:
                    wait(dve, dv_c1h, V(1))
                    v.tensor_tensor(c1_lo[:, :, :], c1[:, :, :], f(c1_hi[:, :, :]), ALU.subtract).then_inc(dv_c1, 1)
                if prev:
                    wait(dve, dv_d, V(0))
                    wait(dve, ac_thz, V(0))
                    v.scalar_tensor_tensor(gd, th_z, 1.0, gd, ALU.add, ALU.mult).then_inc(dv_m, 1)
                if nxt:
                    normalise(0, V, 2, x1, x1, dv_x1)
                if cur:
                    wait(dve, ac_csh, V(1))
                    v.tensor_tensor(cs_lo[:, :], cs[:, :], f(cs_hi[:, :]), ALU.subtract).then_inc(dv_csp, 1)
                if nxt:
                    wait(dve, dv_x1, V(2))
                    wait(dve, f_in[1 - par], dma(1))
                    v.tensor_tensor(x1[0:NODES, 0, :], x1[0:NODES, 0, :], fused_in[1 - par][:, :],
                                    ALU.add).then_inc(dv_fused, 1)
                    hold(dve, dv_fused, V(2))
                    statistics(1, V, 2, lambda c: x1[:, c, :])
                if cur:
                    wait(dve, ac_H, V(1))
                    wait(dve, pe_D[NC - 1], V(0))
                    v.scalar_tensor_tensor(Rf[0:32, :], f(sH[0:32, :]), part_mask[0:32, 1:2], sC[0:32, :],
                                           ALU.mult, ALU.add)
                    v.scalar_tensor_tensor(Rf[64:96, :], f(sH[64:96, :]), part_mask[64:96, 1:2], sC[64:96, :],
                                           ALU.mult, ALU.add).then_inc(dv_R, 1)
                if cur:
                    wait(dve, pe_msg, V(1))
                    wait(dve, ac_msghi, V(1))
                    wait(dve, pe_N, V(0))
                    v.scalar_tensor_tensor(msg_lo[:, :], MS_BANK[:, :], 0.0, f(msg_hi[:, :]), ALU.max,
                                           ALU.subtract).then_inc(dv_msglo, 1)
                if nxt:
                    hold(dve, po_x2b, V(1))
                    normalise(1, V, 2, x2, x1, dv_x2)
                if nxt:
                    wait(dve, dv_x2, V(2))
                    v.tensor_tensor(tv[:, 1], x2[:, :, :], bc(v12[:, 1, :], NC), ALU.mult).then_inc(dv_v, 1)
                if nxt:
                    hold(dve, dv_v, V(2))
                    hold(dve, ac_pf, V(1))
                    v.reduce_sum(ef[:, 1, :], tv[:, 1], X).then_inc(dv_f, 1)
                if cur:
                    weigh(0)
                if nxt:
                    hold(dve, ac_pf, V(2))
                    hold(dve, pe_den, V(1))
                    v.tensor_copy(pf2[:, :, 0], pef[:, 1, :]).then_inc(dv_pfh, 1)
                    hold(dve, pe_agg1, V(2))
                    v.tensor_tensor(x_hi[:, :, :], x2[:, :, :], spread(pef[:, 1, :], D), ALU.mult).then_inc(dv_xshi, 1)
                    wait(dve, dv_pfh, V(2))
                    v.tensor_tensor(pf2[:, :, 1], pef[:, 1, :], f(pf2[:, :, 0]), ALU.subtract).then_inc(dv_pf, 1)
                if cur:
                    weigh(1)
                if nxt:
                    wait(dve, dv_xshi, V(2))
                    for c in range(NC):
                        last = v.scalar_tensor_tensor(x_lo[:, c, :], x2[:, c, :], pef[:, 1, c:c + 1], f(x_hi[:, c, :]),
                                                      ALU.mult, ALU.subtract)
                    last.then_inc(dv_xslo, 1)
                if prev:
                    hold(dve, pe_yT, V(0))
                    statistics(3, V, 0, lambda c: X_BANK[:, ch(c)])
                if nxt:
                    hold(dve, po_v, V(2))
                    hold(dve, ac_pe, V(1))
                    v.reduce_sum(ef[:, 0, :], tv[:, 0], X).then_inc(dv_e, 1)
                if cur:
                    weigh(2)
                    weigh(3)
                    even, odd = (conv.rearrange("p (i r) -> p r i", r=2)[:, r, :] for r in range(2))
                    xe, xo = (x3T[par][:, :].rearrange("p (i r) -> p r i", r=2)[:, r, :] for r in range(2))
                    wait(dve, pe_P1, V(1))
                    wait(dve, ac_x3T, V(1))
                    wait(dve, ac_xchi, V(0))
                    wait(dve, dv_xclo, V(0))
                    v.scalar_tensor_tensor(even, MS_BANK[:, 0:HALF], bn_bias[:, 1:2], xe, ALU.add, ALU.add)
                    v.scalar_tensor_tensor(odd, xo, bn_bias[:, 1:2], MS_BANK[:, 1:HALF + 1], ALU.add,
                                           ALU.subtract).then_inc(dv_ab, 1)
                    wait(dve, dv_ab, V(1))
                    wait(dve, ac_P0s, V(1))
                    v.tensor_tensor(odd, CV_BANK[:, HALF:N], odd, ALU.add).then_inc(dv_q, 1)
                    v.tensor_tensor(even, even, P0s[:, :], ALU.add)
                    wait(dve, dv_q, V(1))
                    v.tensor_tensor(odd, odd, P0s[:, :], ALU.subtract).then_inc(dv_conv, 1)
                if nxt:
                    wait(dve, pe_dcol, V(2))
                    wait(dve, ac_pe, V(2))
                    v.tensor_tensor(dq[:, 0, :], SQ_BANK[:, 0:NC], pef[:, 0, :], ALU.mult).then_inc(dv_q0, 1)
                    hold(dve, dv_q0, V(2))
                    v.reciprocal(dq[:, 1, :], dq[:, 0, :]).then_inc(dv_q1, 1)
                    wait(dve, dv_q1, V(2))
                    v.tensor_tensor(dq[:, 2, :], dq[:, 1, :], pef[:, 0, :], ALU.mult).then_inc(dv_dq, 1)
                    wait(dve, pe_out2, V(2))
                    wait(dve, po_x2b, V(2))
                    wait(dve, dv_dq, V(2))
                    for c in range(NC):
                        last = v.scalar_tensor_tensor(y3[:, c, :], AG_BANK[:, ch(c)], dq[:, 2, c:c + 1], y3[:, c, :],
                                                      ALU.mult, ALU.add)
                    last.then_inc(dv_y3, 1)
                if cur:
                    wait(dve, ac_xchi, V(1))
                    wait(dve, pe_gn, V(0))
                    v.scalar_tensor_tensor(xc_lo[:, :], conv, 0.0, f(xc_hi[:, :]), ALU.max,
                                           ALU.subtract).then_inc(dv_xclo, 1)
                if nxt:
                    hold(dve, dv_y3, V(2))
                    statistics(2, V, 2, lambda c: y3[:, c, :])
                if cur:
                    wait(dve, ac_nmphi, V(1))
                    wait(dve, pe_gn, V(0))
                    v.tensor_tensor(nmp_lo[:, :], X_BANK[:, :], f(nmp_hi[:, :]), ALU.subtract).then_inc(dv_nmplo, 1)
                if nxt:
                    hold(dve, pe_x3T, V(1))
                    normalise(2, V, 2, x3, y3, dv_x3)
                if new:
                    wait(dve, ac_xhi, V(3))
                    wait(dve, x_in[par], dma(2))
                    v.tensor_tensor(x_lo[:, :, :], x_nat[par][:, :, :], f(x_hi[:, :, :]),
                                    ALU.subtract).then_inc(dv_xlo, 1)
                    split_rest(0)
                    split_rest(2)

            over_graphs(dve, turn)

        @block.tensor
        def _(pe):
            t_ = nc.tensor
            def turn(V, dma, par, graph, has, outs):
                cur, nxt, prev, new = has(0), has(1), has(-1), has(2)

                def transpose_adjacency(mc):
                    for c in range(NC):
                        last = t_.transpose(AT_BANK[mc % 2][:, ch(c)], adj_nat[par][:, c, ch(mc)], ident[:, :])
                    last.then_inc(pe_aT[mc], 1)

                def distances(mc):
                    t_.matmul(AT_BANK[mc % 2][:, :], Lf[:, ch(mc)], Rf[:, :], start=True, stop=True
                              ).then_inc(pe_D[mc], 1)

                def taps(o, first, count, hi, lo, start_col, width, done):
                    for k, blk in enumerate(range(first, first + count)):
                        w = range(start_col + k, start_col + k + width)
                        last = three(pe, o, w_hi[:, tapblk(blk), :], w_lo[:, tapblk(blk), :],
                                     hi[:, w.start:w.stop], lo[:, w.start:w.stop], k == 0, k == count - 1)
                    last.then_inc(done, 1)

                def gate(o, parts, done, k):
                    for i, (blk, hi, lo) in enumerate(parts):
                        if i == len(parts) - 1:
                            wait(pe, dv_nmplo, V(k))
                        last = three(pe, o, w_hi[:, blk, :], w_lo[:, blk, :], hi, lo, i == 0, i == len(parts) - 1)
                    last.then_inc(done, 1)

                def of_inputs(g):
                    return [(IH + 2 * g, xc_hi[:, :], xc_lo[:, :]), (IH + 2 * g + 1, nmp_hi[:, :], nmp_lo[:, :])]

                def of_state(g):
                    return [(HH + g, x3T_hi[:, :], x3T_lo[:, :])]

                if cur:
                    wait(pe, dv_x3, V(1))
                    wait(pe, dv_nmplo, V(0))
                    for c in range(NC):
                        last = t_.transpose(X_BANK[:, ch(c)], x3[:, c, :], ident[:, :])
                    last.then_inc(pe_x3T, 1)
                if nxt:
                    wait(pe, ac_xhi, V(2))
                    wait(pe, dv_xlo, V(2))
                    wait(pe, dv_y3, V(1))
                    for mc in range(NC):
                        wait(pe, aTlo[mc], V(2))
                        last = three(pe, AG_BANK[:, :], x_hi[:, mc, :], x_lo[:, mc, :], aT_hi[:, mc, :],
                                     aT_lo[:, mc, :], mc == 0, mc == NC - 1)
                    last.then_inc(pe_agg1, 1)
                if prev:
                    if cur:
                        wait(pe, dv_q0, V(1))
                    gate(SQ_BANK[:, :], of_inputs(2), pe_gn, 0)
                if nxt:
                    wait(pe, ac_agg1, V(2))
                    for c in range(NC):
                        last = t_.matmul(AG_BANK[:, ch(c)], agg_sb[:, ch(c)], w0[:, :], start=True, stop=True)
                    last.then_inc(pe_out0, 1)
                if cur:
                    wait(pe, ac_x3T, V(1))
                    wait(pe, dv_x3Tlo, V(1))
                    wait(pe, ac_thr, V(0))
                    three(pe, CV_BANK[:, :], w_hi[:, CONV1, :], w_lo[:, CONV1, :], x3T_hi[:, :], x3T_lo[:, :],
                          True, True).then_inc(pe_c1, 1)
                    wait(pe, ac_gh, V(0))
                    three(pe, HN_BANK[:, :], w_hi[:, HH + 2, :], w_lo[:, HH + 2, :], x3T_hi[:, :], x3T_lo[:, :],
                          True, True).then_inc(pe_hn, 1)
                if cur:
                    wait(pe, dv_t, V(0))
                    three(pe, SQ_BANK[:, :], w_hi[:, SE, :], w_lo[:, SE, :], x3T_hi[:, :], x3T_lo[:, :],
                          True, True).then_inc(pe_s, 1)
                    wait(pe, ac_thz, V(0))
                    t_.matmul(MS_BANK[:, :], ones_r[:, :], msg_bias[:, :, :].rearrange("p c d -> p (c d)"),
                              start=True, stop=False)
                    for c in range(NC):
                        last = t_.matmul(MS_BANK[:, ch(c)], x3T[par][:, ch(c)], wmsgT, start=False, stop=(c == NC - 1))
                    last.then_inc(pe_msg, 1)
                    wait(pe, ac_s2, V(1))
                    t_.matmul(SQ_BANK[:, :], sq_pick[0:32, :], sC[0:32, :], start=False, stop=True,
                              skip_group_check=True).then_inc(pe_sq, 1)
                    wait(pe, dv_c1, V(1))
                    taps(CV_BANK[:, 0:HALF], 0, EVEN, c1_hi[:, 0, :], c1_lo[:, 0, :], 0, HALF, pe_P0)
                    wait(pe, dv_csp, V(1))
                    taps(CV_BANK[:, HALF:N], EVEN + ODD, EVEN, cs_hi, cs_lo, 0, HALF, pe_Q)
                    wait(pe, dv_R, V(1))
                    wait(pe, po_L, V(1))
                    for mc in range(2):
                        wait(pe, ac_E[mc + 2], V(0))
                        if nxt:
                            wait(pe, ac_aT[mc + 2], V(2))
                        distances(mc)
                    wait(pe, dv_msglo, V(1))
                    taps(MS_BANK[:, 0:P1W], EVEN, ODD, c1_hi[:, 1, :], c1_lo[:, 1, :], 0, P1W, pe_P1)
                if prev:
                    wait(pe, po_y4, V(0))
                    if cur:
                        wait(pe, ac_x3T, V(1))
                    for c in range(NC):
                        last = t_.transpose(X_BANK[:, ch(c)], ga[:, ch(c)], ident[:, :])
                    last.then_inc(pe_yT, 1)
                if cur:
                    for mc in range(2, NC):
                        wait(pe, ac_E[mc - 2], V(1))
                        distances(mc)
                if nxt:
                    wait(pe, dv_pf, V(2))
                    for mc in range(NC):
                        t_.matmul(SQ_BANK[0:2, :], pf2[:, mc, :], aT_hi[:, mc, :], start=(mc == 0), stop=False)
                        last = t_.matmul(SQ_BANK[0:2, :], pf2[:, mc, :], aT_lo[:, mc, :], start=False,
                                         stop=(mc == NC - 1))
                    last.then_inc(pe_den, 1)
                    wait(pe, dv_xslo, V(2))
                    for mc in range(NC):
                        last = three(pe, AG_BANK[:, :], x_hi[:, mc, :], x_lo[:, mc, :], aT_hi[:, mc, :],
                                     aT_lo[:, mc, :], mc == 0, mc == NC - 1)
                    last.then_inc(pe_agg2, 1)
                    wait(pe, ac_den, V(2))
                    for c in range(NC):
                        last = t_.matmul(SQ_BANK[:, c:c + 1], den_sb[0:2, ch(c)], ones[0:2, 0:1], start=True, stop=True)
                    last.then_inc(pe_dcol, 1)
                if new:
                    wait(pe, adj_in[par], dma(2))
                    wait(pe, ac_E[2], V(1))
                    transpose_adjacency(0)
                if nxt:
                    wait(pe, ac_agg2, V(2))
                    for c in range(NC):
                        last = t_.matmul(AG_BANK[:, ch(c)], agg_sb[:, ch(c)], wwT, start=True, stop=True)
                    last.then_inc(pe_out2, 1)
                if cur:
                    if prev:
                        wait(pe, ac_out, V(0))
                    for mc in range(NC):
                        wait(pe, ac_Phi[mc], V(1))
                        wait(pe, po_Plo[mc], V(1))
                        last = three(pe, X_BANK[:, :], msg_hi[:, ch(mc)], msg_lo[:, ch(mc)], P_hi[:, mc, :],
                                     P_lo[:, mc, :], mc == 0, mc == NC - 1)
                    last.then_inc(pe_N, 1)
                if new:
                    wait(pe, ac_E[3], V(1))
                    transpose_adjacency(1)
                if cur:
                    wait(pe, dv_xclo, V(1))
                    gate(MS_BANK[:, :], of_state(1) + of_inputs(1), pe_z, 1)
                if new:
                    for mc in range(2, NC):
                        wait(pe, ac_aT[mc - 2], V(3))
                        transpose_adjacency(mc)
                if cur:
                    gate(CV_BANK[:, :], of_state(0) + of_inputs(0), pe_r, 1)

            over_graphs(pe, turn)


def kernel(**inputs):
    import numpy as _np
    import concourse.bacc as _bacc
    from concourse import mybir as _mybir
    from concourse.bass_utils import run_bass_kernel_spmd as _run

    nc = _bacc.Bacc("TRN2", target_bir_lowering=False, num_devices=1)
    arrays, aps = {}, {}
    for name, value in inputs.items():
        value = _np.ascontiguousarray(value)
        arrays[f"in_{name}_dram"] = value
        aps[name] = nc.dram_tensor(f"in_{name}_dram", value.shape, _mybir.dt.from_np(value.dtype),
                                   kind="ExternalInput").ap()
    out = nc.dram_tensor("out_0_dram", (B, N, D), _mybir.dt.float32, kind="ExternalOutput").ap()
    network_kernel(nc, aps, out)
    r = _run(nc, [arrays], core_ids=[0])
    return r.results[0]["out_0_dram"]
```
